# Optimizing a Trainium2 kernel written in Bass

```python
import numpy as np
import jax
import jax.numpy as jnp

def _softmax(x, axis=-1):
    return jax.nn.softmax(x, axis=axis)

def _gelu(x):
    return jax.nn.gelu(x, approximate=True)

def _silu(x):
    return jax.nn.silu(x)

def _sigmoid(x):
    return jax.nn.sigmoid(x)

def _layernorm(x, axis=-1, eps=1e-05):
    m = jnp.mean(x, axis=axis, keepdims=True)
    v = jnp.var(x, axis=axis, keepdims=True)
    return (x - m) / jnp.sqrt(v + eps)

def _scatter_add(tgt, idx, src, axis=0):
    return tgt.at[idx].add(src)

def _segment_sum(src, seg, n):
    return jax.ops.segment_sum(src, seg, n)
kernel_name = 'mk_vit_tower_d2_tok_img256_r4_f50cce'

def setup_inputs(seed: int=0):
    np.random.seed(seed)
    _w = jnp.asarray

    def _rec_inputs():
        import jax
        import jax.numpy as jnp
        _rk = jax.random.key(seed)
        x = -0.000222058 + 0.999998 * jax.random.normal(jax.random.fold_in(_rk, 1), (16, 3, 128, 128), jnp.float32)
        return x
    x = _rec_inputs()

    def _L0_tok_setup():
        import jax, jax.numpy as jnp
        import numpy as np
        P = 16
        NUM_HEADS = 8
        WINDOW = 64

        def _layer_norm(x, w, b, eps=1e-05):
            mu = jnp.mean(x, axis=-1, keepdims=True)
            var = jnp.var(x, axis=-1, keepdims=True)
            return (x - mu) * jax.lax.rsqrt(var + eps) * w + b

        def _sinusoidal_pe(num_patches, num_features, dtype):
            pos = jnp.arange(num_patches, dtype=jnp.float32)[:, None]
            i = jnp.arange(0, num_features, 2, dtype=jnp.float32)
            div = jnp.exp(-jnp.log(10000.0) * i / num_features)
            ang = pos * div
            pe = jnp.stack([jnp.sin(ang), jnp.cos(ang)], axis=-1).reshape(num_patches, num_features)
            return pe.astype(dtype)

        def _ffn(x, w1, b1, w2, b2):
            h = jax.nn.gelu(jnp.einsum('bnd,hd->bnh', x, w1) + b1)
            return jnp.einsum('bnh,dh->bnd', h, w2) + b2

        def _windowed_attention(x, qkv_w, qkv_b, proj_w, proj_b):
            B, N, D = x.shape
            hd = D // NUM_HEADS
            qkv = jnp.einsum('bnd,ed->bne', x, qkv_w) + qkv_b
            qkv = qkv.reshape(B, N, 3, NUM_HEADS, hd)
            q, k, v = (qkv[:, :, 0], qkv[:, :, 1], qkv[:, :, 2])
            nw = N // WINDOW
            q = q.reshape(B, nw, WINDOW, NUM_HEADS, hd).transpose(0, 3, 1, 2, 4)
            k = k.reshape(B, nw, WINDOW, NUM_HEADS, hd).transpose(0, 3, 1, 2, 4)
            v = v.reshape(B, nw, WINDOW, NUM_HEADS, hd).transpose(0, 3, 1, 2, 4)
            scale = 1.0 / jnp.sqrt(jnp.asarray(hd, x.dtype))
            scores = jnp.einsum('bhwqd,bhwkd->bhwqk', q, k) * scale
            attn = jax.nn.softmax(scores, axis=-1)
            out = jnp.einsum('bhwqk,bhwkd->bhwqd', attn, v)
            out = out.transpose(0, 2, 3, 1, 4).reshape(B, N, D)
            return jnp.einsum('bnd,ed->bne', out, proj_w) + proj_b
        key = jax.random.key(seed)
        ks = jax.random.split(key, 8)
        D, HF = (64, 256)
        s = lambda fan: 1.0 / np.sqrt(fan)
        return {'x': jax.random.normal(ks[0], (32, 3, 128, 128), jnp.float32), 'conv_w': jax.random.normal(ks[1], (D, 3, P, P), jnp.float32) * s(3 * P * P), 'conv_b': jnp.zeros((D,), jnp.float32), 'ln_w': jnp.ones((D,), jnp.float32), 'ln_b': jnp.zeros((D,), jnp.float32), 'qkv_w': jax.random.normal(ks[2], (3 * D, D), jnp.float32) * s(D), 'qkv_b': jnp.zeros((3 * D,), jnp.float32), 'proj_w': jax.random.normal(ks[3], (D, D), jnp.float32) * s(D), 'proj_b': jnp.zeros((D,), jnp.float32), 'ff_w1': jax.random.normal(ks[4], (HF, D), jnp.float32) * s(D), 'ff_b1': jnp.zeros((HF,), jnp.float32), 'ff_w2': jax.random.normal(ks[5], (D, HF), jnp.float32) * s(HF), 'ff_b2': jnp.zeros((D,), jnp.float32)}
    _L0_tok_all = _L0_tok_setup()
    _L0_tok_in = {k: v for k, v in _L0_tok_all.items() if k in ('conv_w', 'conv_b', 'ln_w', 'ln_b', 'qkv_w', 'qkv_b', 'proj_w', 'proj_b', 'ff_w1', 'ff_b1', 'ff_w2', 'ff_b2')}
    del _L0_tok_all

    def _L0_attn_setup():
        import jax, jax.numpy as jnp
        import numpy as np
        NUM_HEADS = 4
        LN_EPS = 1e-05

        def positional_encoding(length, d_model):
            pos = jnp.arange(length, dtype=jnp.float32)[:, None]
            div = jnp.exp(jnp.arange(0, d_model, 2, dtype=jnp.float32) * (-np.log(10000.0) / d_model))
            pe = jnp.zeros((length, d_model), dtype=jnp.float32)
            pe = pe.at[:, 0::2].set(jnp.sin(pos * div))
            pe = pe.at[:, 1::2].set(jnp.cos(pos * div))
            return pe

        def rel_shift(pos_score):
            B, H, S, _ = pos_score.shape
            padded = jnp.pad(pos_score, ((0, 0), (0, 0), (0, 0), (1, 0)))
            padded = padded.reshape(B, H, S + 1, S)
            return padded[:, :, 1:].reshape(B, H, S, S)
        key = jax.random.key(seed)
        ks = jax.random.split(key, 8)
        B, S, D, H = (8, 512, 64, NUM_HEADS)
        dh = D // H
        s = 0.02
        return {'inputs': jax.random.normal(ks[0], (B, S, D), dtype=jnp.float32), 'ln_gamma': jnp.ones((D,), jnp.float32), 'ln_beta': jnp.zeros((D,), jnp.float32), 'Wq': jax.random.normal(ks[1], (D, D), jnp.float32) * s, 'bq': jnp.zeros((D,), jnp.float32), 'Wk': jax.random.normal(ks[2], (D, D), jnp.float32) * s, 'bk': jnp.zeros((D,), jnp.float32), 'Wv': jax.random.normal(ks[3], (D, D), jnp.float32) * s, 'bv': jnp.zeros((D,), jnp.float32), 'Wpos': jax.random.normal(ks[4], (D, D), jnp.float32) * s, 'u_bias': jax.random.normal(ks[5], (H, dh), jnp.float32) * s, 'v_bias': jax.random.normal(ks[6], (H, dh), jnp.float32) * s, 'Wout': jax.random.normal(ks[7], (D, D), jnp.float32) * s, 'bout': jnp.zeros((D,), jnp.float32)}
    _L0_attn_all = _L0_attn_setup()
    _L0_attn_in = {k: v for k, v in _L0_attn_all.items() if k in ('ln_gamma', 'ln_beta', 'Wq', 'bq', 'Wk', 'bk', 'Wv', 'bv', 'Wpos', 'u_bias', 'v_bias', 'Wout', 'bout')}
    del _L0_attn_all

    def _L0_ffn_setup():
        import jax, jax.numpy as jnp
        import numpy as np
        B, S, H, F, E, K = (8, 1024, 64, 128, 16, 2)
        EPS = 1e-05
        key = jax.random.key(seed)
        ks = jax.random.split(key, 9)
        sc = 0.02
        return {'x': jax.random.normal(ks[0], (B, S, H), dtype=jnp.float32), 'gate_w': jax.random.normal(ks[1], (H, E), dtype=jnp.float32) * sc, 'gate_b': jnp.zeros((E,), dtype=jnp.float32), 'w1': jax.random.normal(ks[2], (E, H, F), dtype=jnp.float32) * sc, 'b1': jnp.zeros((E, F), dtype=jnp.float32), 'w2': jax.random.normal(ks[3], (E, F, H), dtype=jnp.float32) * sc, 'b2': jnp.zeros((E, H), dtype=jnp.float32), 'gamma': jnp.ones((H,), dtype=jnp.float32), 'beta': jnp.zeros((H,), dtype=jnp.float32)}
    _L0_ffn_all = _L0_ffn_setup()
    _L0_ffn_in = {k: v for k, v in _L0_ffn_all.items() if k in ('gate_w', 'gate_b', 'w1', 'b1', 'w2', 'b2', 'gamma', 'beta')}
    del _L0_ffn_all

    def _L1_attn_setup():
        import jax, jax.numpy as jnp
        import numpy as np
        EPS = 1e-06

        def _rmsnorm(x, w):
            xf = x.astype(jnp.float32)
            y = xf * jax.lax.rsqrt(jnp.mean(xf * xf, axis=-1, keepdims=True) + EPS)
            return y.astype(x.dtype) * w
        key = jax.random.key(seed)
        k0, k1, k2 = jax.random.split(key, 3)
        B, T, C = (2, 256, 64)
        x = jax.random.normal(k0, (B, T, C), jnp.float32)
        w_qkv = jax.random.normal(k1, (3 * C, C), jnp.float32) / np.float32(np.sqrt(C))
        w_proj = jax.random.normal(k2, (C, C), jnp.float32) / np.float32(np.sqrt(C))
        qn_w = jnp.ones((2,), jnp.float32)
        kn_w = jnp.ones((2,), jnp.float32)
        return {'x': x, 'w_qkv': w_qkv, 'w_proj': w_proj, 'qn_w': qn_w, 'kn_w': kn_w}
    _L1_attn_all = _L1_attn_setup()
    _L1_attn_in = {k: v for k, v in _L1_attn_all.items() if k in ('w_qkv', 'w_proj', 'qn_w', 'kn_w')}
    del _L1_attn_all

    def _L1_ffn_setup():
        import jax, jax.numpy as jnp
        import numpy as np
        B, T, C = (64, 96, 64)
        NH, NKV = (4, 2)
        HD = C // NH
        NREP = NH // NKV
        NE, TOPK = (8, 2)
        HID = int(8 / 3 * C)
        EPS_RMS = 1e-06

        def _rope_tables(t_len):
            inv_freq = 1.0 / 10000.0 ** (np.arange(0, HD, 2, dtype=np.float32) / HD)
            t = np.arange(t_len, dtype=np.float32)
            freqs = np.outer(t, inv_freq)
            emb = np.concatenate([freqs, freqs], axis=-1)
            return (jnp.asarray(np.cos(emb)), jnp.asarray(np.sin(emb)))

        def _rotate_half(x):
            h = x.shape[-1] // 2
            return jnp.concatenate([-x[..., h:], x[..., :h]], axis=-1)

        def _rmsnorm(v, w):
            return v * jax.lax.rsqrt(jnp.mean(v * v, axis=-1, keepdims=True) + EPS_RMS) * w
        key = jax.random.key(seed)
        ks = jax.random.split(key, 10)
        s = lambda k, shape: jax.random.normal(k, shape, jnp.float32) * 0.02
        return {'x': jax.random.normal(ks[0], (B, T, C), jnp.float32), 'ln1_w': jnp.ones((C,), jnp.float32), 'ln2_w': jnp.ones((C,), jnp.float32), 'wq': s(ks[1], (NH * HD, C)), 'wk': s(ks[2], (NKV * HD, C)), 'wv': s(ks[3], (NKV * HD, C)), 'wo': s(ks[4], (C, C)), 'router_w': s(ks[5], (NE, C)), 'w1': s(ks[6], (NE, HID, C)), 'w2': s(ks[7], (NE, C, HID)), 'w3': s(ks[8], (NE, HID, C))}
    _L1_ffn_all = _L1_ffn_setup()
    _L1_ffn_in = {k: v for k, v in _L1_ffn_all.items() if k in ('ln1_w', 'ln2_w', 'wq', 'wk', 'wv', 'wo', 'router_w', 'w1', 'w2', 'w3')}
    del _L1_ffn_all
    return {'x': x, 'L0_tok_conv_w': _L0_tok_in['conv_w'], 'L0_tok_conv_b': _L0_tok_in['conv_b'], 'L0_tok_ln_w': _L0_tok_in['ln_w'], 'L0_tok_ln_b': _L0_tok_in['ln_b'], 'L0_tok_qkv_w': _L0_tok_in['qkv_w'], 'L0_tok_qkv_b': _L0_tok_in['qkv_b'], 'L0_tok_proj_w': _L0_tok_in['proj_w'], 'L0_tok_proj_b': _L0_tok_in['proj_b'], 'L0_tok_ff_w1': _L0_tok_in['ff_w1'], 'L0_tok_ff_b1': _L0_tok_in['ff_b1'], 'L0_tok_ff_w2': _L0_tok_in['ff_w2'], 'L0_tok_ff_b2': _L0_tok_in['ff_b2'], 'L0_attn_ln_gamma': _L0_attn_in['ln_gamma'], 'L0_attn_ln_beta': _L0_attn_in['ln_beta'], 'L0_attn_Wq': _L0_attn_in['Wq'], 'L0_attn_bq': _L0_attn_in['bq'], 'L0_attn_Wk': _L0_attn_in['Wk'], 'L0_attn_bk': _L0_attn_in['bk'], 'L0_attn_Wv': _L0_attn_in['Wv'], 'L0_attn_bv': _L0_attn_in['bv'], 'L0_attn_Wpos': _L0_attn_in['Wpos'], 'L0_attn_u_bias': _L0_attn_in['u_bias'], 'L0_attn_v_bias': _L0_attn_in['v_bias'], 'L0_attn_Wout': _L0_attn_in['Wout'], 'L0_attn_bout': _L0_attn_in['bout'], 'L0_ffn_gate_w': _L0_ffn_in['gate_w'], 'L0_ffn_gate_b': _L0_ffn_in['gate_b'], 'L0_ffn_w1': _L0_ffn_in['w1'], 'L0_ffn_b1': _L0_ffn_in['b1'], 'L0_ffn_w2': _L0_ffn_in['w2'], 'L0_ffn_b2': _L0_ffn_in['b2'], 'L0_ffn_gamma': _L0_ffn_in['gamma'], 'L0_ffn_beta': _L0_ffn_in['beta'], 'L1_attn_w_qkv': _L1_attn_in['w_qkv'], 'L1_attn_w_proj': _L1_attn_in['w_proj'], 'L1_attn_qn_w': _L1_attn_in['qn_w'], 'L1_attn_kn_w': _L1_attn_in['kn_w'], 'L1_ffn_ln1_w': _L1_ffn_in['ln1_w'], 'L1_ffn_ln2_w': _L1_ffn_in['ln2_w'], 'L1_ffn_wq': _L1_ffn_in['wq'], 'L1_ffn_wk': _L1_ffn_in['wk'], 'L1_ffn_wv': _L1_ffn_in['wv'], 'L1_ffn_wo': _L1_ffn_in['wo'], 'L1_ffn_router_w': _L1_ffn_in['router_w'], 'L1_ffn_w1': _L1_ffn_in['w1'], 'L1_ffn_w2': _L1_ffn_in['w2'], 'L1_ffn_w3': _L1_ffn_in['w3']}

def reference(x, L0_tok_conv_w, L0_tok_conv_b, L0_tok_ln_w, L0_tok_ln_b, L0_tok_qkv_w, L0_tok_qkv_b, L0_tok_proj_w, L0_tok_proj_b, L0_tok_ff_w1, L0_tok_ff_b1, L0_tok_ff_w2, L0_tok_ff_b2, L0_attn_ln_gamma, L0_attn_ln_beta, L0_attn_Wq, L0_attn_bq, L0_attn_Wk, L0_attn_bk, L0_attn_Wv, L0_attn_bv, L0_attn_Wpos, L0_attn_u_bias, L0_attn_v_bias, L0_attn_Wout, L0_attn_bout, L0_ffn_gate_w, L0_ffn_gate_b, L0_ffn_w1, L0_ffn_b1, L0_ffn_w2, L0_ffn_b2, L0_ffn_gamma, L0_ffn_beta, L1_attn_w_qkv, L1_attn_w_proj, L1_attn_qn_w, L1_attn_kn_w, L1_ffn_ln1_w, L1_ffn_ln2_w, L1_ffn_wq, L1_ffn_wk, L1_ffn_wv, L1_ffn_wo, L1_ffn_router_w, L1_ffn_w1, L1_ffn_w2, L1_ffn_w3):
    import jax
    import jax.numpy as jnp

    def _L0_tok_ref(x, conv_w, conv_b, ln_w, ln_b, qkv_w, qkv_b, proj_w, proj_b, ff_w1, ff_b1, ff_w2, ff_b2):
        import jax, jax.numpy as jnp
        import numpy as np
        P = 16
        NUM_HEADS = 8
        WINDOW = 64

        def _layer_norm(x, w, b, eps=1e-05):
            mu = jnp.mean(x, axis=-1, keepdims=True)
            var = jnp.var(x, axis=-1, keepdims=True)
            return (x - mu) * jax.lax.rsqrt(var + eps) * w + b

        def _sinusoidal_pe(num_patches, num_features, dtype):
            pos = jnp.arange(num_patches, dtype=jnp.float32)[:, None]
            i = jnp.arange(0, num_features, 2, dtype=jnp.float32)
            div = jnp.exp(-jnp.log(10000.0) * i / num_features)
            ang = pos * div
            pe = jnp.stack([jnp.sin(ang), jnp.cos(ang)], axis=-1).reshape(num_patches, num_features)
            return pe.astype(dtype)

        def _ffn(x, w1, b1, w2, b2):
            h = jax.nn.gelu(jnp.einsum('bnd,hd->bnh', x, w1) + b1)
            return jnp.einsum('bnh,dh->bnd', h, w2) + b2

        def _windowed_attention(x, qkv_w, qkv_b, proj_w, proj_b):
            B, N, D = x.shape
            hd = D // NUM_HEADS
            qkv = jnp.einsum('bnd,ed->bne', x, qkv_w) + qkv_b
            qkv = qkv.reshape(B, N, 3, NUM_HEADS, hd)
            q, k, v = (qkv[:, :, 0], qkv[:, :, 1], qkv[:, :, 2])
            nw = N // WINDOW
            q = q.reshape(B, nw, WINDOW, NUM_HEADS, hd).transpose(0, 3, 1, 2, 4)
            k = k.reshape(B, nw, WINDOW, NUM_HEADS, hd).transpose(0, 3, 1, 2, 4)
            v = v.reshape(B, nw, WINDOW, NUM_HEADS, hd).transpose(0, 3, 1, 2, 4)
            scale = 1.0 / jnp.sqrt(jnp.asarray(hd, x.dtype))
            scores = jnp.einsum('bhwqd,bhwkd->bhwqk', q, k) * scale
            attn = jax.nn.softmax(scores, axis=-1)
            out = jnp.einsum('bhwqk,bhwkd->bhwqd', attn, v)
            out = out.transpose(0, 2, 3, 1, 4).reshape(B, N, D)
            return jnp.einsum('bnd,ed->bne', out, proj_w) + proj_b
        B, C, H, W = x.shape
        D = conv_w.shape[0]
        nH, nW = (H // P, W // P)
        patches = x.reshape(B, C, nH, P, nW, P).transpose(0, 2, 4, 1, 3, 5).reshape(B, nH * nW, C * P * P)
        h = jnp.einsum('bnp,dp->bnd', patches, conv_w.reshape(D, -1)) + conv_b
        h = _layer_norm(h, ln_w, ln_b)
        h = h + _sinusoidal_pe(h.shape[1], D, h.dtype)
        identity = h
        h = _ffn(h, ff_w1, ff_b1, ff_w2, ff_b2)
        h = _windowed_attention(h, qkv_w, qkv_b, proj_w, proj_b)
        h = h + identity
        identity = h
        h = _ffn(h, ff_w1, ff_b1, ff_w2, ff_b2)
        return h + identity

    def _L0_attn_ref(inputs, ln_gamma, ln_beta, Wq, bq, Wk, bk, Wv, bv, Wpos, u_bias, v_bias, Wout, bout):
        import jax, jax.numpy as jnp
        import numpy as np
        NUM_HEADS = 4
        LN_EPS = 1e-05

        def positional_encoding(length, d_model):
            pos = jnp.arange(length, dtype=jnp.float32)[:, None]
            div = jnp.exp(jnp.arange(0, d_model, 2, dtype=jnp.float32) * (-np.log(10000.0) / d_model))
            pe = jnp.zeros((length, d_model), dtype=jnp.float32)
            pe = pe.at[:, 0::2].set(jnp.sin(pos * div))
            pe = pe.at[:, 1::2].set(jnp.cos(pos * div))
            return pe

        def rel_shift(pos_score):
            B, H, S, _ = pos_score.shape
            padded = jnp.pad(pos_score, ((0, 0), (0, 0), (0, 0), (1, 0)))
            padded = padded.reshape(B, H, S + 1, S)
            return padded[:, :, 1:].reshape(B, H, S, S)
        B, S, D = inputs.shape
        H = NUM_HEADS
        dh = D // H
        mu = jnp.mean(inputs, axis=-1, keepdims=True)
        var = jnp.mean(jnp.square(inputs - mu), axis=-1, keepdims=True)
        x = (inputs - mu) / jnp.sqrt(var + LN_EPS) * ln_gamma + ln_beta
        pe = positional_encoding(S, D)
        q = (x @ Wq + bq).reshape(B, S, H, dh)
        k = (x @ Wk + bk).reshape(B, S, H, dh)
        v = (x @ Wv + bv).reshape(B, S, H, dh)
        p = (pe @ Wpos).reshape(S, H, dh)
        content_score = jnp.einsum('bshd,bthd->bhst', q + u_bias, k)
        pos_score = jnp.einsum('bshd,thd->bhst', q + v_bias, p)
        pos_score = rel_shift(pos_score)
        score = (content_score + pos_score) / np.sqrt(D).astype(np.float32)
        attn = jax.nn.softmax(score, axis=-1)
        ctx = jnp.einsum('bhst,bthd->bshd', attn, v).reshape(B, S, D)
        return ctx @ Wout + bout

    def _L0_ffn_ref(x, gate_w, gate_b, w1, b1, w2, b2, gamma, beta):
        import jax, jax.numpy as jnp
        import numpy as np
        B, S, H, F, E, K = (8, 1024, 64, 128, 16, 2)
        EPS = 1e-05
        gate_logits = x @ gate_w + gate_b
        topk_vals, topk_idx = jax.lax.top_k(gate_logits, K)
        topk_w = jax.nn.softmax(topk_vals, axis=-1)
        h = jax.nn.relu(jnp.einsum('bsh,ehf->bsef', x, w1) + b1)
        expert_out = jnp.einsum('bsef,efh->bseh', h, w2) + b2
        sel = jnp.take_along_axis(expert_out, topk_idx[:, :, :, None], axis=2)
        moe = jnp.sum(topk_w[..., None] * sel, axis=2)
        y = x + moe
        mu = jnp.mean(y, axis=-1, keepdims=True)
        var = jnp.var(y, axis=-1, keepdims=True)
        return (y - mu) / jnp.sqrt(var + EPS) * gamma + beta

    def _L1_attn_ref(x, w_qkv, w_proj, qn_w, kn_w):
        import jax, jax.numpy as jnp
        import numpy as np
        EPS = 1e-06

        def _rmsnorm(x, w):
            xf = x.astype(jnp.float32)
            y = xf * jax.lax.rsqrt(jnp.mean(xf * xf, axis=-1, keepdims=True) + EPS)
            return y.astype(x.dtype) * w
        B, T, C = x.shape
        HD = 2
        H = C // HD
        qkv = x @ w_qkv.T
        q, k, v = jnp.split(qkv, 3, axis=-1)
        heads = lambda t: t.reshape(B, T, H, HD).transpose(0, 2, 1, 3)
        q = _rmsnorm(heads(q), qn_w)
        k = _rmsnorm(heads(k), kn_w)
        v = heads(v)
        scale = np.float32(1.0 / np.sqrt(HD))
        att = jnp.einsum('bhtd,bhsd->bhts', q, k) * scale
        causal = jnp.tril(jnp.ones((T, T), bool))
        att = jnp.where(causal, att, jnp.float32(-1e+30))
        att = jax.nn.softmax(att, axis=-1)
        y = jnp.einsum('bhts,bhsd->bhtd', att, v)
        y = y.transpose(0, 2, 1, 3).reshape(B, T, C)
        return y @ w_proj.T

    def _L1_ffn_ref(x, ln1_w, ln2_w, wq, wk, wv, wo, router_w, w1, w2, w3):
        import jax, jax.numpy as jnp
        import numpy as np
        B, T, C = (64, 96, 64)
        NH, NKV = (4, 2)
        HD = C // NH
        NREP = NH // NKV
        NE, TOPK = (8, 2)
        HID = int(8 / 3 * C)
        EPS_RMS = 1e-06

        def _rope_tables(t_len):
            inv_freq = 1.0 / 10000.0 ** (np.arange(0, HD, 2, dtype=np.float32) / HD)
            t = np.arange(t_len, dtype=np.float32)
            freqs = np.outer(t, inv_freq)
            emb = np.concatenate([freqs, freqs], axis=-1)
            return (jnp.asarray(np.cos(emb)), jnp.asarray(np.sin(emb)))

        def _rotate_half(x):
            h = x.shape[-1] // 2
            return jnp.concatenate([-x[..., h:], x[..., :h]], axis=-1)

        def _rmsnorm(v, w):
            return v * jax.lax.rsqrt(jnp.mean(v * v, axis=-1, keepdims=True) + EPS_RMS) * w
        Bx, Tx, Cx = x.shape
        h = _rmsnorm(x, ln1_w)
        q = (h @ wq.T).reshape(Bx, Tx, NH, HD).transpose(0, 2, 1, 3)
        k = (h @ wk.T).reshape(Bx, Tx, NKV, HD).transpose(0, 2, 1, 3)
        v = (h @ wv.T).reshape(Bx, Tx, NKV, HD).transpose(0, 2, 1, 3)
        cos, sin = _rope_tables(Tx)
        cos, sin = (cos[None, None], sin[None, None])
        q = q * cos + _rotate_half(q) * sin
        k = k * cos + _rotate_half(k) * sin
        k = jnp.repeat(k, NREP, axis=1)
        v = jnp.repeat(v, NREP, axis=1)
        scores = jnp.einsum('bhtd,bhsd->bhts', q, k) / jnp.sqrt(jnp.float32(HD))
        causal = jnp.tril(jnp.ones((Tx, Tx), dtype=bool))
        scores = jnp.where(causal[None, None], scores, jnp.float32(-1e+30))
        att = jax.nn.softmax(scores, axis=-1)
        y = jnp.einsum('bhts,bhsd->bhtd', att, v).transpose(0, 2, 1, 3).reshape(Bx, Tx, Cx)
        x = x + y @ wo.T
        flat = _rmsnorm(x, ln2_w).reshape(-1, Cx)
        probs = jax.nn.softmax(flat @ router_w.T, axis=-1)
        tp, ti = jax.lax.top_k(probs, TOPK)
        tp = tp / (jnp.sum(tp, axis=-1, keepdims=True) + 1e-09)
        weights = jnp.sum(tp[..., None] * jax.nn.one_hot(ti, NE, dtype=flat.dtype), axis=1)
        out = jnp.zeros_like(flat)
        for e in range(NE):
            hh = jax.nn.silu(flat @ w1[e].T) * (flat @ w3[e].T)
            out = out + weights[:, e:e + 1] * (hh @ w2[e].T)
        return x + out.reshape(Bx, Tx, Cx)
    h = _L0_tok_ref(x, L0_tok_conv_w, L0_tok_conv_b, L0_tok_ln_w, L0_tok_ln_b, L0_tok_qkv_w, L0_tok_qkv_b, L0_tok_proj_w, L0_tok_proj_b, L0_tok_ff_w1, L0_tok_ff_b1, L0_tok_ff_w2, L0_tok_ff_b2)
    h = h + _L0_attn_ref(_layernorm(h, axis=-1), L0_attn_ln_gamma, L0_attn_ln_beta, L0_attn_Wq, L0_attn_bq, L0_attn_Wk, L0_attn_bk, L0_attn_Wv, L0_attn_bv, L0_attn_Wpos, L0_attn_u_bias, L0_attn_v_bias, L0_attn_Wout, L0_attn_bout)
    h = h + _L0_ffn_ref(_layernorm(h, axis=-1), L0_ffn_gate_w, L0_ffn_gate_b, L0_ffn_w1, L0_ffn_b1, L0_ffn_w2, L0_ffn_b2, L0_ffn_gamma, L0_ffn_beta)
    h = h + _L1_attn_ref(_layernorm(h, axis=-1), L1_attn_w_qkv, L1_attn_w_proj, L1_attn_qn_w, L1_attn_kn_w)
    h = h + _L1_ffn_ref(_layernorm(h, axis=-1), L1_ffn_ln1_w, L1_ffn_ln2_w, L1_ffn_wq, L1_ffn_wk, L1_ffn_wv, L1_ffn_wo, L1_ffn_router_w, L1_ffn_w1, L1_ffn_w2, L1_ffn_w3)
    return h

_drawn_inputs = setup_inputs


def setup_inputs(seed=0):
    import zlib

    import numpy as np

    out = dict(_drawn_inputs(seed))
    spreads = {'L0_tok_conv_b': (0.0, 0.1),
     'L0_tok_ln_w': (1.0, 0.2),
     'L0_tok_ln_b': (0.0, 0.1),
     'L0_tok_qkv_b': (0.0, 0.1),
     'L0_tok_proj_b': (0.0, 0.1),
     'L0_tok_ff_b1': (0.0, 0.1),
     'L0_tok_ff_b2': (0.0, 0.1),
     'L0_attn_ln_gamma': (1.0, 0.6),
     'L0_attn_ln_beta': (0.0, 0.8),
     'L0_attn_bq': (0.0, 0.8),
     'L0_attn_bk': (0.0, 0.8),
     'L0_attn_bv': (0.0, 0.678),
     'L0_attn_bout': (0.0, 0.1),
     'L0_ffn_gate_b': (0.0, 0.285),
     'L0_ffn_b1': (0.0, 0.8),
     'L0_ffn_b2': (0.0, 0.295),
     'L0_ffn_gamma': (1.0, 0.2),
     'L0_ffn_beta': (0.0, 0.1),
     'L1_attn_qn_w': (1.0, 0.6),
     'L1_attn_kn_w': (1.0, 0.6),
     'L1_ffn_ln1_w': (1.0, 0.6),
     'L1_ffn_ln2_w': (1.0, 0.6)}
    factors = {'L0_attn_Wq': 8.0,
     'L0_attn_Wk': 8.0,
     'L0_attn_Wv': 8.0,
     'L0_attn_Wpos': 8.0,
     'L0_attn_u_bias': 8.0,
     'L0_attn_v_bias': 8.0,
     'L0_attn_Wout': 2.865,
     'L0_ffn_w1': 8.0,
     'L0_ffn_w2': 6.901,
     'L1_ffn_wq': 8.0,
     'L1_ffn_wk': 8.0,
     'L1_ffn_wv': 8.0,
     'L1_ffn_wo': 8.0,
     'L1_ffn_router_w': 8.0,
     'L1_ffn_w1': 8.0,
     'L1_ffn_w2': 8.0,
     'L1_ffn_w3': 8.0}
    for name, (base, spread) in spreads.items():
        noise = np.random.default_rng([zlib.crc32(name.encode()), seed]).standard_normal(out[name].shape)
        drawn = base * np.exp(spread * noise) if base else spread * noise
        out[name] = jnp.asarray(drawn.astype(out[name].dtype))
    for name, factor in factors.items():
        out[name] = (out[name] * factor).astype(out[name].dtype)
    return out
```

```python
from contextlib import ExitStack

import numpy as np

import concourse.bass as bass
from concourse import mybir

F32 = mybir.dt.float32
BF16 = mybir.dt.bfloat16
F32R = mybir.dt.float32r
U16 = mybir.dt.uint16
U32 = mybir.dt.uint32
ALU = mybir.AluOpType
ACT = mybir.ActivationFunctionType
AX = mybir.AxisListType

B, C, IMG, PATCH = 16, 3, 128, 16
D = 64
S = (IMG // PATCH) ** 2
NB = B // 2
NT = NB * S
NQ = NT // 128
KC = C * PATCH * PATCH // 128
FF = 256
E0, F0 = 16, 128
E1, F1 = 8, 170
H1ROWS = E1 * F1
T1 = -(-H1ROWS // 128)
NEG = -1e30

PACKS = {
    "first": [("conv_w", KC * D), ("ident", 128), ("cols0", 8), ("pe_t", S), ("up_lo", FF), ("up_hi", FF),
              ("down", 2 * D)],
    "second": [("wq0", 128), ("wk0", 128), ("wv0", 2 * D), ("wp0", 128), ("cols1", 16), ("mask8", 8),
               ("mask4", 4), ("wpos", 128), ("pe_s", S), ("wq1", 128), ("wk1", 128), ("wv1", 2 * D),
               ("wo1", 128), ("bout", D)],
    "third": [("gate", 2 * E0), ("gate_b", E0), ("iota", E0), ("b2", 128), ("b1", E0), ("gamma", D), ("beta", D),
              ("wqk2", 256), ("wv2", 2 * D), ("wp2", 128), ("maskr", 8), ("maskg", 4), ("cols2", 4),
              ("wq3", 128), ("wqs3", 128), ("wk3", 128), ("wks3", 128), ("wv3", 2 * D), ("wo3", 128),
              ("rope_c", S), ("rope_s", S), ("router", 2 * E1)],
    "half": [("identb", 128), ("causal", 512), ("eye3", 2 * E0), ("sel1", 2 * H1ROWS)],
}
COL0 = ["conv_b", "ln_w", "ln_b", "ff_b1a", "ff_b1b", "ff_b2"]
COL1 = ["bq0", "bk0", "bv0", "bp0", "gamma1", "beta1", "bq1", "bk1", "bv1", "u1", "v1"]
COL2 = ["qn", "kn", "ln1", "ln2"]


def width(pack):
    return sum(n for _, n in PACKS[pack])


def tower_program(nc, patches, first, second, third, half_consts, moe0_w1, moe0_w2, moe1_w1, moe1_w3, moe1_w2, out):
    with ExitStack() as ctx:
        def sb(name, shape, dt=F32):
            return ctx.enter_context(nc.sbuf_tensor(name, shape, dt))

        sems = {}

        def sem(name):
            if name not in sems:
                sems[name] = ctx.enter_context(nc.semaphore(name))
            return sems[name]

        P = [ctx.enter_context(nc.psum_tensor(f"bank{i}", [128, 512], F32)) for i in range(8)]
        pos_scratch = nc.dram_tensor("pos_scratch", [2, NB // 2, 8, (S + 1) * S], F32, kind="Internal").ap()

        xt = sb("xt", [128, KC, 2 * NT])
        pk = {n: sb(f"pack_{n}", [128, width(n)], U16 if n == "half" else F32) for n in PACKS}
        w = {}
        for n, items in PACKS.items():
            at = 0
            for name, cols in items:
                w[name] = pk[n][:, at:at + cols].bitcast(BF16) if n == "half" else pk[n][:, at:at + cols]
                at += cols
        col = {}
        for base, names in (("cols0", COL0), ("cols1", COL1), ("cols2", COL2)):
            for i, name in enumerate(names):
                col[name] = w[base][:, i:i + 1]
        ident = w["ident"]
        identb = w["identb"]

        w1_split = [sb(f"w1_split{i}", [128, E0 * F0], F32R) for i in range(2)]
        raw0 = xt[:, 0:2, :].rearrange("p k n -> p (k n)")
        raw1 = xt[:, 2:5, :].rearrange("p k n -> p (k n)")[:, 0:2 * H1ROWS]
        w2_sb = sb("w2_sb", [128, E0 * D])
        u_split = [sb(f"u_split{i}", [128, 2 * H1ROWS], F32R) for i in range(2)]
        x_split = [sb(f"x_split{h}", [128, NT], F32R) for h in range(2)]
        d1_sb = sb("d1_sb", [128, T1 * D])

        def big(name):
            return sb(name, [128, NT])

        conv_t, xn0, h0_t, a0_t, h1_t, h2_t = (big(n) for n in ("conv_t", "xn0", "h0_t", "a0_t", "h1_t", "h2_t"))
        centred, xn = big("centred"), big("xn")
        hid = [sb(f"hid{i}", [128, NT]) for i in range(4)]
        pe_b = sb("pe_b", [128, S])
        stats = sb("stats", [128, 8, 6])
        mv = sb("mv", [128, 8, 2])
        rin = sb("rin", [128, 16])
        rout = sb("rout", [128, 16])
        msq = sb("msq", [128, 8])
        minus_half = sb("minus_half", [128, 16])

        q_bd = sb("q_bd", [128, NB, 128])
        qv_bd = sb("qv_bd", [128, NB, 128])
        k_t = big("k_t")
        R = [sb(f"R{i}", [128, 512]) for i in range(2)]
        L = [qv_bd[:, 4 * i:4 * i + 4, :] for i in range(2)]
        cen_s = [sb(f"cen_s{i}", [128, 512]) for i in range(2)]
        prob = [sb(f"prob{i}", [128, 512]) for i in range(2)]
        prob_t = [sb(f"prob_t{i}", [128, 512]) for i in range(2)]
        rowmax = [sb(f"rowmax{i}", [128, 8]) for i in range(2)]
        rowsum = [sb(f"rowsum{i}", [128, 32]) for i in range(2)]
        ctx_n = [sb(f"ctx_n{i}", [128, 128]) for i in range(2)]
        ctx_t = big("ctx_t")
        V0 = sb("V0", [128, 2 * NB * 4, 2 * 9])
        V4 = sb("V4", [128, 2 * NB * 2, 2 * 17])
        V32 = xt[:, 0:4, :].rearrange("p k n -> p (k n)").rearrange("p (g c) -> p g c", c=32)
        out_ts = [sb(f"out_ts{i}", [128, 512]) for i in range(2)]
        bqu = sb("bqu", [128, 1])
        bqv = sb("bqv", [128, 1])
        p_pos = sb("p_pos", [128, 4, S])
        pos_all = sb("pos_all", [128, 4, 8, S + 1])
        shifted_all = sb("shifted_all", [128, 4, 8, S])
        pos_sb = [pos_all[:, i] for i in range(4)]
        shifted = [shifted_all[:, i] for i in range(4)]
        xa_t, h2_n, h2_nb, h3_n, y_n, y_t, z_t = (big(n) for n in ("xa_t", "h2_n", "h2_nb", "h3_n", "y_n", "y_t", "z_t"))
        h3_nb, h4_n, xb_t = (big(n) for n in ("h3_nb", "h4_n", "xb_t"))
        xc_t, x_n, x2_n, fin_n, f_t, o_t, out_n, h5_n = conv_t, xn0, h0_t, a0_t, h1_t, h2_t, h2_n, h2_nb
        logit = sb("logit", [128, 8, E0])
        top8 = sb("top8", [128, 8, 8])
        top8i = sb("top8i", [128, 8, 8], U32)
        topf = sb("topf", [128, 8, 8])
        gap = sb("gap", [128, 8])
        egap = sb("egap", [128, 8])
        wsum = sb("wsum", [128, 8])
        w12 = sb("w12", [128, 8, 2])
        hot = [sb(f"hot{i}", [128, 8, E0]) for i in range(2)]
        gates = sb("gates", [128, 8, E0])
        resid = sb("resid", [128, 8, E0])
        gates3 = sb("gates3", [128, NQ, 128], BF16)
        gates_t3 = sb("gates_t3", [128, NT], BF16)
        gates_t = sb("gates_t", [2 * E0, NT])
        relu_h = out_ts
        sq = shifted_all[:, 0:2].rearrange("p i g t -> p (i g t)")
        qk_ms, qk_r = (shifted[i].rearrange("p g t -> p (g t)") for i in (2, 3))
        qk_n = pos_all[:].rearrange("p i g t -> p (i g t)")[:, 0:1024].rearrange("p (q o c) -> p q o c", q=NQ, o=2)
        rope = [xt[:, 4 + i // 2, NT * (i % 2):NT * (i % 2) + NT] for i in range(4)]
        gated = hid

        def heads(t, n):
            return t.rearrange("p (a b) -> p a b", a=n)

        def over(t, n):
            return t.unsqueeze(2).to_broadcast([t.shape[0], t.shape[1], n])

        def each(t, n):
            return t.unsqueeze(1).to_broadcast([t.shape[0], n, t.shape[1]])

        class Attn:

            def __init__(self, H, scale, V, mask, signals, units=None, causal=False, shift=False):
                self.H, self.hd, self.scale = H, D // H, scale
                self.per = 8 // H
                self.units = units or NB // self.per
                self.V, self.mask, self.causal, self.shift = V, mask, causal, shift
                self.base = dict(counted)
                for what in ("scores", "centred", "probs", "turned", "probs_t", "mixed"):
                    counted[what] += self.units
                for what, n in signals.items():
                    counted[what] += n

            def s(self, what):
                return sems[f"attn_{what}"]

            def wait(self, engine, what, n):
                engine.wait_ge(sems[f"attn_{what}"], self.base[what] + n)

        counted = dict.fromkeys(("q", "k_psum", "k", "v_psum", "v", "keys", "scores", "centred", "probs", "turned",
                                 "probs_t", "mixed", "context", "context_t", "context_sb"), 0)
        for what in counted:
            sem(f"attn_{what}")
        attn0 = Attn(8, 1.0 / np.sqrt(8.0), V0, w["mask8"],
                     dict(q=2, k_psum=2, k=1, v_psum=1, v=2, keys=8, context=8, context_t=8, context_sb=2))
        attn1 = Attn(4, 1.0 / 8.0, V4, w["mask4"],
                     dict(q=4, k_psum=2, k=1, v_psum=1, v=2, keys=4, context=4, context_t=4, context_sb=1), shift=True)
        attn2 = Attn(8, 1.0 / np.sqrt(2.0), V32, w["maskr"],
                     dict(q=2, k=1, v_psum=1, v=4, context=NB, context_t=NB, context_sb=1), units=4 * NB)
        attn3 = Attn(4, 1.0 / 4.0, V4, w["mask4"],
                     dict(q=2, k=1, v_psum=1, v=2, keys=4, context=4, context_t=4, context_sb=1), causal=True)
        N32 = 4 * NB

        for name in ("conv", "conv_t", "conv_n", "n0", "xn0_turned", "h0", "pe_b", "setup_pos", "p_pos", "bias1",
                     "zeros", "ones", "moe_zeros", "w1_split", "u_split", "moe0_down", "moe1_down", "x0_high", "x0_split", "x1_high",
                     "x1_split", "half_m",
                     "dve_step", "act_step", "pool_step", "rin", "rout", "first", "second", "third", "halfw",
                     "moe0", "moe1", "out",
                     "h1_psum", "h1", "h2", "h2_turned", "h2_n", "h2_nb", "xa_n", "xa_turned", "xa",
                     "pos_psum", "pos_sb", "h3_psum", "h3", "h3_nb", "y_n", "y_turned", "y", "gate_psum", "gap",
                     "egap", "gates", "gates3", "gates_turned", "gates3_turned", "gates_sb",
                     "up0", "gate_b0", "relu0", "hid0", "moe0_out", "z", "z_turned", "h4",
                     "xb_n", "xb_turned", "xb", "qk_psum", "sq", "ms", "root", "qk_n", "qk_turned",
                     "ops2", "ot", "ots", "on", "h5_psum", "h5", "xc_n", "xc_turned", "xc", "x_n",
                     "rope_psum", "rope_q", "x2_psum", "x2", "fin", "f_n", "f_turned", "f",
                     "gate1_psum", "shift1", "exp1", "gates1", "gates31", "gates1_turned", "gates1_sb",
                     "a1", "b1", "g1", "silu1", "hid1", "moe1_out", "o_sb", "o_turned", "out_ready"):
            sem(name)
        for n in range(2):
            for what in ("up", "gelu", "down"):
                sem(f"ffn{n}_{what}")
        s_x = [sem(f"patches{k}") for k in range(KC)]
        s_pos_out = [sem(f"pos_out{i}") for i in range(4)]
        s_pos_in = [sem(f"pos_in{i}") for i in range(4)]
        block = ctx.enter_context(nc.Block())

        @block.sync
        def _(sp):
            sp.dma_start(pk["first"][:], first).then_inc(sems["first"], 16)
            for k in range(KC):
                sp.dma_start(xt[:, k, :], patches[k]).then_inc(s_x[k], 16)
            sp.dma_start(pk["second"][:], second).then_inc(sems["second"], 16)
            sp.dma_start(pk["third"][:], third).then_inc(sems["third"], 16)
            sp.dma_start(pk["half"][:], half_consts).then_inc(sems["halfw"], 16)
            sp.dma_start(w2_sb[:], moe0_w2).then_inc(sems["moe0_down"], 16)
            sp.dma_start(d1_sb[:], moe1_w2).then_inc(sems["moe1_down"], 16)
            sp.wait_ge(sems["conv"], 1)
            for h in range(2):
                sp.dma_start(raw0[64 * h:64 * h + 64, :], moe0_w1).then_inc(sems["moe0"], 16)
            for h in range(2):
                sp.dma_start(raw1[64 * h:64 * h + 64, 0:H1ROWS], moe1_w1).then_inc(sems["moe1"], 16)
                sp.dma_start(raw1[64 * h:64 * h + 64, H1ROWS:2 * H1ROWS], moe1_w3).then_inc(sems["moe1"], 16)
            for u in range(4):
                sp.wait_ge(sems["pos_sb"], u + 1)
                for h in range(2):
                    sp.dma_start(pos_scratch[h, u].rearrange("g (i t) -> i g t", t=S + 1),
                                 pos_sb[u][64 * h:64 * h + 64]).then_inc(s_pos_out[u], 16)
            for u in range(4):
                sp.wait_ge(s_pos_out[u], 32)
                for h in range(2):
                    sp.dma_start(shifted[u][64 * h:64 * h + 64],
                                 pos_scratch[h, u][:, S:].rearrange("g (i t) -> i g t", t=S)
                                 ).then_inc(s_pos_in[u], 16)
            sp.wait_ge(sems["out_ready"], 1)
            sp.dma_start(out, out_n[:]).then_inc(sems["out"], 16)
            sp.wait_ge(sems["out"], 16)

        @block.tensor
        def _(pe):
            mm = nc.tensor.matmul

            def turn(dst, src):
                for q in range(NQ):
                    last = nc.tensor.transpose(dst[:, 128 * q:128 * q + 128], src[:, 128 * q:128 * q + 128], ident)
                return last

            def ffn(n, src):
                banks = [P[i] for i in (2, 3, 4, 5)]
                for f in range(2):
                    for h in range(2):
                        lhs = w["up_lo" if h == 0 else "up_hi"][:, 128 * f:128 * f + 128]
                        mm(banks[2 * f + h][:], lhs, src[:], start=True, stop=True).then_inc(sems[f"ffn{n}_up"], 1)
                for f in range(2):
                    for h in range(2):
                        pe.wait_ge(sems[f"ffn{n}_gelu"], 2 * f + h + 1)
                        last = mm(P[7][64 * h:64 * h + 64, :], w["down"][:, D * f:D * f + D], hid[2 * f + h][:],
                                  start=(f == 0), stop=(f == 1))
                last.then_inc(sems[f"ffn{n}_down"], 1)

            def values(a, src, wv):
                for b in range(NB):
                    for o in range(2):
                        last = mm(P[7][64 * o:64 * o + 64, D * b:D * b + D], src[:, S * b:S * b + S],
                                  wv[:, D * o:D * o + D], start=True, stop=True)
                last.then_inc(a.s("v_psum"), 1)

            def context_t(a, u, images):
                a.wait(pe, "context", u + 1)
                for n, b in enumerate(images):
                    for h in range(2):
                        last = mm(P[6][64 * h:64 * h + 64, S * b:S * b + S], ctx_n[u % 2][:, D * n:D * n + D],
                                  ident[:, 64 * h:64 * h + 64], start=True, stop=True)
                last.then_inc(a.s("context_t"), 1)

            def turn_probs(a, u):
                a.wait(pe, "probs", u + 1)
                if u >= 2:
                    a.wait(pe, "probs_t", u - 1)
                for x in range(4):
                    last = nc.tensor.transpose(P[2 + u % 2][:, 128 * x:128 * x + 128],
                                               prob[u % 2][:, 128 * x:128 * x + 128], ident)
                last.then_inc(a.s("turned"), 1)

            def attention(a):
                wide = 2 * (a.hd + 1)
                for step in range(a.units + 4):
                    u = step
                    if u < a.units:
                        a.wait(pe, "keys", u + 1)
                        if u == 0:
                            a.wait(pe, "q", 2)
                        if u >= 2:
                            a.wait(pe, "centred", u - 1)
                        cols = 512 // a.per
                        for n in range(a.per):
                            if a.causal:
                                mm(P[u % 2][:, cols * n:cols * n + cols], identb, w["causal"][:, 0:cols],
                                   start=True, stop=False)
                            last = mm(P[u % 2][:, cols * n:cols * n + cols], q_bd[:, a.per * u + n, :],
                                      R[u % 2][:, cols * n:cols * n + cols], start=not a.causal, stop=True)
                        last.then_inc(a.s("scores"), 1)
                    u = step - 2
                    if 0 <= u < a.units:
                        turn_probs(a, u)
                    u = step - 3
                    if 0 <= u < a.units:
                        a.wait(pe, "probs_t", u + 1)
                        if u == 0:
                            a.wait(pe, "v", 2)
                        if u >= 2:
                            a.wait(pe, "context", u - 1)
                        for x in range(4):
                            b, hp = a.per * u + x // (4 // a.per), x % (4 // a.per)
                            for h in range(2):
                                last = mm(P[4 + u % 2][64 * h:64 * h + 64, wide * x:wide * x + wide],
                                          prob_t[u % 2][:, 128 * x + 64 * h:128 * x + 64 * h + 64],
                                          a.V[:, (2 * b + h) * (a.H // 2) + hp, :], start=True, stop=True)
                        last.then_inc(a.s("mixed"), 1)
                    u = step - 4
                    if 0 <= u < a.units:
                        context_t(a, u, range(a.per * u, a.per * u + a.per))

            def project_n(src, weight, dst, done):
                for q in range(NQ):
                    last = mm(dst[:, 128 * q:128 * q + 128], src[:, 128 * q:128 * q + 128], weight,
                              start=True, stop=True)
                last.then_inc(done, 1)

            pe.wait_ge(sems["second"], 16)
            mm(P[6][:, 0:S], w["wpos"][0:64, :], w["pe_s"][0:64, :], start=True, stop=True).then_inc(sems["setup_pos"], 1)
            pe.wait_ge(sems["first"], 16)
            for k in range(KC):
                pe.wait_ge(s_x[k], 16)
                for h in range(2):
                    last = mm(P[0][64 * h:64 * h + 64, :], w["conv_w"][:, D * k:D * k + D],
                              xt[:, k, NT * h:NT * h + NT], start=(k == 0), stop=(k == KC - 1))
            last.then_inc(sems["conv"], 1)
            pe.wait_ge(sems["conv_t"], 1)
            turn(P[1], conv_t).then_inc(sems["conv_n"], 1)
            pe.wait_ge(sems["n0"], 1)
            turn(P[2], xn0).then_inc(sems["xn0_turned"], 1)
            pe.wait_ge(sems["h0"], 1)
            ffn(0, h0_t)
            pe.wait_ge(sems["ffn0_down"], 1)
            attn0.wait(pe, "context_sb", 1)
            mm(P[4][:], w["wq0"], a0_t[:], start=True, stop=True).then_inc(attn0.s("k_psum"), 1)
            mm(P[5][:], w["wk0"], a0_t[:], start=True, stop=True).then_inc(attn0.s("k_psum"), 1)
            values(attn0, a0_t, w["wv0"])
            attention(attn0)
            attn0.wait(pe, "context_sb", 2)
            mm(P[0][:], w["wp0"], ctx_t[:], start=True, stop=True).then_inc(sems["h1_psum"], 1)
            pe.wait_ge(sems["h1"], 1)
            ffn(1, h1_t)
            pe.wait_ge(sems["h2"], 1)
            turn(P[0], h2_t).then_inc(sems["h2_turned"], 1)
            pe.wait_ge(sems["xa_n"], 1)
            turn(P[1], xn).then_inc(sems["xa_turned"], 1)
            pe.wait_ge(sems["xa"], 1)
            mm(P[4][:], w["wq1"], xa_t[:], start=True, stop=True).then_inc(attn1.s("k_psum"), 1)
            mm(P[5][:], w["wk1"], xa_t[:], start=True, stop=True).then_inc(attn1.s("k_psum"), 1)
            values(attn1, xa_t, w["wv1"])
            pe.wait_ge(sems["p_pos"], 1)
            attn1.wait(pe, "q", 4)
            for u in range(4):
                if u >= 2:
                    pe.wait_ge(sems["pos_sb"], u - 1)
                for n in range(2):
                    last = mm(P[2 + u % 2][:, 256 * n:256 * n + 256], qv_bd[:, 2 * u + n, :],
                              p_pos[:].rearrange("p h t -> p (h t)"), start=True, stop=True)
                last.then_inc(sems["pos_psum"], 1)
            pe.wait_ge(sems["pos_sb"], 4)
            attention(attn1)
            attn1.wait(pe, "context_sb", 1)
            project_n(ctx_t, w["wo1"], P[0], sems["h3_psum"])
            pe.wait_ge(sems["y_n"], 1)
            turn(P[1], y_n).then_inc(sems["y_turned"], 1)
            pe.wait_ge(sems["y"], 1)
            for q in range(NQ):
                last = mm(P[7][:, 32 * q:32 * q + 32], y_t[:, 128 * q:128 * q + 128], w["gate"], start=True, stop=True)
            last.then_inc(sems["gate_psum"], 1)

            def gates_turn3(dst, wait, done):
                pe.wait_ge(sems[wait], 1)
                t = dst[:].bitcast(BF16)
                for q in range(NQ):
                    last = nc.tensor.transpose(t[:, 128 * q:128 * q + 128], gates3[:, q, :], identb)
                last.then_inc(sems[done], 1)

            pe.wait_ge(sems["gates"], 1)
            for q in range(NQ):
                last = nc.tensor.transpose(P[6][0:32, 128 * q:128 * q + 128],
                                           gates[:, 2 * q:2 * q + 2, :].rearrange("p a b -> p (a b)"), ident)
            last.then_inc(sems["gates_turned"], 1)
            gates_turn3(P[5], "gates3", "gates3_turned")
            pe.wait_ge(sems["gates_sb"], 2)
            pe.wait_ge(sems["moe0_down"], 16)
            pe.wait_ge(sems["w1_split"], 4)
            pe.wait_ge(sems["x0_split"], 2)
            mm(P[4][:], w["b2"][0:2 * E0, :], gates_t[:], start=True, stop=False, skip_group_check=True)
            UB = [P[0], P[1], P[5], P[6]]

            def down0(e):
                for h in range(2):
                    pe.wait_ge(sems["hid0"], 2 * e + h + 1)
                    last = mm(P[4][64 * h:64 * h + 64, :], w2_sb[:, D * e:D * e + D], gated[(2 * e + h) % 4][:],
                              start=False, stop=(e == E0 - 1), skip_group_check=True)
                return last

            for e in range(E0):
                for h in range(2):
                    i = 2 * e + h
                    if i >= 4:
                        pe.wait_ge(sems["relu0"], i - 3)
                    for k in range(2):
                        last = mm(UB[i % 4][:], w1_split[k][:, F0 * e:F0 * e + F0], x_split[h][:], start=(k == 0),
                                  stop=(k == 1))
                    last.then_inc(sems["up0"], 1)
                    if i >= 2:
                        pe.wait_ge(sems["hid0"], i - 1)
                    mm(P[2 + i % 2][:], w["eye3"][:, E0 * h + e:E0 * h + e + 1].to_broadcast([128, 128]),
                       gates_t3[:], start=True, stop=True).then_inc(sems["gate_b0"], 1)
                if e >= 1:
                    down0(e - 1)
            down0(E0 - 1).then_inc(sems["moe0_out"], 1)
            pe.wait_ge(sems["z"], 1)
            turn(P[0], z_t).then_inc(sems["z_turned"], 1)
            pe.wait_ge(sems["xb_n"], 1)
            turn(P[1], xn).then_inc(sems["xb_turned"], 1)
            pe.wait_ge(sems["xb"], 1)
            for q in range(NQ):
                last = mm(P[2 + q // 2][:, 256 * (q % 2):256 * (q % 2) + 256], xb_t[:, 128 * q:128 * q + 128],
                          w["wqk2"], start=True, stop=True)
                if q % 2:
                    last.then_inc(sems["qk_psum"], 1)
            values(attn2, xb_t, w["wv2"])
            pe.wait_ge(sems["qk_n"], 2)
            for o in range(2):
                for q in range(NQ):
                    last = nc.tensor.transpose(P[4 + o][:, 128 * q:128 * q + 128], qk_n[:, q, o, :], ident)
                last.then_inc(sems["qk_turned"], 1)
            a = attn2
            for step in range(N32 + 7):
                u = step
                if u < N32:
                    b, g = u // 4, u % 4
                    if g == 0:
                        pe.wait_ge(sems["ops2"], 2 * b + 2)
                    if u >= 2:
                        a.wait(pe, "centred", u - 1)
                    mm(P[u % 2][:], identb, w["causal"], start=True, stop=False)
                    mm(P[u % 2][:], L[b % 2][:, g, :], R[b % 2][:], start=False, stop=True).then_inc(a.s("scores"), 1)
                u = step - 2
                if 0 <= u < N32:
                    turn_probs(a, u)
                u = step - 3
                if 0 <= u < N32:
                    b, g = u // 4, u % 4
                    a.wait(pe, "probs_t", u + 1)
                    if u == 0:
                        a.wait(pe, "v", 4)
                    if g == 0 and b >= 2:
                        pe.wait_ge(sems["ots"], b - 1)
                    for x in range(4):
                        last = mm(P[4 + b % 2][32 * x:32 * x + 32, 128 * g:128 * g + 128],
                                  V32[:, 16 * b + 4 * g + x, :], prob_t[u % 2][:, 128 * x:128 * x + 128],
                                  start=True, stop=True)
                    last.then_inc(a.s("mixed"), 1)
                u = step - 5
                if 0 <= u < N32 and u % 4 == 3:
                    b = u // 4
                    pe.wait_ge(sems["ots"], b + 1)
                    if b >= 1:
                        a.wait(pe, "context", b)
                    for g in range(4):
                        last = nc.tensor.transpose(P[7][:, 128 * g:128 * g + 128],
                                                   out_ts[b % 2][:, 128 * g:128 * g + 128], ident)
                    last.then_inc(sems["on"], 1)
                u = step - 6
                if 0 <= u < N32 and u % 4 == 3:
                    context_t(a, u // 4, [u // 4])
            a.wait(pe, "context_sb", 1)
            project_n(ctx_t, w["wp2"], P[0], sems["h5_psum"])
            pe.wait_ge(sems["xc_n"], 1)
            turn(P[1], xn).then_inc(sems["xc_turned"], 1)
            pe.wait_ge(sems["xc"], 1)
            for bank, name in ((4, "wq3"), (5, "wqs3"), (2, "wk3"), (3, "wks3")):
                mm(P[bank][:], w[name], xc_t[:], start=True, stop=True).then_inc(sems["rope_psum"], 1)
            values(attn3, xc_t, w["wv3"])
            attention(attn3)
            attn3.wait(pe, "context_sb", 1)
            project_n(ctx_t, w["wo3"], P[0], sems["x2_psum"])
            pe.wait_ge(sems["f_n"], 1)
            turn(P[1], xn).then_inc(sems["f_turned"], 1)
            pe.wait_ge(sems["f"], 1)
            for q in range(NQ):
                last = mm(P[7][:, 16 * q:16 * q + 16], f_t[:, 128 * q:128 * q + 128], w["router"], start=True, stop=True)
            last.then_inc(sems["gate1_psum"], 1)
            gates_turn3(P[7], "gates31", "gates1_turned")
            pe.wait_ge(sems["gates1_sb"], 1)
            pe.wait_ge(sems["moe1_down"], 16)
            pe.wait_ge(sems["u_split"], 4)
            pe.wait_ge(sems["x1_split"], 2)

            def down1(t):
                rows = min(128, H1ROWS - 128 * t)
                for h in range(2):
                    pe.wait_ge(sems["hid1"], 2 * t + h + 1)
                    last = mm(P[4][64 * h:64 * h + 64, :], d1_sb[0:rows, D * t:D * t + D],
                              gated[(2 * t + h) % 4][0:rows, :], start=(t == 0), stop=(t == T1 - 1))
                return last

            for t in range(T1):
                rows = min(128, H1ROWS - 128 * t)
                for h in range(2):
                    i = 2 * t + h
                    if i >= 2:
                        pe.wait_ge(sems["silu1"], i - 1)
                    for k in range(2):
                        last = mm(P[i % 2][0:rows, :], u_split[k][:, 128 * t:128 * t + rows], x_split[h][:],
                                  start=(k == 0), stop=(k == 1))
                    last.then_inc(sems["a1"], 1)
                    if i >= 2:
                        pe.wait_ge(sems["hid1"], i - 1)
                    for k in range(2):
                        last = mm(P[2 + i % 2][0:rows, :], u_split[k][:, H1ROWS + 128 * t:H1ROWS + 128 * t + rows],
                                  x_split[h][:], start=(k == 0), stop=(k == 1))
                    last.then_inc(sems["b1"], 1)
                    mm(P[5 + i % 2][0:rows, :], w["sel1"][:, H1ROWS * h + 128 * t:H1ROWS * h + 128 * t + rows],
                       gates_t3[:], start=True, stop=True).then_inc(sems["g1"], 1)
                if t >= 1:
                    down1(t - 1)
            down1(T1 - 1).then_inc(sems["moe1_out"], 1)
            pe.wait_ge(sems["o_sb"], 1)
            turn(P[0], o_t).then_inc(sems["o_turned"], 1)

        @block.scalar
        def _(act):
            ac = nc.scalar.activation

            def gelu(n):
                for i in range(4):
                    act.wait_ge(sems[f"ffn{n}_up"], i + 1)
                    ac(hid[i][:], P[2 + i][:], ACT.Gelu_apprx_tanh,
                       bias=col["ff_b1a" if i < 2 else "ff_b1b"]).then_inc(sems[f"ffn{n}_gelu"], 1)

            def even_values(a):
                a.wait(act, "v_psum", 1)
                ac(a.V[0:64, :, 0:a.hd], P[7][0:64, :].rearrange("p (a b) -> p a b", b=a.hd),
                   ACT.Copy).then_inc(a.s("v"), 1)

            def attention(a, units):
                for step in range(units + 1):
                    u = step
                    if u < units:
                        a.wait(act, "centred", u + 1)
                        if u >= 2:
                            a.wait(act, "turned", u - 1)
                        ac(prob[u % 2][:], cen_s[u % 2][:], ACT.Exp, scale=a.scale).then_inc(a.s("probs"), 1)
                    u = step - 1
                    if 0 <= u < units:
                        a.wait(act, "turned", u + 1)
                        if u >= 2:
                            a.wait(act, "mixed", u - 1)
                        ac(prob_t[u % 2][:], P[2 + u % 2][:], ACT.Copy).then_inc(a.s("probs_t"), 1)
                        if units == N32 and u % 4 == 1 and u > 4:
                            gather(u // 4 - 1)
                if units == N32:
                    gather(NB - 1)

            def gather(b):
                attn2.wait(act, "mixed", 4 * b + 4)
                if b >= 2:
                    act.wait_ge(sems["on"], b - 1)
                ac(out_ts[b % 2][:], P[4 + b % 2][:], ACT.Copy).then_inc(sems["ots"], 1)

            act.wait_ge(sems["first"], 16)
            act.wait_ge(sems["conv"], 1)
            ac(conv_t[:], P[0][:], ACT.Identity, bias=col["conv_b"]).then_inc(sems["conv_t"], 1)
            gelu(0)
            act.wait_ge(sems["second"], 16)
            act.wait_ge(sems["zeros"], 5)
            attn0.wait(act, "k_psum", 2)
            ac(k_t[:], P[5][:], ACT.Identity, bias=col["bk0"]).then_inc(attn0.s("k"), 1)
            ac(q_bd[0:64, :, 0:64], heads(P[4][0:64, :], NB), ACT.Identity,
               bias=col["bq0"][0:64]).then_inc(attn0.s("q"), 1)
            even_values(attn0)
            attention(attn0, attn0.units)
            attn0.wait(act, "context_t", attn0.units)
            ac(ctx_t[:], P[6][:], ACT.Identity, bias=col["bv0"]).then_inc(attn0.s("context_sb"), 1)
            gelu(1)
            act.wait_ge(sems["h2_turned"], 1)
            ac(h2_n[:], P[0][:], ACT.Copy).then_inc(sems["h2_n"], 1)
            act.wait_ge(sems["xa_turned"], 1)
            ac(xa_t[:], P[1][:], ACT.Identity, bias=col["beta1"], scale=col["gamma1"]).then_inc(sems["xa"], 1)
            act.wait_ge(sems["bias1"], 2)
            attn1.wait(act, "k_psum", 1)
            ac(qv_bd[0:64, :, 0:64], heads(P[4][0:64, :], NB), ACT.Identity,
               bias=bqv[0:64]).then_inc(attn1.s("q"), 1)
            ac(q_bd[0:64, :, 0:64], heads(P[4][0:64, :], NB), ACT.Identity,
               bias=bqu[0:64]).then_inc(attn1.s("q"), 1)
            attn1.wait(act, "k_psum", 2)
            ac(k_t[:], P[5][:], ACT.Identity, bias=col["bk1"]).then_inc(attn1.s("k"), 1)
            even_values(attn1)
            for u in range(4):
                act.wait_ge(sems["pos_psum"], u + 1)
                ac(pos_sb[u][:, :, 1:S + 1], heads(P[2 + u % 2][:], 8), ACT.Copy).then_inc(sems["pos_sb"], 1)
            attention(attn1, attn1.units)
            attn1.wait(act, "context_t", attn1.units)
            ac(ctx_t[:], P[6][:], ACT.Identity, bias=col["bv1"]).then_inc(attn1.s("context_sb"), 1)
            act.wait_ge(sems["third"], 16)
            act.wait_ge(sems["y_turned"], 1)
            ac(y_t[:], P[1][:], ACT.Copy).then_inc(sems["y"], 1)
            act.wait_ge(sems["gap"], 1)
            ac(egap[:], gap[:], ACT.Exp).then_inc(sems["egap"], 1)
            act.wait_ge(sems["gates_turned"], 1)
            ac(gates_t[:], P[6][0:32, :], ACT.Copy).then_inc(sems["gates_sb"], 1)
            UB = [P[0], P[1], P[5], P[6]]
            for i in range(2 * E0):
                act.wait_ge(sems["up0"], i + 1)
                if i >= 2:
                    act.wait_ge(sems["hid0"], i - 1)
                ac(relu_h[i % 2][:], UB[i % 4][:], ACT.Relu,
                   bias=w["b1"][:, i // 2:i // 2 + 1]).then_inc(sems["relu0"], 1)
            act.wait_ge(sems["moe_zeros"], 6)
            act.wait_ge(sems["xb_turned"], 1)
            ac(xb_t[:], P[1][:], ACT.Copy).then_inc(sems["xb"], 1)
            for n in range(2):
                act.wait_ge(sems["qk_psum"], n + 1)
                ac(sq[:, 512 * n:512 * n + 512], P[2 + n][:], ACT.Square).then_inc(sems["sq"], 1)
            attn2.wait(act, "v_psum", 1)
            v_in = P[7][:].rearrange("p (b h g d) -> p b h g d", b=NB, h=2, d=2)
            v_out = V32.rearrange("p (b g) c -> p b g c", b=NB)
            for h in range(2):
                ac(v_out[0:64, :, :, 6 * h:6 * h + 2], v_in[0:64, :, h], ACT.Copy).then_inc(attn2.s("v"), 1)
            act.wait_ge(sems["ms"], 2)
            ac(qk_r, qk_ms, ACT.Sqrt).then_inc(sems["root"], 1)
            act.wait_ge(sems["qk_turned"], 1)
            ac(q_bd[0:64, :, 0:64], heads(P[4][0:64, :], NB), ACT.Copy,
               scale=col["qn"][0:64]).then_inc(attn2.s("q"), 1)
            act.wait_ge(sems["qk_turned"], 2)
            ac(k_t[:], P[5][:], ACT.Copy, scale=col["kn"]).then_inc(attn2.s("k"), 1)
            attention(attn2, N32)
            attn2.wait(act, "context_t", NB)
            ac(ctx_t[:], P[6][:], ACT.Copy).then_inc(attn2.s("context_sb"), 1)
            act.wait_ge(sems["xc_turned"], 1)
            ac(xc_t[:], P[1][:], ACT.Copy, scale=col["ln1"]).then_inc(sems["xc"], 1)
            even_values(attn3)
            attention(attn3, attn3.units)
            attn3.wait(act, "context_t", attn3.units)
            ac(ctx_t[:], P[6][:], ACT.Copy).then_inc(attn3.s("context_sb"), 1)
            act.wait_ge(sems["f_turned"], 1)
            ac(f_t[:], P[1][:], ACT.Copy, scale=col["ln2"]).then_inc(sems["f"], 1)
            act.wait_ge(sems["shift1"], 1)
            ac(resid[:, :, 0:E1], logit[:, :, 0:E1], ACT.Exp).then_inc(sems["exp1"], 1)
            for i in range(2 * T1):
                rows = min(128, H1ROWS - 128 * (i // 2))
                act.wait_ge(sems["a1"], i + 1)
                if i >= 2:
                    act.wait_ge(sems["hid1"], i - 1)
                ac(relu_h[i % 2][0:rows, :], P[i % 2][0:rows, :], ACT.Silu).then_inc(sems["silu1"], 1)
            act.wait_ge(sems["moe1_out"], 1)
            ac(o_t[:], P[4][:], ACT.Copy).then_inc(sems["o_sb"], 1)

        @block.vector
        def _(dve):
            v = nc.vector
            steps = [0]

            def link(ins):
                steps[0] += 1
                ins.then_inc(sems["dve_step"], 1)
                dve.wait_ge(sems["dve_step"], steps[0])

            def link_all(ins):
                steps[0] += 1
                ins.then_inc(sems["dve_step"], 1)

            def moments(src):
                for g in range(8):
                    link_all(v.bn_stats(stats[:, g, :], src[:, D * g:D * g + D]))
                dve.wait_ge(sems["dve_step"], steps[0])
                for g in range(8):
                    link_all(v.bn_aggr(mv[:, g, :], stats[:, g, :]))
                dve.wait_ge(sems["dve_step"], steps[0])

            powers = [0]

            def root(n):
                powers[0] += 1
                dve.wait_ge(sems["rout"], powers[0])

            def centre(src):
                link(v.tensor_tensor(heads(centred[:], 8), heads(src, 8), over(mv[:, :, 0], D), ALU.subtract))

            def scaled(dst, r):
                return v.tensor_tensor(heads(dst, 8), heads(centred[:], 8), over(r, D), ALU.mult)

            EPS = 1e-5

            def double_norm(src, dst, done, eps2):
                moments(src)
                v.tensor_scalar(rin[:, 0:8], mv[:, :, 1], 1.0 + eps2, EPS * eps2, ALU.mult,
                                ALU.add).then_inc(sems["rin"], 1)
                centre(src)
                root(1)
                scaled(dst, rout[:, 0:8]).then_inc(done, 1)

            def odd_values(a):
                a.wait(dve, "v_psum", 1)
                v.tensor_copy(a.V[64:128, :, a.hd + 1:2 * a.hd + 1],
                              P[7][64:128, :].rearrange("p (a b) -> p a b", b=a.hd)).then_inc(a.s("v"), 1)

            def centre_scores(a, u):
                a.wait(dve, "scores", u + 1)
                if u >= 2:
                    a.wait(dve, "probs", u - 1)
                src = P[u % 2][:]
                if a.shift:
                    dve.wait_ge(s_pos_in[u], 32)
                    src = cen_s[u % 2][:]
                    link(v.tensor_tensor(src, P[u % 2][:], shifted[u].rearrange("p g t -> p (g t)"), ALU.add))
                link(v.tensor_reduce(rowmax[u % 2][:], heads(src, 8), AX.X, ALU.max))
                v.tensor_tensor(heads(cen_s[u % 2][:], 8), heads(src, 8), over(rowmax[u % 2][:], S),
                                ALU.subtract).then_inc(a.s("centred"), 1)

            def normalise(a, u):
                a.wait(dve, "mixed", u + 1)
                if u >= 2:
                    a.wait(dve, "context_t", u - 1)
                o = P[4 + u % 2][:, 0:8 * (a.hd + 1)].rearrange("p (g d) -> p g d", g=8)
                link(v.reciprocal(rowsum[u % 2][:, 0:8], o[:, :, a.hd]))
                v.tensor_tensor(ctx_n[u % 2][:, 0:8 * a.hd].rearrange("p (g d) -> p g d", g=8), o[:, :, 0:a.hd],
                                over(rowsum[u % 2][:, 0:8], a.hd), ALU.mult).then_inc(a.s("context"), 1)

            def attention(a):
                for step in range(a.units + 3):
                    if step < a.units:
                        centre_scores(a, step)
                    if step >= 3:
                        normalise(a, step - 3)

            def one_hots(n, done):
                iota = each(w["iota"][:, 0:n], 8)
                for k in range(2):
                    link_all(v.tensor_tensor(hot[k][:, :, 0:n], iota, over(topf[:, :, k], n), ALU.is_equal))
                dve.wait_ge(sems["dve_step"], steps[0])
                for k in range(2):
                    link_all(v.tensor_tensor(hot[k][:, :, 0:n], hot[k][:, :, 0:n], over(w12[:, :, k], n), ALU.mult))
                dve.wait_ge(sems["dve_step"], steps[0])
                v.tensor_tensor(gates[:, :, 0:n], hot[0][:, :, 0:n], hot[1][:, :, 0:n],
                                ALU.add).then_inc(sems[done], 1)
                dve.wait_ge(sems[done], 1)

            def split3(n, done):
                def part(k):
                    return gates3[:, :, 2 * n * k:2 * n * k + 2 * n].rearrange("p q (h e) -> p q h e", h=2)
                g = gates[:, :, 0:n].rearrange("p (q h) e -> p q h e", h=2)
                r = resid[:, :, 0:n].rearrange("p (q h) e -> p q h e", h=2)
                link(v.tensor_copy(part(0), g))
                link(v.tensor_tensor(r, g, part(0), ALU.subtract))
                link(v.tensor_copy(part(1), r))
                v.tensor_tensor(part(2), r, part(1), ALU.subtract).then_inc(sems[done], 1)

            def split_x(src, ready, done):
                dve.wait_ge(sems[ready], 1)
                for h in range(2):
                    p = slice(64 * h, 64 * h + 64)
                    link_all(v.tensor_copy(x_split[h][p, :], src[p, :]))
                dve.wait_ge(sems["dve_step"], steps[0])
                for h in range(2):
                    p, other = slice(64 * h, 64 * h + 64), slice(64 - 64 * h, 128 - 64 * h)
                    v.tensor_tensor(x_split[h][other, :], src[p, :], x_split[h][p, :].bitcast(F32),
                                    ALU.subtract).then_inc(sems[done], 1)

            dve.wait_ge(sems["second"], 16)
            dve.wait_ge(sems["setup_pos"], 1)
            v.tensor_tensor(p_pos[:], each(P[6][:, 0:S], 4), over(w["mask4"], S), ALU.mult).then_inc(sems["p_pos"], 1)
            dve.wait_ge(sems["conv_n"], 1)
            moments(P[1])
            v.tensor_scalar(rin[:, 0:8], mv[:, :, 1], EPS, None, ALU.add).then_inc(sems["rin"], 1)
            centre(P[1][:])
            root(1)
            scaled(xn0[:], rout[:, 0:8]).then_inc(sems["n0"], 1)
            dve.wait_ge(sems["xn0_turned"], 1)
            dve.wait_ge(sems["pe_b"], 1)
            v.scalar_tensor_tensor(out=heads(h0_t[:], NB), in0=heads(P[2][:], NB), scalar=col["ln_w"],
                                   in1=each(pe_b[:], NB), op0=ALU.mult, op1=ALU.add).then_inc(sems["h0"], 1)
            dve.wait_ge(sems["ffn0_down"], 1)
            v.tensor_scalar(a0_t[:], P[7][:], col["ff_b2"], None, ALU.add).then_inc(attn0.s("context_sb"), 1)
            dve.wait_ge(sems["zeros"], 5)
            attn0.wait(dve, "k_psum", 1)
            v.tensor_scalar(q_bd[64:128, :, 64:128], heads(P[4][64:128, :], NB), col["bq0"][64:128], None,
                            ALU.add).then_inc(attn0.s("q"), 1)
            odd_values(attn0)
            attention(attn0)
            dve.wait_ge(sems["h1_psum"], 1)
            v.scalar_tensor_tensor(out=h1_t[:], in0=P[0][:], scalar=col["bp0"], in1=h0_t[:], op0=ALU.add,
                                   op1=ALU.add).then_inc(sems["h1"], 1)
            dve.wait_ge(sems["h1"], 1)
            dve.wait_ge(sems["ffn1_down"], 1)
            v.scalar_tensor_tensor(out=h2_t[:], in0=P[7][:], scalar=col["ff_b2"], in1=h1_t[:], op0=ALU.add,
                                   op1=ALU.add).then_inc(sems["h2"], 1)
            dve.wait_ge(sems["h2_n"], 1)
            double_norm(h2_n[:], xn[:], sems["xa_n"], EPS)
            dve.wait_ge(sems["bias1"], 2)
            attn1.wait(dve, "k_psum", 1)
            v.tensor_scalar(qv_bd[64:128, :, 64:128], heads(P[4][64:128, :], NB), bqv[64:128], None,
                            ALU.add).then_inc(attn1.s("q"), 1)
            v.tensor_scalar(q_bd[64:128, :, 64:128], heads(P[4][64:128, :], NB), bqu[64:128], None,
                            ALU.add).then_inc(attn1.s("q"), 1)
            odd_values(attn1)
            attention(attn1)
            dve.wait_ge(sems["h3_psum"], 1)
            dve.wait_ge(sems["h2_nb"], 1)
            v.tensor_tensor(h3_n[:], P[0][:], h2_nb[:], ALU.add).then_inc(sems["h3"], 1)
            dve.wait_ge(sems["h3"], 1)
            moments(h3_n)
            v.tensor_scalar(rin[:, 0:8], mv[:, :, 1], EPS, None, ALU.add).then_inc(sems["rin"], 1)
            centre(h3_n[:])
            root(1)
            scaled(y_n[:], rout[:, 0:8]).then_inc(sems["y_n"], 1)
            split_x(y_t, "y", "x0_split")
            dve.wait_ge(sems["third"], 16)
            dve.wait_ge(sems["gate_psum"], 1)
            link(v.tensor_tensor(logit[:], P[7][:, 0:8 * E0].rearrange("p (g e) -> p g e", g=8),
                                 each(w["gate_b"], 8), ALU.add))
            for g in range(8):
                link_all(v.max(top8[:, g, :], logit[:, g, :]))
            dve.wait_ge(sems["dve_step"], steps[0])
            for g in range(8):
                link_all(v.max_index(top8i[:, g, :], top8[:, g, :], logit[:, g, :]))
            v.tensor_tensor(gap[:], top8[:, :, 1], top8[:, :, 0], ALU.subtract).then_inc(sems["gap"], 1)
            dve.wait_ge(sems["dve_step"], steps[0])
            link(v.tensor_copy(topf[:], top8i[:]))
            dve.wait_ge(sems["egap"], 1)
            link(v.tensor_scalar(wsum[:], egap[:], 1.0, None, ALU.add))
            link(v.reciprocal(w12[:, :, 0], wsum[:]))
            link(v.tensor_tensor(w12[:, :, 1], w12[:, :, 0], egap[:], ALU.mult))
            one_hots(E0, "gates")
            dve.wait_ge(sems["zeros"], 5)
            split3(E0, "gates3")
            dve.wait_ge(sems["gates3_turned"], 1)
            v.tensor_copy(gates_t3[:], P[5][:].bitcast(BF16)[:, 0:NT]).then_inc(sems["gates_sb"], 1)
            for i in range(2 * E0):
                dve.wait_ge(sems["relu0"], i + 1)
                dve.wait_ge(sems["gate_b0"], i + 1)
                v.tensor_tensor(gated[i % 4][:], P[2 + i % 2][:], relu_h[i % 2][:], ALU.mult).then_inc(sems["hid0"], 1)
            dve.wait_ge(sems["moe0_out"], 1)
            v.tensor_tensor(z_t[:], P[4][:], y_t[:], ALU.add).then_inc(sems["z"], 1)
            dve.wait_ge(sems["z_turned"], 1)
            moments(P[0])
            v.tensor_scalar(rin[:, 0:8], mv[:, :, 1], EPS, None, ALU.add).then_inc(sems["rin"], 1)
            centre(P[0][:])
            root(1)
            link(scaled(xn[:], rout[:, 0:8]))
            link(v.tensor_tensor(heads(centred[:], 8), heads(xn[:], 8), each(w["gamma"], 8), ALU.mult))
            dve.wait_ge(sems["h3_nb"], 1)
            v.tensor_tensor(h4_n[:], centred[:], h3_nb[:], ALU.add).then_inc(sems["h4"], 1)
            dve.wait_ge(sems["h4"], 1)
            moments(h4_n)
            v.tensor_scalar(rin[:, 0:8], mv[:, :, 1], EPS, None, ALU.add).then_inc(sems["rin"], 1)
            centre(h4_n[:])
            root(1)
            scaled(xn[:], rout[:, 0:8]).then_inc(sems["xb_n"], 1)
            for n in range(2):
                dve.wait_ge(sems["sq"], n + 1)
                pair = sq[:, 512 * n:512 * n + 512].rearrange("p (a d) -> p a d", d=2)
                link(v.tensor_tensor(qk_ms[:, 256 * n:256 * n + 256], pair[:, :, 0], pair[:, :, 1], ALU.add))
                v.tensor_scalar(qk_ms[:, 256 * n:256 * n + 256], qk_ms[:, 256 * n:256 * n + 256], 0.5, 1e-6,
                                ALU.mult, ALU.add).then_inc(sems["ms"], 1)
            attn2.wait(dve, "v_psum", 1)
            v_in = P[7][:].rearrange("p (b h g d) -> p b h g d", b=NB, h=2, d=2)
            v_out = V32.rearrange("p (b g) c -> p b g c", b=NB)
            for h in range(2):
                v.tensor_copy(v_out[64:128, :, :, 6 * h + 3:6 * h + 5], v_in[64:128, :, h]).then_inc(attn2.s("v"), 1)
            dve.wait_ge(sems["root"], 1)
            link(v.reciprocal(qk_ms, qk_r))
            for n in range(2):
                v.tensor_tensor(qk_n[:, 2 * n:2 * n + 2].rearrange("p q o (a d) -> p (q o a) d", d=2),
                                P[2 + n][:].rearrange("p (a d) -> p a d", d=2),
                                over(qk_ms[:, 256 * n:256 * n + 256], 2), ALU.mult).then_inc(sems["qk_n"], 1)
            dve.wait_ge(sems["qk_turned"], 1)
            v.tensor_scalar(q_bd[64:128, :, 64:128], heads(P[4][64:128, :], NB), col["qn"][64:128], None,
                            ALU.mult).then_inc(attn2.s("q"), 1)

            def normalise32(b):
                dve.wait_ge(sems["on"], b + 1)
                if b >= 2:
                    attn2.wait(dve, "context_t", b - 1)
                o = P[7][:].rearrange("p (a c) -> p a c", c=32)
                rs = rowsum[b % 2][:].rearrange("p (a o) -> p a o", o=2)
                cn = ctx_n[b % 2][:, 0:D].rearrange("p (a o d) -> p a o d", o=2, d=2)
                for h in range(2):
                    p = slice(64 * h, 64 * h + 64)
                    of = o[p, :, 6 * h:6 * h + 6].rearrange("p a (o d) -> p a o d", o=2)
                    link_all(v.reciprocal(rs[p], of[:, :, :, 2]))
                dve.wait_ge(sems["dve_step"], steps[0])
                for h in range(2):
                    p = slice(64 * h, 64 * h + 64)
                    of = o[p, :, 6 * h:6 * h + 6].rearrange("p a (o d) -> p a o d", o=2)
                    last = v.tensor_tensor(cn[p], of[:, :, :, 0:2],
                                           rs[p].unsqueeze(3).to_broadcast([64, 16, 2, 2]), ALU.mult)
                    if h == 0:
                        link_all(last)
                last.then_inc(attn2.s("context"), 1)

            for step in range(N32 + 7):
                if step < N32:
                    centre_scores(attn2, step)
                u = step - 6
                if 0 <= u < N32 and u % 4 == 3:
                    normalise32(u // 4)
            dve.wait_ge(sems["h5_psum"], 1)
            v.tensor_tensor(h5_n[:], P[0][:], h4_n[:], ALU.add).then_inc(sems["h5"], 1)
            dve.wait_ge(sems["h5"], 1)
            moments(h5_n)
            link(v.tensor_scalar(rin[:, 8:16], mv[:, :, 1], EPS, None, ALU.add))
            v.tensor_scalar(rin[:, 0:8], mv[:, :, 1], 1.0 + 1e-6, EPS * 1e-6, ALU.mult,
                            ALU.add).then_inc(sems["rin"], 1)
            centre(h5_n[:])
            root(1)
            scaled(xn[:], rout[:, 0:8]).then_inc(sems["xc_n"], 1)
            scaled(x_n[:], rout[:, 8:16]).then_inc(sems["x_n"], 1)
            for i, bank in enumerate((4, 5, 2, 3)):
                dve.wait_ge(sems["rope_psum"], i + 1)
                link_all(v.tensor_tensor(heads(rope[i], NB), heads(P[bank][:], NB),
                                         each(w["rope_c" if i % 2 == 0 else "rope_s"], NB), ALU.mult))
                if i == 1:
                    dve.wait_ge(sems["dve_step"], steps[0])
                    for h in range(2):
                        p = slice(64 * h, 64 * h + 64)
                        v.tensor_tensor(q_bd[p, :, 64 * h:64 * h + 64], heads(rope[0][p, :], NB),
                                        heads(rope[1][p, :], NB), ALU.add).then_inc(attn3.s("q"), 1)
            dve.wait_ge(sems["dve_step"], steps[0])
            v.tensor_tensor(k_t[:], rope[2], rope[3], ALU.add).then_inc(attn3.s("k"), 1)
            odd_values(attn3)
            attention(attn3)
            dve.wait_ge(sems["x2_psum"], 1)
            dve.wait_ge(sems["x_n"], 1)
            v.tensor_tensor(x2_n[:], P[0][:], x_n[:], ALU.add).then_inc(sems["x2"], 1)
            dve.wait_ge(sems["x2"], 1)
            moments(x2_n)
            link(v.tensor_tensor(msq[:], mv[:, :, 0], mv[:, :, 0], ALU.mult))
            link(v.scalar_tensor_tensor(out=rin[:, 0:8], in0=mv[:, :, 1], scalar=1e-6, in1=msq[:], op0=ALU.add,
                                        op1=ALU.add))
            v.tensor_copy(rin[:, 8:16], rin[:, 0:8]).then_inc(sems["rin"], 1)
            root(1)
            v.tensor_tensor(heads(xn[:], 8), heads(x2_n[:], 8), over(rout[:, 0:8], D), ALU.mult).then_inc(sems["f_n"], 1)
            split_x(f_t, "f", "x1_split")
            dve.wait_ge(sems["gate1_psum"], 1)
            lg = P[7][:, 0:8 * E1].rearrange("p (g e) -> p g e", g=8)
            link(v.tensor_reduce(gap[:], lg, AX.X, ALU.max))
            v.tensor_tensor(logit[:, :, 0:E1], lg, over(gap[:], E1), ALU.subtract).then_inc(sems["shift1"], 1)
            dve.wait_ge(sems["exp1"], 1)
            link(v.tensor_reduce(wsum[:], resid[:, :, 0:E1], AX.X, ALU.add))
            link(v.reciprocal(gap[:], wsum[:]))
            link(v.tensor_tensor(logit[:, :, 0:E1], resid[:, :, 0:E1], over(gap[:], E1), ALU.mult))
            for g in range(8):
                link_all(v.max(top8[:, g, :], logit[:, g, 0:E1]))
            dve.wait_ge(sems["dve_step"], steps[0])
            for g in range(8):
                link_all(v.max_index(top8i[:, g, :], top8[:, g, :], logit[:, g, 0:E1]))
            link_all(v.tensor_tensor(wsum[:], top8[:, :, 0], top8[:, :, 1], ALU.add))
            dve.wait_ge(sems["dve_step"], steps[0])
            link_all(v.tensor_copy(topf[:], top8i[:]))
            link(v.tensor_scalar(wsum[:], wsum[:], 1e-9, None, ALU.add))
            link(v.reciprocal(gap[:], wsum[:]))
            link(v.tensor_tensor(w12[:], top8[:, :, 0:2], over(gap[:], 2), ALU.mult))
            one_hots(E1, "gates1")
            dve.wait_ge(sems["half_m"], 2)
            split3(E1, "gates31")
            dve.wait_ge(sems["gates1_turned"], 1)
            v.tensor_copy(gates_t3[:], P[7][:].bitcast(BF16)[:, 0:NT]).then_inc(sems["gates1_sb"], 1)
            for i in range(2 * T1):
                rows = min(128, H1ROWS - 128 * (i // 2))
                dve.wait_ge(sems["silu1"], i + 1)
                dve.wait_ge(sems["b1"], i + 1)
                link(v.tensor_tensor(relu_h[i % 2][0:rows, :], P[2 + i % 2][0:rows, :], relu_h[i % 2][0:rows, :],
                                     ALU.mult))
                dve.wait_ge(sems["g1"], i + 1)
                v.tensor_tensor(gated[i % 4][0:rows, :], P[5 + i % 2][0:rows, :], relu_h[i % 2][0:rows, :],
                                ALU.mult).then_inc(sems["hid1"], 1)
            dve.wait_ge(sems["o_turned"], 1)
            dve.wait_ge(sems["fin"], 1)
            v.tensor_tensor(out_n[:], P[0][:], fin_n[:], ALU.add).then_inc(sems["out_ready"], 1)

        @block.gpsimd
        def _(pool):
            g = nc.gpsimd
            n_pow = [0]

            def power(cols):
                n_pow[0] += 1
                pool.wait_ge(sems["rin"], n_pow[0])
                g.tensor_tensor(rout[:, 0:cols], rin[:, 0:cols], minus_half[:, 0:cols],
                                ALU.pow).then_inc(sems["rout"], 1)

            def keys(a):
                cols = S * a.per
                for u in range(a.units):
                    if u == 0:
                        a.wait(pool, "k", 1)
                    if u >= 2:
                        a.wait(pool, "scores", u - 1)
                    for n in range(a.per):
                        b = a.per * u + n
                        ins = g.tensor_tensor(
                            R[u % 2][:, 512 // a.per * n:512 // a.per * (n + 1)].rearrange("p (h j) -> p h j", j=S),
                            each(k_t[:, S * b:S * b + S], a.H), over(a.mask, S), ALU.mult)
                    ins.then_inc(a.s("keys"), 1)

            def split_weights(raw, split, loaded, n, done):
                pool.wait_ge(sems[loaded], n)
                for h in range(2):
                    p = slice(64 * h, 64 * h + 64)
                    g.tensor_copy(split[h][p, :], raw[p, :]).then_inc(sems[done], 1)
                pool.wait_ge(sems[done], 2)
                for h in range(2):
                    p = slice(64 * h, 64 * h + 64)
                    g.tensor_tensor(split[1 - h][p, :], raw[p, :], split[h][p, :].bitcast(F32),
                                    ALU.subtract).then_inc(sems[done], 1)
                pool.wait_ge(sems[done], 4)

            g.memset(minus_half[:], -0.5).then_inc(sems["half_m"], 1)
            g.memset(q_bd[:], 0.0).then_inc(sems["zeros"], 1)
            g.memset(V0[:], 0.0).then_inc(sems["zeros"], 1)
            g.memset(qv_bd[:], 0.0).then_inc(sems["zeros"], 1)
            pool.wait_ge(sems["zeros"], 3)
            g.memset(V0[0:64, :, 8:9], 1.0).then_inc(sems["zeros"], 1)
            g.memset(V0[64:128, :, 17:18], 1.0).then_inc(sems["zeros"], 1)
            pool.wait_ge(sems["zeros"], 5)
            pool.wait_ge(sems["first"], 16)
            g.tensor_scalar(pe_b[:], w["pe_t"], col["ln_b"], None, ALU.add).then_inc(sems["pe_b"], 1)
            pool.wait_ge(sems["half_m"], 1)
            power(8)
            g.memset(V4[:], 0.0).then_inc(sems["ones"], 1)
            for i in range(4):
                g.memset(pos_sb[i], 0.0).then_inc(sems["ones"], 1)
            pool.wait_ge(sems["ones"], 5)
            g.memset(V4[0:64, :, 16:17], 1.0).then_inc(sems["ones"], 1)
            g.memset(V4[64:128, :, 33:34], 1.0).then_inc(sems["ones"], 1)
            pool.wait_ge(sems["ones"], 7)
            keys(attn0)
            attn0.wait(pool, "keys", attn0.units)
            split_weights(raw0, w1_split, "moe0", 32, "w1_split")
            pool.wait_ge(sems["second"], 16)
            g.tensor_tensor(bqv[:], col["bq1"], col["v1"], ALU.add).then_inc(sems["bias1"], 1)
            g.tensor_tensor(bqu[:], col["bq1"], col["u1"], ALU.add).then_inc(sems["bias1"], 1)
            power(8)
            pool.wait_ge(sems["h2_n"], 1)
            g.tensor_tensor(heads(h2_nb[:], 8), heads(h2_n[:], 8), each(w["bout"], 8), ALU.add).then_inc(sems["h2_nb"], 1)
            keys(attn1)
            g.memset(gates3[:], 0.0).then_inc(sems["moe_zeros"], 1)
            power(8)
            pool.wait_ge(sems["third"], 16)
            g.tensor_tensor(heads(h3_nb[:], 8), heads(h3_n[:], 8), each(w["beta"], 8), ALU.add).then_inc(sems["h3_nb"], 1)
            pool.wait_ge(sems["h3_nb"], 1)
            split_weights(raw1, u_split, "moe1", 64, "u_split")
            g.memset(V32, 0.0).then_inc(sems["moe_zeros"], 1)
            pool.wait_ge(sems["moe_zeros"], 2)
            for h in range(2):
                g.memset(V32[0:64, :, 6 * h + 2:6 * h + 3], 1.0).then_inc(sems["moe_zeros"], 1)
                g.memset(V32[64:128, :, 6 * h + 5:6 * h + 6], 1.0).then_inc(sems["moe_zeros"], 1)
            pool.wait_ge(sems["moe_zeros"], 6)
            power(8)
            power(8)
            attn2.wait(pool, "k", 1)
            attn2.wait(pool, "q", 2)
            for b in range(NB):
                if b >= 2:
                    attn2.wait(pool, "scores", 4 * (b - 1))
                g.tensor_tensor(heads(R[b % 2][:], 8), each(k_t[:, S * b:S * b + S], 8), over(w["maskr"], S),
                                ALU.mult).then_inc(sems["ops2"], 1)
                g.tensor_tensor(L[b % 2], each(q_bd[:, b, :], 4), over(w["maskg"], 128),
                                ALU.mult).then_inc(sems["ops2"], 1)
            power(16)
            keys(attn3)
            pool.wait_ge(sems["x2"], 1)
            g.tensor_tensor(fin_n[:], x2_n[:], h5_n[:], ALU.add).then_inc(sems["fin"], 1)
            g.memset(gates3[:], 0.0).then_inc(sems["half_m"], 1)
            power(16)


def block_diagonal(a):
    k, n = a.shape
    out = np.zeros((2 * k, 2 * n), a.dtype)
    out[:k, :n] = a
    out[k:, n:] = a
    return out


def rows128(a):
    out = np.zeros((128, a.shape[1]), a.dtype)
    out[:a.shape[0]] = a
    return out


def twice(a):
    return np.concatenate([a, a], axis=0)


def value_weights(wv, H):
    d = D // H
    v = wv.reshape(D, H // 2, 2, d)
    return np.concatenate([block_diagonal(np.ascontiguousarray(v[:, :, o, :]).reshape(D, D // 2)) for o in range(2)],
                          axis=1)


def angles(n, positions):
    i = np.arange(0, n, 2, dtype=np.float32)
    return i, np.arange(positions, dtype=np.float32)[:, None]


def lay_out(a):
    f = np.float32
    a = {k: np.asarray(v) for k, v in a.items()}
    x = a["x"].reshape(B, C, IMG // PATCH, PATCH, IMG // PATCH, PATCH)
    patches = np.ascontiguousarray(x.transpose(1, 3, 5, 0, 2, 4)).reshape(KC, 128, 2 * NT)

    i, pos = angles(D, S)
    div = np.exp(-np.log(f(10000.0)) * i / f(D)).astype(f)
    pe = np.zeros((S, D), f)
    pe[:, 0::2], pe[:, 1::2] = np.sin(pos * div), np.cos(pos * div)
    div1 = np.exp(i * f(-np.log(10000.0) / D)).astype(f)
    pe1 = np.zeros((S, D), f)
    pe1[:, 0::2], pe1[:, 1::2] = np.sin(pos * div1), np.cos(pos * div1)

    c = np.arange(D)

    def mask(n, of):
        return twice((of[:, None] == np.arange(n)[None, :]).astype(f))

    def column(*cols):
        return np.stack([twice(x.reshape(-1, 1))[:, 0] if x.size == D else x.reshape(-1) for x in cols], axis=1)

    def pad(m, n):
        return np.concatenate([m, np.zeros((128, n - m.shape[1]), m.dtype)], axis=1)

    qkv = a["L0_tok_qkv_w"].T
    qkv_b = a["L0_tok_qkv_b"]
    ffup = a["L0_tok_ff_w1"].T
    zero = np.zeros((D, FF), f)
    ffb = a["L0_tok_ff_b1"]
    qn, kn = (np.tile(a[f"L1_attn_{n}n_w"], D // 2) for n in "qk")
    first = {
        "conv_w": a["L0_tok_conv_w"].reshape(D, KC, 128).transpose(2, 1, 0).reshape(128, KC * D),
        "ident": np.eye(128, dtype=f),
        "cols0": pad(column(a["L0_tok_conv_b"], a["L0_tok_ln_w"], a["L0_tok_ln_b"], ffb[:128], ffb[128:],
                            a["L0_tok_ff_b2"]), 8),
        "pe_t": twice(pe.T),
        "up_lo": np.concatenate([ffup, zero]), "up_hi": np.concatenate([zero, ffup]),
        "down": a["L0_tok_ff_w2"].T.reshape(2, 128, D).transpose(1, 0, 2).reshape(128, 2 * D),
    }
    second = {
        "wq0": block_diagonal(qkv[:, :D]), "wk0": block_diagonal(qkv[:, D:2 * D]),
        "wv0": value_weights(qkv[:, 2 * D:], 8), "wp0": block_diagonal(a["L0_tok_proj_w"].T),
        "cols1": pad(column(qkv_b[:D], qkv_b[D:2 * D], qkv_b[2 * D:], a["L0_tok_proj_b"], a["L0_attn_ln_gamma"],
                            a["L0_attn_ln_beta"], a["L0_attn_bq"], a["L0_attn_bk"], a["L0_attn_bv"],
                            a["L0_attn_u_bias"].reshape(-1), a["L0_attn_v_bias"].reshape(-1)), 16),
        "mask8": mask(8, c // 8), "mask4": mask(4, c // 16),
        "wpos": rows128(np.concatenate([a["L0_attn_Wpos"]] * 2, axis=1)), "pe_s": rows128(pe1.T),
        "wq1": block_diagonal(a["L0_attn_Wq"]), "wk1": block_diagonal(a["L0_attn_Wk"]),
        "wv1": value_weights(a["L0_attn_Wv"], 4), "wo1": block_diagonal(a["L0_attn_Wout"]),
        "bout": np.tile(a["L0_attn_bout"], (128, 1)),
    }
    wq, wk, wv = (a[f"L1_ffn_w{n}"].T for n in "qkv")
    rep = (np.arange(4)[:, None] // 2 * 16 + np.arange(16)[None, :]).reshape(-1)
    swap = (np.arange(4)[:, None] * 16 + (np.arange(16)[None, :] + 8) % 16).reshape(-1)
    wk, wv = wk[:, rep], wv[:, rep]
    inv = 1.0 / 10000.0 ** (np.arange(0, 16, 2, dtype=f) / 16)
    fr = np.outer(np.arange(S, dtype=f), inv)
    emb = np.concatenate([fr, fr], axis=-1)
    cos, sin = np.cos(emb).astype(f), np.sin(emb).astype(f)
    sign = np.where(np.arange(16) < 8, -1.0, 1.0).astype(f)
    qk2 = a["L1_attn_w_qkv"].T
    third = {
        "gate": block_diagonal(a["L0_ffn_gate_w"]), "gate_b": np.tile(a["L0_ffn_gate_b"], (128, 1)),
        "iota": np.tile(np.arange(E0, dtype=f), (128, 1)), "b2": rows128(block_diagonal(a["L0_ffn_b2"])),
        "b1": a["L0_ffn_b1"].T, "gamma": np.tile(a["L0_ffn_gamma"], (128, 1)),
        "beta": np.tile(a["L0_ffn_beta"], (128, 1)),
        "wqk2": np.concatenate([block_diagonal(qk2[:, :D]), block_diagonal(qk2[:, D:2 * D])], axis=1),
        "wv2": value_weights(qk2[:, 2 * D:], 32), "wp2": block_diagonal(a["L1_attn_w_proj"].T),
        "maskr": mask(8, c // 2 % 8), "maskg": mask(4, c // 16),
        "cols2": column(qn, kn, a["L1_ffn_ln1_w"], a["L1_ffn_ln2_w"]),
        "wq3": block_diagonal(wq), "wqs3": block_diagonal(wq[:, swap]),
        "wk3": block_diagonal(wk), "wks3": block_diagonal(wk[:, swap]),
        "wv3": value_weights(wv, 4), "wo3": block_diagonal(a["L1_ffn_wo"].T),
        "rope_c": twice(np.tile(cos.T, (4, 1))), "rope_s": twice(np.tile((sin * sign).T, (4, 1))),
        "router": block_diagonal(a["L1_ffn_router_w"].T),
    }
    key = np.arange(512) % S
    query = np.arange(128) % S
    sel1 = np.zeros((128, 2, H1ROWS), f)
    eye3 = np.zeros((128, 2 * E0), f)
    for p in range(3):
        eye3[2 * E0 * p:2 * E0 * (p + 1)] = np.eye(2 * E0, dtype=f)
        for h in range(2):
            for e in range(E1):
                sel1[2 * E1 * p + E1 * h + e, h, F1 * e:F1 * (e + 1)] = 1.0
    half = {"identb": np.eye(128, dtype=f), "causal": np.where(key[None, :] > query[:, None], f(NEG), f(0.0)),
            "eye3": eye3, "sel1": sel1.reshape(128, -1)}

    def packed(name, parts):
        got = [parts[n] for n, _ in PACKS[name]]
        assert [g.shape[1] for g in got] == [n for _, n in PACKS[name]], name
        return np.ascontiguousarray(np.concatenate(got, axis=1))

    def hidden(wt):
        return np.ascontiguousarray(wt.reshape(H1ROWS, D).T)

    w2 = np.zeros((T1 * 128, D), f)
    w2[:H1ROWS] = a["L1_ffn_w2"].transpose(0, 2, 1).reshape(H1ROWS, D)
    return {
        "patches": patches,
        "first": packed("first", first), "second": packed("second", second), "third": packed("third", third),
        "half_consts": np.ascontiguousarray(packed("half", half).view(np.uint16)[:, 1::2]),
        "moe0_w1": np.ascontiguousarray(a["L0_ffn_w1"].transpose(1, 0, 2)).reshape(D, E0 * F0),
        "moe0_w2": np.ascontiguousarray(a["L0_ffn_w2"].transpose(1, 0, 2)).reshape(F0, E0 * D),
        "moe1_w1": hidden(a["L1_ffn_w1"]), "moe1_w3": hidden(a["L1_ffn_w3"]),
        "moe1_w2": np.ascontiguousarray(w2.reshape(T1, 128, D).transpose(1, 0, 2)).reshape(128, T1 * D),
    }


def kernel(**inputs):
    import concourse.bacc as bacc
    from concourse.bass_utils import run_bass_kernel_spmd

    arrays = lay_out(inputs)
    nc = bacc.Bacc("TRN2", target_bir_lowering=False, num_devices=1)
    args = {n: nc.dram_tensor(f"in_{n}", x.shape, mybir.dt.from_np(x.dtype), kind="ExternalInput").ap()
            for n, x in arrays.items()}
    out = nc.dram_tensor("out_tokens", (128, NT), F32, kind="ExternalOutput").ap()
    tower_program(nc, **args, out=out)
    r = run_bass_kernel_spmd(nc, [{f"in_{n}": x for n, x in arrays.items()}], core_ids=[0])
    got = r.results[0]["out_tokens"]
    return np.ascontiguousarray(got.reshape(2, S, NQ, 2, D).transpose(3, 2, 0, 1, 4)).reshape(B, S, D)
```

```python
from contextlib import ExitStack

import numpy as np

import concourse.bass as bass
from concourse import mybir

F32 = mybir.dt.float32
BF16 = mybir.dt.bfloat16
F32R = mybir.dt.float32r
U16 = mybir.dt.uint16
U32 = mybir.dt.uint32
ALU = mybir.AluOpType
ACT = mybir.ActivationFunctionType
AX = mybir.AxisListType

B, C, IMG, PATCH = 16, 3, 128, 16
D = 64
S = (IMG // PATCH) ** 2
NB = B // 2
NT = NB * S
NQ = NT // 128
KC = C * PATCH * PATCH // 128
FF = 256
E0, F0 = 16, 128
E1, F1 = 8, 170
H1ROWS = E1 * F1
T1 = -(-H1ROWS // 128)
NEG = -1e30

PACKS = {
    "first": [("conv_w", KC * D), ("ident", 128), ("cols0", 8), ("pe_t", S)],
    "ffn": [("up_lo", FF), ("up_hi", FF), ("down", 2 * D)],
    "second": [("wq0", 128), ("wk0", 128), ("wv0", 2 * D), ("wp0", 128), ("cols1", 16), ("mask8", 8),
               ("mask4", 4), ("wpos", 128), ("pe_s", S), ("wq1", 128), ("wk1", 128), ("wv1", 2 * D),
               ("wo1", 128), ("bout", D)],
    "third": [("gate", 2 * E0), ("gate_b", E0), ("iota", E0), ("b2", 128), ("b1", E0), ("gamma", D), ("beta", D),
              ("wqk2", 256), ("wv2", 2 * D), ("wp2", 128), ("maskr", 8), ("maskh", 2), ("cols2", 4),
              ("wq3", 128), ("wqs3", 128), ("wk3", 128), ("wks3", 128), ("wv3", 2 * D), ("wo3", 128),
              ("rope_c", S), ("rope_s", S), ("router", 2 * E1)],
    "half": [("identb", 128), ("causal", 512), ("eye3", 2 * E0), ("sel1", 2 * H1ROWS)],
}
COL0 = ["conv_b", "ln_w", "ln_b", "ff_b1a", "ff_b1b", "ff_b2"]
COL1 = ["bq0", "bk0", "bv0", "bp0", "gamma1", "beta1", "bq1", "bk1", "bv1", "u1", "v1"]
COL2 = ["qn", "kn", "ln1", "ln2"]


def width(pack):
    return sum(n for _, n in PACKS[pack])


def tower_program(nc, patches, first, ffn_w, second, third, half_consts, expand, moe0_w1, moe0_w2,
                  moe1_w1, moe1_w3, moe1_w2, out):
    with ExitStack() as ctx:
        def sb(name, shape, dt=F32):
            return ctx.enter_context(nc.sbuf_tensor(name, shape, dt))

        sems = {}

        def sem(name):
            if name not in sems:
                sems[name] = ctx.enter_context(nc.semaphore(name))
            return sems[name]

        P = [ctx.enter_context(nc.psum_tensor(f"bank{i}", [128, 512], F32)) for i in range(8)]
        pos_scratch = nc.dram_tensor("pos_scratch", [NB // 2, 8, 2 * (S + 1) * S], F32, kind="Internal").ap()

        xt = sb("xt", [128, KC, 2 * NT])
        pk = {n: sb(f"pack_{n}", [128, width(n)], U16 if n == "half" else F32) for n in PACKS}
        w = {}
        for n, items in PACKS.items():
            at = 0
            for name, cols in items:
                w[name] = pk[n][:, at:at + cols].bitcast(BF16) if n == "half" else pk[n][:, at:at + cols]
                at += cols
        col = {}
        for base, names in (("cols0", COL0), ("cols1", COL1), ("cols2", COL2)):
            for i, name in enumerate(names):
                col[name] = w[base][:, i:i + 1]
        ident = w["ident"]
        identb = w["identb"]

        w1_both = sb("w1_both", [128, 2 * E0 * F0], F32R)
        w1_split = [w1_both[:, E0 * F0 * i:E0 * F0 * (i + 1)] for i in range(2)]
        raw0 = xt[:, 0:2, :].rearrange("p k n -> p (k n)")
        raw1 = xt[:, 2:5, :].rearrange("p k n -> p (k n)")[:, 0:2 * H1ROWS]
        w2_sb = sb("w2_sb", [128, E0 * D])
        u_split = [sb(f"u_split{i}", [128, 2 * H1ROWS], F32R) for i in range(2)]
        x_split = [sb(f"x_split{h}", [128, NT], F32R) for h in range(2)]
        d1_sb = sb("d1_sb", [128, T1 * D])

        def big(name):
            return sb(name, [128, NT])

        conv_t, xn0, h0_t, a0_t, h1_t, h2_t = (big(n) for n in ("conv_t", "xn0", "h0_t", "a0_t", "h1_t", "h2_t"))
        centred, xn = big("centred"), big("xn")
        hid_all = sb("hid_all", [128, 4, NT])
        hid = [hid_all[:, i] for i in range(4)]
        pe_b = sb("pe_b", [128, S])
        stats = sb("stats", [128, 8, 6])
        mv = sb("mv", [128, 8, 2])
        rin = sb("rin", [128, 16])
        rout = sb("rout", [128, 16])
        msq = sb("msq", [128, 8])
        root_sb = sb("root_sb", [128, 16])
        one = sb("one", [128, 1])
        scrap = sb("scrap", [128, 24])

        q_bd = sb("q_bd", [128, NB, 128])
        qv_bd = sb("qv_bd", [128, NB, 128])
        k_t = big("k_t")
        R = [sb(f"R{i}", [128, 512]) for i in range(2)]
        cen_s = [sb(f"cen_s{i}", [128, 512]) for i in range(2)]
        prob = [sb(f"prob{i}", [128, 512]) for i in range(2)]
        prob_t = [sb(f"prob_t{i}", [128, 512]) for i in range(2)]
        queries32 = w1_both[:].rearrange("p (g b h i) -> p g b h i", g=4, b=NB, h=2)
        keys32 = hid_all
        R32 = x_split
        q_parts = [sb(f"q_part{x}", [128, NT], F32R) for x in range(2)]
        k_parts = [sb(f"k_part{x}", [128, NT], F32R) for x in range(2)]
        expand_raw = xt[:, 4:6, :].rearrange("p k n -> p (k n)")
        expander = sb("expander", [128, 4 * 4 * 128], F32R)
        kq_w = sb("kq_w", [128, 1])
        rowmax = [sb(f"rowmax{i}", [128, 8]) for i in range(2)]
        rowsum = [sb(f"rowsum{i}", [128, 32]) for i in range(2)]
        ctx_n = [sb(f"ctx_n{i}", [128, 128]) for i in range(2)]
        ctx_t = big("ctx_t")
        V0 = sb("V0", [128, 2 * NB * 4, 2 * 9])
        V4 = sb("V4", [128, 2 * NB * 2, 2 * 17])
        V32 = xt[:, 0:4, :].rearrange("p k n -> p (k n)").rearrange("p (g c) -> p g c", c=32)
        out_ts = [sb(f"out_ts{i}", [128, 512]) for i in range(2)]
        bqu = sb("bqu", [128, 1])
        bqv = sb("bqv", [128, 1])
        p_pos = sb("p_pos", [128, 4, S])
        pos_all = sb("pos_all", [128, 4, 8, S + 1])
        shifted_all = sb("shifted_all", [128, 4, 8, S])
        pos_sb = [pos_all[:, i] for i in range(4)]
        shifted = [shifted_all[:, i] for i in range(4)]
        h2_n, h2_nb, h4_n = (big(n) for n in ("h2_n", "h2_nb", "h4_n"))
        xa_t, xb_t, y_n, y_t, z_t, h3_n, h3_nb = a0_t, a0_t, conv_t, xn0, a0_t, h0_t, h2_n
        xc_t, x_n, x2_n, fin_n, f_t, o_t, out_n, h5_n = conv_t, xn0, h0_t, a0_t, h1_t, h2_t, h2_n, h2_nb
        logit = sb("logit", [128, 8, E0])
        top8 = sb("top8", [128, 8, 8])
        top8i = sb("top8i", [128, 8, 8], U32)
        topf = sb("topf", [128, 8, 8])
        gap = sb("gap", [128, 8])
        egap = sb("egap", [128, 8])
        wsum = sb("wsum", [128, 8])
        w12 = sb("w12", [128, 8, 2])
        hot = [sb(f"hot{i}", [128, 8, E0]) for i in range(2)]
        gates = sb("gates", [128, 8, E0])
        resid = sb("resid", [128, 8, E0])
        gates3 = sb("gates3", [128, NQ, 128], BF16)
        gates_t3 = sb("gates_t3", [128, NT], BF16)
        gates_t = ctx_t[0:2 * E0, :]
        relu_h = out_ts
        sq = shifted_all[:, 0:2].rearrange("p i g t -> p (i g t)")
        qk_ms, qk_r = (shifted[i].rearrange("p g t -> p (g t)") for i in (2, 3))
        qk_n = pos_all[:].rearrange("p i g t -> p (i g t)")[:, 0:1024].rearrange("p (q o c) -> p q o c", q=NQ, o=2)
        rope = [xt[:, 4 + i // 2, NT * (i % 2):NT * (i % 2) + NT] for i in range(4)]
        gated = hid

        def heads(t, n):
            return t.rearrange("p (a b) -> p a b", a=n)

        def over(t, n):
            return t.unsqueeze(2).to_broadcast([t.shape[0], t.shape[1], n])

        def each(t, n):
            return t.unsqueeze(1).to_broadcast([t.shape[0], n, t.shape[1]])

        class Attn:

            def __init__(self, H, scale, V, mask, signals, units=None, causal=False, shift=False):
                self.H, self.hd, self.scale = H, D // H, scale
                self.per = 8 // H
                self.units = units or NB // self.per
                self.V, self.mask, self.causal, self.shift = V, mask, causal, shift
                self.base = dict(counted)
                for what in ("scores", "centred", "probs", "turned", "probs_t", "mixed"):
                    counted[what] += self.units
                for what, n in signals.items():
                    counted[what] += n

            def s(self, what):
                return sems[f"attn_{what}"]

            def wait(self, engine, what, n):
                engine.wait_ge(sems[f"attn_{what}"], self.base[what] + n)

        counted = dict.fromkeys(("q", "k_psum", "k", "v_psum", "v", "keys", "scores", "centred", "probs", "turned",
                                 "probs_t", "mixed", "context", "context_t", "context_sb"), 0)
        for what in counted:
            sem(f"attn_{what}")
        attn0 = Attn(8, 1.0 / np.sqrt(8.0), V0, w["mask8"],
                     dict(q=2, k_psum=2, k=1, v_psum=1, v=2, keys=8, context=8, context_t=8, context_sb=2))
        attn1 = Attn(4, 1.0 / 8.0, V4, w["mask4"],
                     dict(q=4, k_psum=2, k=1, v_psum=1, v=2, keys=4, context=4, context_t=4, context_sb=1), shift=True)
        attn2 = Attn(8, 1.0 / np.sqrt(2.0), V32, w["maskr"],
                     dict(v_psum=1, v=4, context=NB, context_t=NB, context_sb=1), units=4 * NB)
        attn3 = Attn(4, 1.0 / 4.0, V4, w["mask4"],
                     dict(q=2, k=1, v_psum=1, v=2, keys=4, context=4, context_t=4, context_sb=1), causal=True)
        N32 = 4 * NB

        for name in ("conv", "conv_t", "conv_n", "n0", "xn0_turned", "h0", "pe_b", "setup_pos", "p_pos", "bias1",
                     "zeros", "ones", "moe_zeros", "w1_split", "u_split", "moe0_down", "moe1_down", "x0_split",
                     "x1_split", "half_m", "dve_step", "rin", "rout", "one", "first", "ffn_w", "second", "third",
                     "halfw", "moe0", "moe1", "out", "h1_psum", "h1", "h2", "h2_turned", "h2_n", "h2_nb", "xa_n",
                     "xa_turned", "xa", "pos_psum", "pos_sb", "pos_sb_odd", "h3_psum", "h3", "h3_nb", "y_n", "y_turned", "y",
                     "gate_psum", "gap", "egap", "gates", "gates3", "gates_turned", "gates3_turned", "gates_sb",
                     "up0", "gate_b0", "relu0", "hid0", "moe0_out", "z", "z_turned", "h4", "xb_n", "xb_turned",
                     "xb", "qk_psum", "sq", "ms", "root", "qk_n", "qk_turned", "kq_w", "expander", "q_high",
                     "q_low", "k32", "k_high", "k_low", "q_rows", "k_rows", "queries32", "keys32", "ops2", "ots",
                     "on", "h5_psum", "h5", "xc_n", "xc_turned", "xc", "x_n", "rope_psum", "x2_psum", "x2", "fin",
                     "f_n", "f_turned", "f", "gate1_psum", "shift1", "exp1", "gates1", "gates31", "gates1_turned",
                     "gates1_sb", "a1", "b1", "g1", "silu1", "hid1", "moe1_out", "o_sb", "o_turned", "out_ready"):
            sem(name)
        for n in range(2):
            for what in ("up", "gelu", "down"):
                sem(f"ffn{n}_{what}")
        s_x = [sem(f"patches{k}") for k in range(KC)]
        s_pos_out = [sem(f"pos_out{i}") for i in range(4)]
        s_pos_in = [sem(f"pos_in{i}") for i in range(4)]
        block = ctx.enter_context(nc.Block())

        @block.sync
        def _(sp):
            sp.dma_start(pk["first"][:], first).then_inc(sems["first"], 16)
            for k in range(KC):
                sp.dma_start(xt[:, k, :], patches[k]).then_inc(s_x[k], 16)
            sp.dma_start(pk["ffn"][:], ffn_w).then_inc(sems["ffn_w"], 16)
            sp.dma_start(pk["second"][:], second).then_inc(sems["second"], 16)
            sp.dma_start(pk["third"][:], third).then_inc(sems["third"], 16)
            sp.dma_start(pk["half"][:], half_consts).then_inc(sems["halfw"], 16)
            sp.dma_start(w2_sb[:], moe0_w2).then_inc(sems["moe0_down"], 16)
            sp.dma_start(d1_sb[:], moe1_w2).then_inc(sems["moe1_down"], 16)
            sp.wait_ge(sems["conv"], 1)
            for h in range(2):
                sp.dma_start(raw0[64 * h:64 * h + 64, :], moe0_w1).then_inc(sems["moe0"], 16)
            for h in range(2):
                sp.dma_start(raw1[64 * h:64 * h + 64, 0:H1ROWS], moe1_w1).then_inc(sems["moe1"], 16)
                sp.dma_start(raw1[64 * h:64 * h + 64, H1ROWS:2 * H1ROWS], moe1_w3).then_inc(sems["moe1"], 16)
            half = (S + 1) * S
            for step in range(6):
                u = step
                if u < 4:
                    sp.wait_ge(sems["pos_sb_odd" if u % 2 else "pos_sb"], u // 2 + 1)
                    sp.dma_start(pos_scratch[u].rearrange("g (p t) -> p g t", t=S + 1),
                                 pos_sb[u]).then_inc(s_pos_out[u], 16)
                u = step - 2
                if 0 <= u < 4:
                    sp.wait_ge(s_pos_out[u], 16)
                    for h in range(2):
                        sp.dma_start(shifted[u][64 * h:64 * h + 64],
                                     pos_scratch[u, :, half * h + S:half * (h + 1)].rearrange("g (i t) -> i g t", t=S)
                                     ).then_inc(s_pos_in[u], 16)
            sp.wait_ge(sems["u_split"], 4)
            sp.dma_start(expand_raw, expand).then_inc(sems["expander"], 16)
            sp.wait_ge(sems["out_ready"], 1)
            sp.dma_start(out, out_n[:]).then_inc(sems["out"], 16)
            sp.wait_ge(sems["out"], 16)

        @block.tensor
        def _(pe):
            mm = nc.tensor.matmul

            def keep_warm(n, bank, early=False):
                for _ in range(n):
                    if early:
                        mm(P[bank][:, 0:128], ident, ident, start=True, stop=True)
                    else:
                        mm(P[bank][:], identb, w["causal"], start=True, stop=True)

            def turn(dst, src):
                for q in range(NQ):
                    last = nc.tensor.transpose(dst[:, 128 * q:128 * q + 128], src[:, 128 * q:128 * q + 128], ident)
                return last

            def ffn(n, src):
                banks = [P[i] for i in (2, 3, 4, 5)]
                for f in range(2):
                    for h in range(2):
                        lhs = w["up_lo" if h == 0 else "up_hi"][:, 128 * f:128 * f + 128]
                        mm(banks[2 * f + h][:], lhs, src[:], start=True, stop=True).then_inc(sems[f"ffn{n}_up"], 1)
                for f in range(2):
                    for h in range(2):
                        pe.wait_ge(sems[f"ffn{n}_gelu"], 2 * f + h + 1)
                        last = mm(P[7][64 * h:64 * h + 64, :], w["down"][:, D * f:D * f + D], hid[2 * f + h][:],
                                  start=(f == 0), stop=(f == 1))
                last.then_inc(sems[f"ffn{n}_down"], 1)

            def values(a, src, wv):
                for b in range(NB):
                    for o in range(2):
                        last = mm(P[7][64 * o:64 * o + 64, D * b:D * b + D], src[:, S * b:S * b + S],
                                  wv[:, D * o:D * o + D], start=True, stop=True)
                last.then_inc(a.s("v_psum"), 1)

            def context_t(a, u, images):
                a.wait(pe, "context", u + 1)
                for n, b in enumerate(images):
                    for h in range(2):
                        last = mm(P[6][64 * h:64 * h + 64, S * b:S * b + S], ctx_n[u % 2][:, D * n:D * n + D],
                                  ident[:, 64 * h:64 * h + 64], start=True, stop=True)
                last.then_inc(a.s("context_t"), 1)

            def turn_probs(a, u):
                a.wait(pe, "probs", u + 1)
                if u >= 2:
                    a.wait(pe, "probs_t", u - 1)
                for x in range(4):
                    last = nc.tensor.transpose(P[2 + u % 2][:, 128 * x:128 * x + 128],
                                               prob[u % 2][:, 128 * x:128 * x + 128], ident)
                last.then_inc(a.s("turned"), 1)

            def attention(a):
                wide = 2 * (a.hd + 1)
                for step in range(a.units + 4):
                    u = step
                    if u < a.units:
                        a.wait(pe, "keys", u + 1)
                        if u == 0:
                            a.wait(pe, "q", 2)
                        if u >= 2:
                            a.wait(pe, "centred", u - 1)
                        cols = 512 // a.per
                        for n in range(a.per):
                            if a.causal:
                                mm(P[u % 2][:, cols * n:cols * n + cols], identb, w["causal"][:, 0:cols],
                                   start=True, stop=False)
                            last = mm(P[u % 2][:, cols * n:cols * n + cols], q_bd[:, a.per * u + n, :],
                                      R[u % 2][:, cols * n:cols * n + cols], start=not a.causal, stop=True)
                        last.then_inc(a.s("scores"), 1)
                    u = step - 2
                    if 0 <= u < a.units:
                        turn_probs(a, u)
                    u = step - 3
                    if 0 <= u < a.units:
                        a.wait(pe, "probs_t", u + 1)
                        if u == 0:
                            a.wait(pe, "v", 2)
                        if u >= 2:
                            a.wait(pe, "context", u - 1)
                        for x in range(4):
                            b, hp = a.per * u + x // (4 // a.per), x % (4 // a.per)
                            for h in range(2):
                                last = mm(P[4 + u % 2][64 * h:64 * h + 64, wide * x:wide * x + wide],
                                          prob_t[u % 2][:, 128 * x + 64 * h:128 * x + 64 * h + 64],
                                          a.V[:, (2 * b + h) * (a.H // 2) + hp, :], start=True, stop=True)
                        last.then_inc(a.s("mixed"), 1)
                    u = step - 4
                    if 0 <= u < a.units:
                        context_t(a, u, range(a.per * u, a.per * u + a.per))

            def project_n(src, weight, dst, done):
                for q in range(NQ):
                    last = mm(dst[:, 128 * q:128 * q + 128], src[:, 128 * q:128 * q + 128], weight,
                              start=True, stop=True)
                last.then_inc(done, 1)

            pe.wait_ge(sems["first"], 16)
            for k in range(KC):
                pe.wait_ge(s_x[k], 16)
                for h in range(2):
                    last = mm(P[0][64 * h:64 * h + 64, :], w["conv_w"][:, D * k:D * k + D],
                              xt[:, k, NT * h:NT * h + NT], start=(k == 0), stop=(k == KC - 1))
            last.then_inc(sems["conv"], 1)
            keep_warm(3, 7, early=True)
            pe.wait_ge(sems["conv_t"], 1)
            turn(P[1], conv_t).then_inc(sems["conv_n"], 1)
            keep_warm(15, 7, early=True)
            pe.wait_ge(sems["n0"], 1)
            turn(P[2], xn0).then_inc(sems["xn0_turned"], 1)
            keep_warm(4, 7, early=True)
            pe.wait_ge(sems["h0"], 1)
            pe.wait_ge(sems["ffn_w"], 16)
            ffn(0, h0_t)
            pe.wait_ge(sems["second"], 16)
            mm(P[6][:, 0:S], w["wpos"][0:64, :], w["pe_s"][0:64, :], start=True, stop=True).then_inc(sems["setup_pos"], 1)
            pe.wait_ge(sems["ffn0_down"], 1)
            pe.wait_ge(sems["halfw"], 16)
            keep_warm(3, 1, early=True)
            attn0.wait(pe, "context_sb", 1)
            mm(P[4][:], w["wq0"], a0_t[:], start=True, stop=True).then_inc(attn0.s("k_psum"), 1)
            mm(P[5][:], w["wk0"], a0_t[:], start=True, stop=True).then_inc(attn0.s("k_psum"), 1)
            values(attn0, a0_t, w["wv0"])
            keep_warm(3, 3)
            attention(attn0)
            keep_warm(4, 1)
            attn0.wait(pe, "context_sb", 2)
            mm(P[0][:], w["wp0"], ctx_t[:], start=True, stop=True).then_inc(sems["h1_psum"], 1)
            keep_warm(4, 1)
            pe.wait_ge(sems["h1"], 1)
            ffn(1, h1_t)
            keep_warm(4, 1)
            pe.wait_ge(sems["h2"], 1)
            turn(P[0], h2_t).then_inc(sems["h2_turned"], 1)
            keep_warm(18, 3)
            pe.wait_ge(sems["xa_n"], 1)
            turn(P[1], xn).then_inc(sems["xa_turned"], 1)
            keep_warm(4, 3)
            pe.wait_ge(sems["xa"], 1)
            mm(P[4][:], w["wq1"], xa_t[:], start=True, stop=True).then_inc(attn1.s("k_psum"), 1)
            keep_warm(4, 0)
            pe.wait_ge(sems["p_pos"], 1)
            attn1.wait(pe, "q", 2)
            for u in range(4):
                if u >= 2:
                    pe.wait_ge(sems["pos_sb_odd" if u % 2 else "pos_sb"], u // 2)
                for n in range(2):
                    last = mm(P[2 + u % 2][:, 256 * n:256 * n + 256], qv_bd[:, 2 * u + n, :],
                              p_pos[:].rearrange("p h t -> p (h t)"), start=True, stop=True)
                last.then_inc(sems["pos_psum"], 1)
                if u == 1:
                    mm(P[5][:], w["wk1"], xa_t[:], start=True, stop=True).then_inc(attn1.s("k_psum"), 1)
            values(attn1, xa_t, w["wv1"])
            attn1.wait(pe, "q", 4)
            keep_warm(2, 0)
            attention(attn1)
            keep_warm(4, 1)
            attn1.wait(pe, "context_sb", 1)
            project_n(ctx_t, w["wo1"], P[0], sems["h3_psum"])
            keep_warm(18, 3)
            pe.wait_ge(sems["y_n"], 1)
            turn(P[1], y_n).then_inc(sems["y_turned"], 1)
            keep_warm(3, 3)
            pe.wait_ge(sems["y"], 1)
            for q in range(NQ):
                last = mm(P[7][:, 32 * q:32 * q + 32], y_t[:, 128 * q:128 * q + 128], w["gate"], start=True, stop=True)
            last.then_inc(sems["gate_psum"], 1)

            def gates_turn3(dst, wait, done):
                pe.wait_ge(sems[wait], 1)
                t = dst[:].bitcast(BF16)
                for q in range(NQ):
                    last = nc.tensor.transpose(t[:, 128 * q:128 * q + 128], gates3[:, q, :], identb)
                last.then_inc(sems[done], 1)

            UB = [P[0], P[1], P[5], P[6]]

            def up0(i):
                e, h = i // 2, i % 2
                if i >= 4:
                    pe.wait_ge(sems["relu0"], i - 3)
                for k in range(2):
                    last = mm(UB[i % 4][:], w1_split[k][:, F0 * e:F0 * e + F0], x_split[h][:], start=(k == 0),
                              stop=(k == 1))
                last.then_inc(sems["up0"], 1)

            pe.wait_ge(sems["w1_split"], 4)
            keep_warm(5, 3)
            pe.wait_ge(sems["x0_split"], 2)
            for i in range(4):
                up0(i)
            keep_warm(8, 3)
            pe.wait_ge(sems["gates"], 1)
            for q in range(NQ):
                last = nc.tensor.transpose(P[2][0:32, 128 * q:128 * q + 128],
                                           gates[:, 2 * q:2 * q + 2, :].rearrange("p a b -> p (a b)"), ident)
            last.then_inc(sems["gates_turned"], 1)
            gates_turn3(P[3], "gates3", "gates3_turned")
            pe.wait_ge(sems["gates_sb"], 2)
            pe.wait_ge(sems["moe0_down"], 16)

            def down0(e):
                for h in range(2):
                    pe.wait_ge(sems["hid0"], 2 * e + h + 1)
                    last = mm(P[4][64 * h:64 * h + 64, :], w2_sb[:, D * e:D * e + D], gated[(2 * e + h) % 4][:],
                              start=(e == 0), stop=False, skip_group_check=True)
                return last

            for e in range(E0):
                for h in range(2):
                    i = 2 * e + h
                    if i >= 4:
                        up0(i)
                    if i >= 2:
                        pe.wait_ge(sems["hid0"], i - 1)
                    mm(P[2 + i % 2][:], w["eye3"][:, E0 * h + e:E0 * h + e + 1].to_broadcast([128, 128]),
                       gates_t3[:], start=True, stop=True).then_inc(sems["gate_b0"], 1)
                if e >= 1:
                    down0(e - 1)
            down0(E0 - 1)
            mm(P[4][:], w["b2"][0:2 * E0, :], gates_t, start=False, stop=True,
               skip_group_check=True).then_inc(sems["moe0_out"], 1)
            keep_warm(3, 3)
            pe.wait_ge(sems["z"], 1)
            turn(P[0], z_t).then_inc(sems["z_turned"], 1)
            keep_warm(36, 3)
            pe.wait_ge(sems["xb_n"], 1)
            turn(P[1], xn).then_inc(sems["xb_turned"], 1)
            keep_warm(4, 6)
            pe.wait_ge(sems["xb"], 1)
            for q in range(NQ):
                last = mm(P[2 + q // 2][:, 256 * (q % 2):256 * (q % 2) + 256], xb_t[:, 128 * q:128 * q + 128],
                          w["wqk2"], start=True, stop=True)
                if q % 2:
                    last.then_inc(sems["qk_psum"], 1)
            values(attn2, xb_t, w["wv2"])
            keep_warm(11, 6)
            for n in range(2):
                pe.wait_ge(sems["qk_n"], n + 1)
                for o in range(2):
                    for q in (2 * n, 2 * n + 1):
                        last = nc.tensor.transpose(P[4 + o][:, 128 * q:128 * q + 128], qk_n[:, q, o, :], ident)
                    if n == 1:
                        last.then_inc(sems["qk_turned"], 1)
            keep_warm(5, 6)
            pe.wait_ge(sems["expander"], 17)
            attn2.wait(pe, "v", 4)
            sides = ((0, (6, 7, 2, 3), q_parts, "q_high", "q_low", "q_rows"),
                     (1, (0, 1, 4, 5), k_parts, "k_high", "k_low", "k_rows"))
            for side, g in ((0, 0), (0, 1), (1, 0), (1, 1), (0, 2), (1, 2), (0, 3), (1, 3)):
                o, banks, parts, high, low, done = sides[side]
                pe.wait_ge(sems[high], 1)
                pe.wait_ge(sems[low], 1)
                for x in range(2):
                    at = 128 * (4 * (2 * o + x) + g)
                    last = mm(P[banks[g]][:], expander[:, at:at + 128], parts[x][:], start=(x == 0), stop=(x == 1))
                last.then_inc(sems[done], 1)
            a = attn2
            for step in range(N32 + 7):
                u = step
                if u < N32:
                    b, g = u // 4, u % 4
                    pe.wait_ge(sems["ops2"], u + 1)
                    if u < 4:
                        pe.wait_ge(sems["queries32"], g + 1)
                    if u < 2:
                        pe.wait_ge(sems["keys32"], u + 1)
                    if u >= 2:
                        a.wait(pe, "centred", u - 1)
                    mm(P[u % 2][:], identb, w["causal"], start=True, stop=False)
                    mm(P[u % 2][:], queries32[:, g, b].rearrange("p h i -> p (h i)"), R32[u % 2][:],
                       start=False, stop=True).then_inc(a.s("scores"), 1)
                u = step - 2
                if 0 <= u < N32:
                    if u == 0:
                        pe.wait_ge(sems["queries32"], 4)
                    turn_probs(a, u)
                u = step - 3
                if 0 <= u < N32:
                    b, g = u // 4, u % 4
                    a.wait(pe, "probs_t", u + 1)
                    if u == 0:
                        pe.wait_ge(sems["keys32"], 4)
                    if g == 0 and b >= 2:
                        pe.wait_ge(sems["ots"], b - 1)
                    for x in range(4):
                        last = mm(P[4 + b % 2][32 * x:32 * x + 32, 128 * g:128 * g + 128],
                                  V32[:, 16 * b + 4 * g + x, :], prob_t[u % 2][:, 128 * x:128 * x + 128],
                                  start=True, stop=True)
                    last.then_inc(a.s("mixed"), 1)
                u = step - 5
                if 0 <= u < N32 and u % 4 == 3:
                    b = u // 4
                    pe.wait_ge(sems["ots"], b + 1)
                    if b >= 1:
                        a.wait(pe, "context", b)
                    for g in range(4):
                        last = nc.tensor.transpose(P[7][:, 128 * g:128 * g + 128],
                                                   out_ts[b % 2][:, 128 * g:128 * g + 128], ident)
                    last.then_inc(sems["on"], 1)
                u = step - 6
                if 0 <= u < N32 and u % 4 == 3:
                    context_t(a, u // 4, [u // 4])
            keep_warm(4, 1)
            a.wait(pe, "context_sb", 1)
            project_n(ctx_t, w["wp2"], P[0], sems["h5_psum"])
            keep_warm(19, 3)
            pe.wait_ge(sems["xc_n"], 1)
            turn(P[1], xn).then_inc(sems["xc_turned"], 1)
            keep_warm(4, 6)
            pe.wait_ge(sems["xc"], 1)
            for bank, name in ((4, "wq3"), (5, "wqs3"), (2, "wk3"), (3, "wks3")):
                mm(P[bank][:], w[name], xc_t[:], start=True, stop=True).then_inc(sems["rope_psum"], 1)
            values(attn3, xc_t, w["wv3"])
            keep_warm(9, 6)
            attention(attn3)
            keep_warm(3, 1)
            attn3.wait(pe, "context_sb", 1)
            project_n(ctx_t, w["wo3"], P[0], sems["x2_psum"])
            keep_warm(17, 3)
            pe.wait_ge(sems["f_n"], 1)
            turn(P[1], xn).then_inc(sems["f_turned"], 1)
            keep_warm(4, 3)
            pe.wait_ge(sems["f"], 1)
            for q in range(NQ):
                last = mm(P[7][:, 16 * q:16 * q + 16], f_t[:, 128 * q:128 * q + 128], w["router"], start=True, stop=True)
            last.then_inc(sems["gate1_psum"], 1)
            pe.wait_ge(sems["u_split"], 4)
            keep_warm(5, 3)
            pe.wait_ge(sems["x1_split"], 2)

            def ups1(i):
                t, h = i // 2, i % 2
                rows = min(128, H1ROWS - 128 * t)
                if i >= 2:
                    pe.wait_ge(sems["silu1"], i - 1)
                for k in range(2):
                    last = mm(P[h][0:rows, :], u_split[k][:, 128 * t:128 * t + rows], x_split[h][:],
                              start=(k == 0), stop=(k == 1))
                last.then_inc(sems["a1"], 1)
                if i >= 2:
                    pe.wait_ge(sems["hid1"], i - 1)
                for k in range(2):
                    last = mm(P[2 + h][0:rows, :], u_split[k][:, H1ROWS + 128 * t:H1ROWS + 128 * t + rows],
                              x_split[h][:], start=(k == 0), stop=(k == 1))
                last.then_inc(sems["b1"], 1)

            def down1(t):
                rows = min(128, H1ROWS - 128 * t)
                for h in range(2):
                    pe.wait_ge(sems["hid1"], 2 * t + h + 1)
                    last = mm(P[4][64 * h:64 * h + 64, :], d1_sb[0:rows, D * t:D * t + D],
                              gated[(2 * t + h) % 4][0:rows, :], start=(t == 0), stop=(t == T1 - 1))
                return last

            for i in range(2):
                ups1(i)
            keep_warm(15, 5)
            gates_turn3(P[7], "gates31", "gates1_turned")
            pe.wait_ge(sems["gates1_sb"], 1)
            pe.wait_ge(sems["moe1_down"], 16)
            for t in range(T1):
                rows = min(128, H1ROWS - 128 * t)
                for h in range(2):
                    if t >= 1:
                        ups1(2 * t + h)
                    mm(P[5 + h][0:rows, :], w["sel1"][:, H1ROWS * h + 128 * t:H1ROWS * h + 128 * t + rows],
                       gates_t3[:], start=True, stop=True).then_inc(sems["g1"], 1)
                if t >= 1:
                    down1(t - 1)
            down1(T1 - 1).then_inc(sems["moe1_out"], 1)
            keep_warm(3, 1)
            pe.wait_ge(sems["o_sb"], 1)
            turn(P[0], o_t).then_inc(sems["o_turned"], 1)

        @block.scalar
        def _(act):
            ac = nc.scalar.activation

            def gelu(n):
                for i in range(4):
                    act.wait_ge(sems[f"ffn{n}_up"], i + 1)
                    ac(hid[i][:], P[2 + i][:], ACT.Gelu_apprx_tanh,
                       bias=col["ff_b1a" if i < 2 else "ff_b1b"]).then_inc(sems[f"ffn{n}_gelu"], 1)

            roots, loads = [0], [0]

            def load_table(function):
                loads[0] += 1
                ac(scrap[:, loads[0]:loads[0] + 1], one[:], function)

            def root(cols=8, then=None):
                roots[0] += 1
                act.wait_ge(sems["rin"], roots[0])
                ac(root_sb[:, 0:cols], rin[:, 0:cols], ACT.Sqrt).then_inc(sems["rout"], 1)
                if then is not None:
                    load_table(then)

            def even_values(a):
                a.wait(act, "v_psum", 1)
                ac(a.V[0:64, :, 0:a.hd], P[7][0:64, :].rearrange("p (a b) -> p a b", b=a.hd),
                   ACT.Copy).then_inc(a.s("v"), 1)

            def attention(a, units):
                for step in range(units + 1):
                    u = step
                    if u < units:
                        a.wait(act, "centred", u + 1)
                        if u >= 2:
                            a.wait(act, "turned", u - 1)
                        ac(prob[u % 2][:], cen_s[u % 2][:], ACT.Exp, scale=a.scale).then_inc(a.s("probs"), 1)
                    u = step - 1
                    if 0 <= u < units:
                        a.wait(act, "turned", u + 1)
                        if u >= 2:
                            a.wait(act, "mixed", u - 1)
                        ac(prob_t[u % 2][:], P[2 + u % 2][:], ACT.Copy).then_inc(a.s("probs_t"), 1)
                        if units == N32 and u % 4 == 1 and u > 4:
                            gather(u // 4 - 1)
                if units == N32:
                    gather(NB - 1)

            def gather(b):
                attn2.wait(act, "mixed", 4 * b + 4)
                if b >= 2:
                    act.wait_ge(sems["on"], b - 1)
                ac(out_ts[b % 2][:], P[4 + b % 2][:], ACT.Copy).then_inc(sems["ots"], 1)

            act.wait_ge(sems["one"], 1)
            load_table(ACT.Sqrt)
            act.wait_ge(sems["first"], 16)
            act.wait_ge(sems["conv"], 1)
            ac(conv_t[:], P[0][:], ACT.Identity, bias=col["conv_b"]).then_inc(sems["conv_t"], 1)
            root(then=ACT.Gelu_apprx_tanh)
            gelu(0)
            load_table(ACT.Exp)
            act.wait_ge(sems["second"], 16)
            act.wait_ge(sems["zeros"], 5)
            attn0.wait(act, "k_psum", 2)
            ac(k_t[:], P[5][:], ACT.Identity, bias=col["bk0"]).then_inc(attn0.s("k"), 1)
            ac(q_bd[0:64, :, 0:64], heads(P[4][0:64, :], NB), ACT.Identity,
               bias=col["bq0"][0:64]).then_inc(attn0.s("q"), 1)
            even_values(attn0)
            attention(attn0, attn0.units)
            load_table(ACT.Gelu_apprx_tanh)
            attn0.wait(act, "context_t", attn0.units)
            ac(ctx_t[:], P[6][:], ACT.Identity, bias=col["bv0"]).then_inc(attn0.s("context_sb"), 1)
            gelu(1)
            load_table(ACT.Sqrt)
            act.wait_ge(sems["h2_turned"], 1)
            ac(h2_n[:], P[0][:], ACT.Copy).then_inc(sems["h2_n"], 1)
            root(then=ACT.Exp)
            act.wait_ge(sems["xa_turned"], 1)
            ac(xa_t[:], P[1][:], ACT.Identity, bias=col["beta1"], scale=col["gamma1"]).then_inc(sems["xa"], 1)
            act.wait_ge(sems["bias1"], 2)
            attn1.wait(act, "k_psum", 1)
            ac(qv_bd[0:64, :, 0:64], heads(P[4][0:64, :], NB), ACT.Identity,
               bias=bqv[0:64]).then_inc(attn1.s("q"), 1)
            for u in range(0, 4, 2):
                act.wait_ge(sems["pos_psum"], u + 1)
                ac(pos_sb[u][:, :, 1:S + 1], heads(P[2 + u % 2][:], 8), ACT.Copy).then_inc(sems["pos_sb"], 1)
                if u == 0:
                    ac(q_bd[0:64, :, 0:64], heads(P[4][0:64, :], NB), ACT.Identity,
                       bias=bqu[0:64]).then_inc(attn1.s("q"), 1)
            attn1.wait(act, "k_psum", 2)
            ac(k_t[:], P[5][:], ACT.Identity, bias=col["bk1"]).then_inc(attn1.s("k"), 1)
            even_values(attn1)
            attention(attn1, attn1.units)
            load_table(ACT.Sqrt)
            attn1.wait(act, "context_t", attn1.units)
            ac(ctx_t[:], P[6][:], ACT.Identity, bias=col["bv1"]).then_inc(attn1.s("context_sb"), 1)
            act.wait_ge(sems["third"], 16)
            root(then=ACT.Exp)
            act.wait_ge(sems["y_turned"], 1)
            ac(y_t[:], P[1][:], ACT.Copy).then_inc(sems["y"], 1)
            act.wait_ge(sems["gap"], 1)
            ac(egap[:], gap[:], ACT.Exp).then_inc(sems["egap"], 1)
            UB = [P[0], P[1], P[5], P[6]]
            for i in range(2 * E0):
                if i == 2:
                    act.wait_ge(sems["gates_turned"], 1)
                    ac(gates_t, P[2][0:32, :], ACT.Copy).then_inc(sems["gates_sb"], 1)
                act.wait_ge(sems["up0"], i + 1)
                if i >= 2:
                    act.wait_ge(sems["hid0"], i - 1)
                ac(relu_h[i % 2][:], UB[i % 4][:], ACT.Relu,
                   bias=w["b1"][:, i // 2:i // 2 + 1]).then_inc(sems["relu0"], 1)
            load_table(ACT.Sqrt)
            root()
            root()
            act.wait_ge(sems["moe_zeros"], 6)
            act.wait_ge(sems["xb_turned"], 1)
            ac(xb_t[:], P[1][:], ACT.Copy).then_inc(sems["xb"], 1)
            for n in range(2):
                act.wait_ge(sems["qk_psum"], n + 1)
                ac(sq[:, 512 * n:512 * n + 512], P[2 + n][:], ACT.Square).then_inc(sems["sq"], 1)
            for n in range(2):
                act.wait_ge(sems["ms"], n + 1)
                ac(qk_r[:, 256 * n:256 * n + 256], qk_ms[:, 256 * n:256 * n + 256],
                   ACT.Sqrt).then_inc(sems["root"], 1)
            attn2.wait(act, "v_psum", 1)
            v_in = P[7][:].rearrange("p (b h g d) -> p b h g d", b=NB, h=2, d=2)
            v_out = V32.rearrange("p (b g) c -> p b g c", b=NB)
            for h in range(2):
                ac(v_out[0:64, :, :, 6 * h:6 * h + 2], v_in[0:64, :, h], ACT.Copy).then_inc(attn2.s("v"), 1)
            load_table(ACT.Exp)
            act.wait_ge(sems["qk_turned"], 1)
            ac(q_parts[0][:], P[4][:], ACT.Copy).then_inc(sems["q_high"], 1)
            act.wait_ge(sems["qk_turned"], 2)
            act.wait_ge(sems["kq_w"], 1)
            ac(k_t[:], P[5][:], ACT.Copy, scale=kq_w[:]).then_inc(sems["k32"], 1)
            for g in range(4):
                act.wait_ge(sems["q_rows"], g + 1)
                for h in range(2):
                    last = ac(queries32[:, g, :, h], heads(P[(6, 7, 2, 3)[g]][:], NB), ACT.Copy,
                              scale=w["maskh"][:, h:h + 1])
                last.then_inc(sems["queries32"], 1)
            attention(attn2, N32)
            load_table(ACT.Sqrt)
            attn2.wait(act, "context_t", NB)
            ac(ctx_t[:], P[6][:], ACT.Copy).then_inc(attn2.s("context_sb"), 1)
            root(16, then=ACT.Exp)
            act.wait_ge(sems["xc_turned"], 1)
            ac(xc_t[:], P[1][:], ACT.Copy, scale=col["ln1"]).then_inc(sems["xc"], 1)
            even_values(attn3)
            attention(attn3, attn3.units)
            load_table(ACT.Sqrt)
            attn3.wait(act, "context_t", attn3.units)
            ac(ctx_t[:], P[6][:], ACT.Copy).then_inc(attn3.s("context_sb"), 1)
            root(then=ACT.Exp)
            act.wait_ge(sems["f_turned"], 1)
            ac(f_t[:], P[1][:], ACT.Copy, scale=col["ln2"]).then_inc(sems["f"], 1)
            act.wait_ge(sems["shift1"], 1)
            ac(resid[:, :, 0:E1], logit[:, :, 0:E1], ACT.Exp).then_inc(sems["exp1"], 1)
            load_table(ACT.Silu)
            for i in range(2 * T1):
                rows = min(128, H1ROWS - 128 * (i // 2))
                act.wait_ge(sems["a1"], i + 1)
                if i >= 2:
                    act.wait_ge(sems["hid1"], i - 1)
                ac(relu_h[i % 2][0:rows, :], P[i % 2][0:rows, :], ACT.Silu).then_inc(sems["silu1"], 1)
            act.wait_ge(sems["moe1_out"], 1)
            ac(o_t[:], P[4][:], ACT.Copy).then_inc(sems["o_sb"], 1)

        @block.vector
        def _(dve):
            v = nc.vector
            steps = [0]

            def link(ins):
                steps[0] += 1
                ins.then_inc(sems["dve_step"], 1)
                dve.wait_ge(sems["dve_step"], steps[0])

            def link_all(ins):
                steps[0] += 1
                ins.then_inc(sems["dve_step"], 1)

            def moments(src):
                for g in range(8):
                    link_all(v.bn_stats(stats[:, g, :], src[:, D * g:D * g + D]))
                dve.wait_ge(sems["dve_step"], steps[0])
                for g in range(8):
                    link_all(v.bn_aggr(mv[:, g, :], stats[:, g, :]))
                dve.wait_ge(sems["dve_step"], steps[0])

            roots = [0]

            def root(cols=8):
                roots[0] += 1
                dve.wait_ge(sems["rout"], roots[0])
                link(v.reciprocal(rout[:, 0:cols], root_sb[:, 0:cols]))

            def centre(src):
                link(v.tensor_tensor(heads(centred[:], 8), heads(src, 8), over(mv[:, :, 0], D), ALU.subtract))

            def scaled(dst, r):
                return v.tensor_tensor(heads(dst, 8), heads(centred[:], 8), over(r, D), ALU.mult)

            EPS = 1e-5

            def double_norm(src, dst, done, eps2):
                moments(src)
                v.tensor_scalar(rin[:, 0:8], mv[:, :, 1], 1.0 + eps2, EPS * eps2, ALU.mult,
                                ALU.add).then_inc(sems["rin"], 1)
                centre(src)
                root()
                scaled(dst, rout[:, 0:8]).then_inc(done, 1)

            def odd_values(a):
                a.wait(dve, "v_psum", 1)
                v.tensor_copy(a.V[64:128, :, a.hd + 1:2 * a.hd + 1],
                              P[7][64:128, :].rearrange("p (a b) -> p a b", b=a.hd)).then_inc(a.s("v"), 1)

            def centre_scores(a, u):
                a.wait(dve, "scores", u + 1)
                if u >= 2:
                    a.wait(dve, "probs", u - 1)
                src = P[u % 2][:]
                if a.shift:
                    dve.wait_ge(s_pos_in[u], 32)
                    src = cen_s[u % 2][:]
                    link(v.tensor_tensor(src, P[u % 2][:], shifted[u].rearrange("p g t -> p (g t)"), ALU.add))
                link(v.tensor_reduce(rowmax[u % 2][:], heads(src, 8), AX.X, ALU.max))
                v.tensor_tensor(heads(cen_s[u % 2][:], 8), heads(src, 8), over(rowmax[u % 2][:], S),
                                ALU.subtract).then_inc(a.s("centred"), 1)

            def normalise(a, u):
                a.wait(dve, "mixed", u + 1)
                if u >= 2:
                    a.wait(dve, "context_t", u - 1)
                o = P[4 + u % 2][:, 0:8 * (a.hd + 1)].rearrange("p (g d) -> p g d", g=8)
                link(v.reciprocal(rowsum[u % 2][:, 0:8], o[:, :, a.hd]))
                v.tensor_tensor(ctx_n[u % 2][:, 0:8 * a.hd].rearrange("p (g d) -> p g d", g=8), o[:, :, 0:a.hd],
                                over(rowsum[u % 2][:, 0:8], a.hd), ALU.mult).then_inc(a.s("context"), 1)

            def attention(a):
                for step in range(a.units + 3):
                    if step < a.units:
                        centre_scores(a, step)
                    if step >= 3:
                        normalise(a, step - 3)

            def one_hots(n):
                for k in range(2):
                    link_all(v.tensor_tensor(hot[k][:, :, 0:n], each(w["iota"][:, 0:n], 8), over(topf[:, :, k], n),
                                             ALU.is_equal))

            def weigh(n, done):
                for k in range(2):
                    link_all(v.tensor_tensor(hot[k][:, :, 0:n], hot[k][:, :, 0:n], over(w12[:, :, k], n), ALU.mult))
                dve.wait_ge(sems["dve_step"], steps[0])
                v.tensor_tensor(gates[:, :, 0:n], hot[0][:, :, 0:n], hot[1][:, :, 0:n],
                                ALU.add).then_inc(sems[done], 1)
                dve.wait_ge(sems[done], 1)

            def split3(n, done):
                def part(k):
                    return gates3[:, :, 2 * n * k:2 * n * k + 2 * n].rearrange("p q (h e) -> p q h e", h=2)
                g = gates[:, :, 0:n].rearrange("p (q h) e -> p q h e", h=2)
                r = resid[:, :, 0:n].rearrange("p (q h) e -> p q h e", h=2)
                link(v.tensor_copy(part(0), g))
                link(v.tensor_tensor(r, g, part(0), ALU.subtract))
                link(v.tensor_copy(part(1), r))
                v.tensor_tensor(part(2), r, part(1), ALU.subtract).then_inc(sems[done], 1)

            def split_x(src, ready, done):
                dve.wait_ge(sems[ready], 1)
                for h in range(2):
                    p = slice(64 * h, 64 * h + 64)
                    link_all(v.tensor_copy(x_split[h][p, :], src[p, :]))
                dve.wait_ge(sems["dve_step"], steps[0])
                for h in range(2):
                    p, other = slice(64 * h, 64 * h + 64), slice(64 - 64 * h, 128 - 64 * h)
                    v.tensor_tensor(x_split[h][other, :], src[p, :], x_split[h][p, :].bitcast(F32),
                                    ALU.subtract).then_inc(sems[done], 1)

            dve.wait_ge(sems["conv_n"], 1)
            moments(P[1])
            v.tensor_scalar(rin[:, 0:8], mv[:, :, 1], EPS, None, ALU.add).then_inc(sems["rin"], 1)
            centre(P[1][:])
            root()
            scaled(xn0[:], rout[:, 0:8]).then_inc(sems["n0"], 1)
            dve.wait_ge(sems["xn0_turned"], 1)
            dve.wait_ge(sems["pe_b"], 1)
            v.scalar_tensor_tensor(out=heads(h0_t[:], NB), in0=heads(P[2][:], NB), scalar=col["ln_w"],
                                   in1=each(pe_b[:], NB), op0=ALU.mult, op1=ALU.add).then_inc(sems["h0"], 1)
            dve.wait_ge(sems["ffn0_down"], 1)
            v.tensor_scalar(a0_t[:], P[7][:], col["ff_b2"], None, ALU.add).then_inc(attn0.s("context_sb"), 1)
            dve.wait_ge(sems["second"], 16)
            dve.wait_ge(sems["setup_pos"], 1)
            v.tensor_tensor(p_pos[:], each(P[6][:, 0:S], 4), over(w["mask4"], S), ALU.mult).then_inc(sems["p_pos"], 1)
            dve.wait_ge(sems["zeros"], 5)
            attn0.wait(dve, "k_psum", 1)
            v.tensor_scalar(q_bd[64:128, :, 64:128], heads(P[4][64:128, :], NB), col["bq0"][64:128], None,
                            ALU.add).then_inc(attn0.s("q"), 1)
            odd_values(attn0)
            attention(attn0)
            dve.wait_ge(sems["h1_psum"], 1)
            v.scalar_tensor_tensor(out=h1_t[:], in0=P[0][:], scalar=col["bp0"], in1=h0_t[:], op0=ALU.add,
                                   op1=ALU.add).then_inc(sems["h1"], 1)
            dve.wait_ge(sems["h1"], 1)
            dve.wait_ge(sems["ffn1_down"], 1)
            v.scalar_tensor_tensor(out=h2_t[:], in0=P[7][:], scalar=col["ff_b2"], in1=h1_t[:], op0=ALU.add,
                                   op1=ALU.add).then_inc(sems["h2"], 1)
            dve.wait_ge(sems["h2_n"], 1)
            double_norm(h2_n[:], xn[:], sems["xa_n"], EPS)
            dve.wait_ge(sems["bias1"], 2)
            attn1.wait(dve, "k_psum", 1)
            v.tensor_scalar(qv_bd[64:128, :, 64:128], heads(P[4][64:128, :], NB), bqv[64:128], None,
                            ALU.add).then_inc(attn1.s("q"), 1)
            for u in range(1, 4, 2):
                dve.wait_ge(sems["pos_psum"], u + 1)
                v.tensor_copy(pos_sb[u][:, :, 1:S + 1], heads(P[3][:], 8)).then_inc(sems["pos_sb_odd"], 1)
                if u == 1:
                    v.tensor_scalar(q_bd[64:128, :, 64:128], heads(P[4][64:128, :], NB), bqu[64:128], None,
                                    ALU.add).then_inc(attn1.s("q"), 1)
            odd_values(attn1)
            attention(attn1)
            dve.wait_ge(sems["h3_psum"], 1)
            dve.wait_ge(sems["h2_nb"], 1)
            v.tensor_tensor(h3_n[:], P[0][:], h2_nb[:], ALU.add).then_inc(sems["h3"], 1)
            dve.wait_ge(sems["h3"], 1)
            moments(h3_n)
            v.tensor_scalar(rin[:, 0:8], mv[:, :, 1], EPS, None, ALU.add).then_inc(sems["rin"], 1)
            centre(h3_n[:])
            root()
            scaled(y_n[:], rout[:, 0:8]).then_inc(sems["y_n"], 1)
            split_x(y_t, "y", "x0_split")
            dve.wait_ge(sems["third"], 16)
            dve.wait_ge(sems["gate_psum"], 1)
            link(v.tensor_tensor(logit[:], P[7][:, 0:8 * E0].rearrange("p (g e) -> p g e", g=8),
                                 each(w["gate_b"], 8), ALU.add))
            for g in range(8):
                link_all(v.max(top8[:, g, :], logit[:, g, :]))
            dve.wait_ge(sems["dve_step"], steps[0])
            for g in range(8):
                link_all(v.max_index(top8i[:, g, :], top8[:, g, :], logit[:, g, :]))
            v.tensor_tensor(gap[:], top8[:, :, 1], top8[:, :, 0], ALU.subtract).then_inc(sems["gap"], 1)
            dve.wait_ge(sems["dve_step"], steps[0])
            link(v.tensor_copy(topf[:], top8i[:]))
            one_hots(E0)
            dve.wait_ge(sems["egap"], 1)
            link(v.tensor_scalar(wsum[:], egap[:], 1.0, None, ALU.add))
            link(v.reciprocal(w12[:, :, 0], wsum[:]))
            link(v.tensor_tensor(w12[:, :, 1], w12[:, :, 0], egap[:], ALU.mult))
            weigh(E0, "gates")
            dve.wait_ge(sems["moe_zeros"], 1)
            split3(E0, "gates3")
            dve.wait_ge(sems["gates3_turned"], 1)
            v.tensor_copy(gates_t3[:], P[3][:].bitcast(BF16)[:, 0:NT]).then_inc(sems["gates_sb"], 1)
            for i in range(2 * E0):
                dve.wait_ge(sems["relu0"], i + 1)
                dve.wait_ge(sems["gate_b0"], i + 1)
                v.tensor_tensor(gated[i % 4][:], P[2 + i % 2][:], relu_h[i % 2][:], ALU.mult).then_inc(sems["hid0"], 1)
            dve.wait_ge(sems["moe0_out"], 1)
            v.tensor_tensor(z_t[:], P[4][:], y_t[:], ALU.add).then_inc(sems["z"], 1)
            dve.wait_ge(sems["z_turned"], 1)
            moments(P[0])
            v.tensor_scalar(rin[:, 0:8], mv[:, :, 1], EPS, None, ALU.add).then_inc(sems["rin"], 1)
            centre(P[0][:])
            root()
            link(scaled(xn[:], rout[:, 0:8]))
            link(v.tensor_tensor(heads(centred[:], 8), heads(xn[:], 8), each(w["gamma"], 8), ALU.mult))
            dve.wait_ge(sems["h3_nb"], 1)
            v.tensor_tensor(h4_n[:], centred[:], h3_nb[:], ALU.add).then_inc(sems["h4"], 1)
            dve.wait_ge(sems["h4"], 1)
            v.tensor_tensor(kq_w[:], col["kn"], col["qn"], ALU.mult).then_inc(sems["kq_w"], 1)
            moments(h4_n)
            v.tensor_scalar(rin[:, 0:8], mv[:, :, 1], EPS, None, ALU.add).then_inc(sems["rin"], 1)
            centre(h4_n[:])
            root()
            scaled(xn[:], rout[:, 0:8]).then_inc(sems["xb_n"], 1)
            for n in range(2):
                dve.wait_ge(sems["sq"], n + 1)
                pair = sq[:, 512 * n:512 * n + 512].rearrange("p (a d) -> p a d", d=2)
                link(v.tensor_tensor(qk_ms[:, 256 * n:256 * n + 256], pair[:, :, 0], pair[:, :, 1], ALU.add))
                v.tensor_scalar(qk_ms[:, 256 * n:256 * n + 256], qk_ms[:, 256 * n:256 * n + 256], 0.5, 1e-6,
                                ALU.mult, ALU.add).then_inc(sems["ms"], 1)
            for n in range(2):
                dve.wait_ge(sems["root"], n + 1)
                link(v.reciprocal(qk_ms[:, 256 * n:256 * n + 256], qk_r[:, 256 * n:256 * n + 256]))
                v.tensor_tensor(qk_n[:, 2 * n:2 * n + 2].rearrange("p q o (a d) -> p (q o a) d", d=2),
                                P[2 + n][:].rearrange("p (a d) -> p a d", d=2),
                                over(qk_ms[:, 256 * n:256 * n + 256], 2), ALU.mult).then_inc(sems["qk_n"], 1)
            attn2.wait(dve, "v_psum", 1)
            v_in = P[7][:].rearrange("p (b h g d) -> p b h g d", b=NB, h=2, d=2)
            v_out = V32.rearrange("p (b g) c -> p b g c", b=NB)
            for h in range(2):
                v.tensor_copy(v_out[64:128, :, :, 6 * h + 3:6 * h + 5], v_in[64:128, :, h]).then_inc(attn2.s("v"), 1)
            dve.wait_ge(sems["q_high"], 1)
            v.tensor_tensor(q_parts[1][:], P[4][:], q_parts[0][:].bitcast(F32), ALU.subtract).then_inc(sems["q_low"], 1)
            dve.wait_ge(sems["k32"], 1)
            v.tensor_copy(k_parts[0][:], k_t[:]).then_inc(sems["k_high"], 1)
            dve.wait_ge(sems["k_high"], 1)
            v.tensor_tensor(k_parts[1][:], k_t[:], k_parts[0][:].bitcast(F32), ALU.subtract).then_inc(sems["k_low"], 1)
            for g in range(4):
                dve.wait_ge(sems["k_rows"], g + 1)
                v.tensor_copy(keys32[:, g, :], P[(0, 1, 4, 5)[g]][:]).then_inc(sems["keys32"], 1)

            def normalise32(b):
                dve.wait_ge(sems["on"], b + 1)
                if b >= 2:
                    attn2.wait(dve, "context_t", b - 1)
                o = P[7][:].rearrange("p (a c) -> p a c", c=32)
                rs = rowsum[b % 2][:].rearrange("p (a o) -> p a o", o=2)
                cn = ctx_n[b % 2][:, 0:D].rearrange("p (a o d) -> p a o d", o=2, d=2)
                for h in range(2):
                    p = slice(64 * h, 64 * h + 64)
                    of = o[p, :, 6 * h:6 * h + 6].rearrange("p a (o d) -> p a o d", o=2)
                    link_all(v.reciprocal(rs[p], of[:, :, :, 2]))
                dve.wait_ge(sems["dve_step"], steps[0])
                for h in range(2):
                    p = slice(64 * h, 64 * h + 64)
                    of = o[p, :, 6 * h:6 * h + 6].rearrange("p a (o d) -> p a o d", o=2)
                    last = v.tensor_tensor(cn[p], of[:, :, :, 0:2],
                                           rs[p].unsqueeze(3).to_broadcast([64, 16, 2, 2]), ALU.mult)
                    if h == 0:
                        link_all(last)
                last.then_inc(attn2.s("context"), 1)

            for step in range(N32 + 7):
                if step < N32:
                    centre_scores(attn2, step)
                u = step - 6
                if 0 <= u < N32 and u % 4 == 3:
                    normalise32(u // 4)
            dve.wait_ge(sems["h5_psum"], 1)
            v.tensor_tensor(h5_n[:], P[0][:], h4_n[:], ALU.add).then_inc(sems["h5"], 1)
            dve.wait_ge(sems["h5"], 1)
            moments(h5_n)
            link(v.tensor_scalar(rin[:, 8:16], mv[:, :, 1], EPS, None, ALU.add))
            v.tensor_scalar(rin[:, 0:8], mv[:, :, 1], 1.0 + 1e-6, EPS * 1e-6, ALU.mult,
                            ALU.add).then_inc(sems["rin"], 1)
            centre(h5_n[:])
            root(16)
            scaled(xn[:], rout[:, 0:8]).then_inc(sems["xc_n"], 1)
            scaled(x_n[:], rout[:, 8:16]).then_inc(sems["x_n"], 1)
            for i, bank in enumerate((4, 5, 2, 3)):
                dve.wait_ge(sems["rope_psum"], i + 1)
                link_all(v.tensor_tensor(heads(rope[i], NB), heads(P[bank][:], NB),
                                         each(w["rope_c" if i % 2 == 0 else "rope_s"], NB), ALU.mult))
                if i == 1:
                    dve.wait_ge(sems["dve_step"], steps[0])
                    for h in range(2):
                        p = slice(64 * h, 64 * h + 64)
                        v.tensor_tensor(q_bd[p, :, 64 * h:64 * h + 64], heads(rope[0][p, :], NB),
                                        heads(rope[1][p, :], NB), ALU.add).then_inc(attn3.s("q"), 1)
            dve.wait_ge(sems["dve_step"], steps[0])
            v.tensor_tensor(k_t[:], rope[2], rope[3], ALU.add).then_inc(attn3.s("k"), 1)
            odd_values(attn3)
            attention(attn3)
            dve.wait_ge(sems["x2_psum"], 1)
            dve.wait_ge(sems["x_n"], 1)
            v.tensor_tensor(x2_n[:], P[0][:], x_n[:], ALU.add).then_inc(sems["x2"], 1)
            dve.wait_ge(sems["x2"], 1)
            moments(x2_n)
            link(v.tensor_tensor(msq[:], mv[:, :, 0], mv[:, :, 0], ALU.mult))
            v.scalar_tensor_tensor(out=rin[:, 0:8], in0=mv[:, :, 1], scalar=1e-6, in1=msq[:], op0=ALU.add,
                                   op1=ALU.add).then_inc(sems["rin"], 1)
            root()
            v.tensor_tensor(heads(xn[:], 8), heads(x2_n[:], 8), over(rout[:, 0:8], D), ALU.mult).then_inc(sems["f_n"], 1)
            split_x(f_t, "f", "x1_split")
            dve.wait_ge(sems["gate1_psum"], 1)
            lg = P[7][:, 0:8 * E1].rearrange("p (g e) -> p g e", g=8)
            link(v.tensor_reduce(gap[:], lg, AX.X, ALU.max))
            v.tensor_tensor(logit[:, :, 0:E1], lg, over(gap[:], E1), ALU.subtract).then_inc(sems["shift1"], 1)
            dve.wait_ge(sems["exp1"], 1)
            link(v.tensor_reduce(wsum[:], resid[:, :, 0:E1], AX.X, ALU.add))
            link(v.reciprocal(gap[:], wsum[:]))
            link(v.tensor_tensor(logit[:, :, 0:E1], resid[:, :, 0:E1], over(gap[:], E1), ALU.mult))
            for g in range(8):
                link_all(v.max(top8[:, g, :], logit[:, g, 0:E1]))
            dve.wait_ge(sems["dve_step"], steps[0])
            for g in range(8):
                link_all(v.max_index(top8i[:, g, :], top8[:, g, :], logit[:, g, 0:E1]))
            link_all(v.tensor_tensor(wsum[:], top8[:, :, 0], top8[:, :, 1], ALU.add))
            dve.wait_ge(sems["dve_step"], steps[0])
            link_all(v.tensor_copy(topf[:], top8i[:]))
            link(v.tensor_scalar(wsum[:], wsum[:], 1e-9, None, ALU.add))
            one_hots(E1)
            link(v.reciprocal(gap[:], wsum[:]))
            link(v.tensor_tensor(w12[:], top8[:, :, 0:2], over(gap[:], 2), ALU.mult))
            weigh(E1, "gates1")
            dve.wait_ge(sems["half_m"], 1)
            split3(E1, "gates31")
            dve.wait_ge(sems["gates1_turned"], 1)
            v.tensor_copy(gates_t3[:], P[7][:].bitcast(BF16)[:, 0:NT]).then_inc(sems["gates1_sb"], 1)
            for i in range(2 * T1):
                rows = min(128, H1ROWS - 128 * (i // 2))
                dve.wait_ge(sems["silu1"], i + 1)
                dve.wait_ge(sems["b1"], i + 1)
                link(v.tensor_tensor(relu_h[i % 2][0:rows, :], P[2 + i % 2][0:rows, :], relu_h[i % 2][0:rows, :],
                                     ALU.mult))
                dve.wait_ge(sems["g1"], i + 1)
                v.tensor_tensor(gated[i % 4][0:rows, :], P[5 + i % 2][0:rows, :], relu_h[i % 2][0:rows, :],
                                ALU.mult).then_inc(sems["hid1"], 1)
            dve.wait_ge(sems["o_turned"], 1)
            dve.wait_ge(sems["fin"], 1)
            v.tensor_tensor(out_n[:], P[0][:], fin_n[:], ALU.add).then_inc(sems["out_ready"], 1)

        @block.gpsimd
        def _(pool):
            g = nc.gpsimd
            def keys(a):
                cols = S * a.per
                for u in range(a.units):
                    if u == 0:
                        a.wait(pool, "k", 1)
                    if u >= 2:
                        a.wait(pool, "scores", u - 1)
                    for n in range(a.per):
                        b = a.per * u + n
                        ins = g.tensor_tensor(
                            R[u % 2][:, 512 // a.per * n:512 // a.per * (n + 1)].rearrange("p (h j) -> p h j", j=S),
                            each(k_t[:, S * b:S * b + S], a.H), over(a.mask, S), ALU.mult)
                    ins.then_inc(a.s("keys"), 1)

            def split_weights(raw, split, loaded, n, done):
                pool.wait_ge(sems[loaded], n)
                for h in range(2):
                    p = slice(64 * h, 64 * h + 64)
                    g.tensor_copy(split[h][p, :], raw[p, :]).then_inc(sems[done], 1)
                pool.wait_ge(sems[done], 2)
                for h in range(2):
                    p = slice(64 * h, 64 * h + 64)
                    g.tensor_tensor(split[1 - h][p, :], raw[p, :], split[h][p, :].bitcast(F32),
                                    ALU.subtract).then_inc(sems[done], 1)
                pool.wait_ge(sems[done], 4)

            g.memset(one[:], 1.0).then_inc(sems["one"], 1)
            g.memset(q_bd[:], 0.0).then_inc(sems["zeros"], 1)
            g.memset(V0[:], 0.0).then_inc(sems["zeros"], 1)
            g.memset(qv_bd[:], 0.0).then_inc(sems["zeros"], 1)
            pool.wait_ge(sems["zeros"], 3)
            g.memset(V0[0:64, :, 8:9], 1.0).then_inc(sems["zeros"], 1)
            g.memset(V0[64:128, :, 17:18], 1.0).then_inc(sems["zeros"], 1)
            pool.wait_ge(sems["zeros"], 5)
            pool.wait_ge(sems["first"], 16)
            g.tensor_scalar(pe_b[:], w["pe_t"], col["ln_b"], None, ALU.add).then_inc(sems["pe_b"], 1)
            g.memset(V4[:], 0.0).then_inc(sems["ones"], 1)
            for i in range(4):
                g.memset(pos_sb[i], 0.0).then_inc(sems["ones"], 1)
            pool.wait_ge(sems["ones"], 5)
            g.memset(V4[0:64, :, 16:17], 1.0).then_inc(sems["ones"], 1)
            g.memset(V4[64:128, :, 33:34], 1.0).then_inc(sems["ones"], 1)
            pool.wait_ge(sems["ones"], 7)
            keys(attn0)
            attn0.wait(pool, "keys", attn0.units)
            split_weights(raw0, w1_split, "moe0", 32, "w1_split")
            pool.wait_ge(sems["second"], 16)
            g.tensor_tensor(bqv[:], col["bq1"], col["v1"], ALU.add).then_inc(sems["bias1"], 1)
            g.tensor_tensor(bqu[:], col["bq1"], col["u1"], ALU.add).then_inc(sems["bias1"], 1)
            pool.wait_ge(sems["h2_n"], 1)
            g.tensor_tensor(heads(h2_nb[:], 8), heads(h2_n[:], 8), each(w["bout"], 8), ALU.add).then_inc(sems["h2_nb"], 1)
            keys(attn1)
            g.memset(gates3[:], 0.0).then_inc(sems["moe_zeros"], 1)
            pool.wait_ge(sems["third"], 16)
            pool.wait_ge(sems["h3"], 1)
            g.tensor_tensor(heads(h3_nb[:], 8), heads(h3_n[:], 8), each(w["beta"], 8), ALU.add).then_inc(sems["h3_nb"], 1)
            pool.wait_ge(sems["h3_nb"], 1)
            split_weights(raw1, u_split, "moe1", 64, "u_split")
            g.memset(V32, 0.0).then_inc(sems["moe_zeros"], 1)
            pool.wait_ge(sems["moe_zeros"], 2)
            for h in range(2):
                g.memset(V32[0:64, :, 6 * h + 2:6 * h + 3], 1.0).then_inc(sems["moe_zeros"], 1)
                g.memset(V32[64:128, :, 6 * h + 5:6 * h + 6], 1.0).then_inc(sems["moe_zeros"], 1)
            pool.wait_ge(sems["moe_zeros"], 6)
            pool.wait_ge(sems["expander"], 16)
            g.tensor_copy(expander[:], expand_raw).then_inc(sems["expander"], 1)
            for u in range(N32):
                b, grp = u // 4, u % 4
                if u < 4:
                    pool.wait_ge(sems["keys32"], grp + 1)
                if u >= 2:
                    attn2.wait(pool, "scores", u - 1)
                g.tensor_tensor(heads(R32[u % 2][:], 8), each(keys32[:, grp, S * b:S * b + S], 8),
                                over(w["maskr"], S), ALU.mult).then_inc(sems["ops2"], 1)
            keys(attn3)
            pool.wait_ge(sems["x2"], 1)
            g.tensor_tensor(fin_n[:], x2_n[:], h5_n[:], ALU.add).then_inc(sems["fin"], 1)
            g.memset(gates3[:], 0.0).then_inc(sems["half_m"], 1)


def block_diagonal(a):
    k, n = a.shape
    out = np.zeros((2 * k, 2 * n), a.dtype)
    out[:k, :n] = a
    out[k:, n:] = a
    return out


def rows128(a):
    out = np.zeros((128, a.shape[1]), a.dtype)
    out[:a.shape[0]] = a
    return out


def twice(a):
    return np.concatenate([a, a], axis=0)


def value_weights(wv, H):
    d = D // H
    v = wv.reshape(D, H // 2, 2, d)
    return np.concatenate([block_diagonal(np.ascontiguousarray(v[:, :, o, :]).reshape(D, D // 2)) for o in range(2)],
                          axis=1)


def angles(n, positions):
    i = np.arange(0, n, 2, dtype=np.float32)
    return i, np.arange(positions, dtype=np.float32)[:, None]


def lay_out(a):
    f = np.float32
    a = {k: np.asarray(v) for k, v in a.items()}
    x = a["x"].reshape(B, C, IMG // PATCH, PATCH, IMG // PATCH, PATCH)
    patches = np.ascontiguousarray(x.transpose(1, 3, 5, 0, 2, 4)).reshape(KC, 128, 2 * NT)

    i, pos = angles(D, S)
    div = np.exp(-np.log(f(10000.0)) * i / f(D)).astype(f)
    pe = np.zeros((S, D), f)
    pe[:, 0::2], pe[:, 1::2] = np.sin(pos * div), np.cos(pos * div)
    div1 = np.exp(i * f(-np.log(10000.0) / D)).astype(f)
    pe1 = np.zeros((S, D), f)
    pe1[:, 0::2], pe1[:, 1::2] = np.sin(pos * div1), np.cos(pos * div1)

    c = np.arange(D)

    def mask(n, of):
        return twice((of[:, None] == np.arange(n)[None, :]).astype(f))

    def column(*cols):
        return np.stack([twice(x.reshape(-1, 1))[:, 0] if x.size == D else x.reshape(-1) for x in cols], axis=1)

    def pad(m, n):
        return np.concatenate([m, np.zeros((128, n - m.shape[1]), m.dtype)], axis=1)

    qkv = a["L0_tok_qkv_w"].T
    qkv_b = a["L0_tok_qkv_b"]
    ffup = a["L0_tok_ff_w1"].T
    zero = np.zeros((D, FF), f)
    ffb = a["L0_tok_ff_b1"]
    qn, kn = (np.tile(a[f"L1_attn_{n}n_w"], D // 2) for n in "qk")
    first = {
        "conv_w": a["L0_tok_conv_w"].reshape(D, KC, 128).transpose(2, 1, 0).reshape(128, KC * D),
        "ident": np.eye(128, dtype=f),
        "cols0": pad(column(a["L0_tok_conv_b"], a["L0_tok_ln_w"], a["L0_tok_ln_b"], ffb[:128], ffb[128:],
                            a["L0_tok_ff_b2"]), 8),
        "pe_t": twice(pe.T),
    }
    ffn_w = {
        "up_lo": np.concatenate([ffup, zero]), "up_hi": np.concatenate([zero, ffup]),
        "down": a["L0_tok_ff_w2"].T.reshape(2, 128, D).transpose(1, 0, 2).reshape(128, 2 * D),
    }
    second = {
        "wq0": block_diagonal(qkv[:, :D]), "wk0": block_diagonal(qkv[:, D:2 * D]),
        "wv0": value_weights(qkv[:, 2 * D:], 8), "wp0": block_diagonal(a["L0_tok_proj_w"].T),
        "cols1": pad(column(qkv_b[:D], qkv_b[D:2 * D], qkv_b[2 * D:], a["L0_tok_proj_b"], a["L0_attn_ln_gamma"],
                            a["L0_attn_ln_beta"], a["L0_attn_bq"], a["L0_attn_bk"], a["L0_attn_bv"],
                            a["L0_attn_u_bias"].reshape(-1), a["L0_attn_v_bias"].reshape(-1)), 16),
        "mask8": mask(8, c // 8), "mask4": mask(4, c // 16),
        "wpos": rows128(np.concatenate([a["L0_attn_Wpos"]] * 2, axis=1)), "pe_s": rows128(pe1.T),
        "wq1": block_diagonal(a["L0_attn_Wq"]), "wk1": block_diagonal(a["L0_attn_Wk"]),
        "wv1": value_weights(a["L0_attn_Wv"], 4), "wo1": block_diagonal(a["L0_attn_Wout"]),
        "bout": np.tile(a["L0_attn_bout"], (128, 1)),
    }
    wq, wk, wv = (a[f"L1_ffn_w{n}"].T for n in "qkv")
    rep = (np.arange(4)[:, None] // 2 * 16 + np.arange(16)[None, :]).reshape(-1)
    swap = (np.arange(4)[:, None] * 16 + (np.arange(16)[None, :] + 8) % 16).reshape(-1)
    wk, wv = wk[:, rep], wv[:, rep]
    inv = 1.0 / 10000.0 ** (np.arange(0, 16, 2, dtype=f) / 16)
    fr = np.outer(np.arange(S, dtype=f), inv)
    emb = np.concatenate([fr, fr], axis=-1)
    cos, sin = np.cos(emb).astype(f), np.sin(emb).astype(f)
    sign = np.where(np.arange(16) < 8, -1.0, 1.0).astype(f)
    qk2 = a["L1_attn_w_qkv"].T
    third = {
        "gate": block_diagonal(a["L0_ffn_gate_w"]), "gate_b": np.tile(a["L0_ffn_gate_b"], (128, 1)),
        "iota": np.tile(np.arange(E0, dtype=f), (128, 1)), "b2": rows128(block_diagonal(a["L0_ffn_b2"])),
        "b1": a["L0_ffn_b1"].T, "gamma": np.tile(a["L0_ffn_gamma"], (128, 1)),
        "beta": np.tile(a["L0_ffn_beta"], (128, 1)),
        "wqk2": np.concatenate([block_diagonal(qk2[:, :D]), block_diagonal(qk2[:, D:2 * D])], axis=1),
        "wv2": value_weights(qk2[:, 2 * D:], 32), "wp2": block_diagonal(a["L1_attn_w_proj"].T),
        "maskr": mask(8, c // 2 % 8), 
        "maskh": (np.arange(128)[:, None] // 16 % 2 == np.arange(2)[None, :]).astype(f),
        "cols2": column(qn, kn, a["L1_ffn_ln1_w"], a["L1_ffn_ln2_w"]),
        "wq3": block_diagonal(wq), "wqs3": block_diagonal(wq[:, swap]),
        "wk3": block_diagonal(wk), "wks3": block_diagonal(wk[:, swap]),
        "wv3": value_weights(wv, 4), "wo3": block_diagonal(a["L1_ffn_wo"].T),
        "rope_c": twice(np.tile(cos.T, (4, 1))), "rope_s": twice(np.tile((sin * sign).T, (4, 1))),
        "router": block_diagonal(a["L1_ffn_router_w"].T),
    }
    key = np.arange(512) % S
    query = np.arange(128) % S
    sel1 = np.zeros((128, 2, H1ROWS), f)
    eye3 = np.zeros((128, 2 * E0), f)
    for p in range(3):
        eye3[2 * E0 * p:2 * E0 * (p + 1)] = np.eye(2 * E0, dtype=f)
        for h in range(2):
            for e in range(E1):
                sel1[2 * E1 * p + E1 * h + e, h, F1 * e:F1 * (e + 1)] = 1.0
    half = {"identb": np.eye(128, dtype=f), "causal": np.where(key[None, :] > query[:, None], f(NEG), f(0.0)),
            "eye3": eye3, "sel1": sel1.reshape(128, -1)}

    row = np.arange(128)
    spread = np.zeros((128, 4, 4, 128), f)
    for part in range(4):
        of = row // 64 if part < 2 else row // 32 % 2
        for g in range(4):
            spread[64 * (row // 16 % 2) + 16 * g + row % 16, part, g, row] = of == part % 2

    def packed(name, parts):
        got = [parts[n] for n, _ in PACKS[name]]
        assert [g.shape[1] for g in got] == [n for _, n in PACKS[name]], name
        return np.ascontiguousarray(np.concatenate(got, axis=1))

    def hidden(wt):
        return np.ascontiguousarray(wt.reshape(H1ROWS, D).T)

    w2 = np.zeros((T1 * 128, D), f)
    w2[:H1ROWS] = a["L1_ffn_w2"].transpose(0, 2, 1).reshape(H1ROWS, D)
    return {
        "patches": patches,
        "first": packed("first", first), "ffn_w": packed("ffn", ffn_w), "second": packed("second", second), "third": packed("third", third),
        "half_consts": np.ascontiguousarray(packed("half", half).view(np.uint16)[:, 1::2]),
        "expand": spread.reshape(128, -1),
        "moe0_w1": np.ascontiguousarray(a["L0_ffn_w1"].transpose(1, 0, 2)).reshape(D, E0 * F0),
        "moe0_w2": np.ascontiguousarray(a["L0_ffn_w2"].transpose(1, 0, 2)).reshape(F0, E0 * D),
        "moe1_w1": hidden(a["L1_ffn_w1"]), "moe1_w3": hidden(a["L1_ffn_w3"]),
        "moe1_w2": np.ascontiguousarray(w2.reshape(T1, 128, D).transpose(1, 0, 2)).reshape(128, T1 * D),
    }


def kernel(**inputs):
    import concourse.bacc as bacc
    from concourse.bass_utils import run_bass_kernel_spmd

    arrays = lay_out(inputs)
    nc = bacc.Bacc("TRN2", target_bir_lowering=False, num_devices=1)
    args = {n: nc.dram_tensor(f"in_{n}", x.shape, mybir.dt.from_np(x.dtype), kind="ExternalInput").ap()
            for n, x in arrays.items()}
    out = nc.dram_tensor("out_tokens", (128, NT), F32, kind="ExternalOutput").ap()
    tower_program(nc, **args, out=out)
    r = run_bass_kernel_spmd(nc, [{f"in_{n}": x for n, x in arrays.items()}], core_ids=[0])
    got = r.results[0]["out_tokens"]
    return np.ascontiguousarray(got.reshape(2, S, NQ, 2, D).transpose(3, 2, 0, 1, 4)).reshape(B, S, D)
```

```python
from contextlib import ExitStack

import numpy as np

import concourse.bass as bass
from concourse import mybir

F32 = mybir.dt.float32
BF16 = mybir.dt.bfloat16
F32R = mybir.dt.float32r
U16 = mybir.dt.uint16
U32 = mybir.dt.uint32
ALU = mybir.AluOpType
ACT = mybir.ActivationFunctionType
AX = mybir.AxisListType

B, C, IMG, PATCH = 16, 3, 128, 16
D = 64
S = (IMG // PATCH) ** 2
NB = B // 2
NT = NB * S
NQ = NT // 128
KC = C * PATCH * PATCH // 128
FF = 256
E0, F0 = 16, 128
E1, F1 = 8, 170
H1ROWS = E1 * F1
T1 = -(-H1ROWS // 128)
NEG = -1e30
EARLY = 6

PACKS = {
    "first": [("conv_w", KC * D), ("ident", 128), ("cols0", 8), ("pe_t", S)],
    "ffn": [("up_lo", FF), ("up_hi", FF), ("down", 2 * D)],
    "second": [("wq0", 128), ("wk0", 128), ("wv0", 2 * D), ("wp0", 128), ("cols1", 16), ("mask8", 8),
               ("mask4", 4), ("wpos", 128), ("pe_s", S), ("wq1", 128), ("wk1", 128), ("wv1", 2 * D),
               ("wo1", 128), ("bout", D)],
    "third": [("gate", 2 * E0), ("gate_b", E0), ("iota", E0), ("b2", 128), ("b1", E0), ("gamma", D), ("beta", D),
              ("wqk2", 256), ("wv2", 2 * D), ("wp2", 128), ("maskr", 8), ("maskh", 2), ("cols2", 4),
              ("wq3", 128), ("wqs3", 128), ("wk3", 128), ("wks3", 128), ("wv3", 2 * D), ("wo3", 128),
              ("rope_c", S), ("rope_s", S), ("router", 2 * E1)],
    "half": [("identb", 128), ("causal", 512), ("eye3", 2 * E0), ("sel1", 2 * H1ROWS)],
}
COL0 = ["conv_b", "ln_w", "ln_b", "ff_b1a", "ff_b1b", "ff_b2"]
COL1 = ["bq0", "bk0", "bv0", "bp0", "gamma1", "beta1", "bq1", "bk1", "bv1", "u1", "v1"]
COL2 = ["qn", "kn", "ln1", "ln2"]


def width(pack):
    return sum(n for _, n in PACKS[pack])


def tower_program(nc, patches, first, ffn_w, second, third, half_consts, expand, moe0_w1, moe0_w2,
                  moe1_w1, moe1_w3, moe1_w2, out):
    with ExitStack() as ctx:
        def sb(name, shape, dt=F32):
            return ctx.enter_context(nc.sbuf_tensor(name, shape, dt))

        sems = {}

        def sem(name):
            if name not in sems:
                sems[name] = ctx.enter_context(nc.semaphore(name))
            return sems[name]

        P = [ctx.enter_context(nc.psum_tensor(f"bank{i}", [128, 512], F32)) for i in range(8)]
        pos_scratch = nc.dram_tensor("pos_scratch", [NB // 2, 8, 2 * (S + 1) * S], F32, kind="Internal").ap()

        xt = sb("xt", [128, KC, 2 * NT])
        pk = {n: sb(f"pack_{n}", [128, width(n)], U16 if n == "half" else F32) for n in PACKS}
        w = {}
        for n, items in PACKS.items():
            at = 0
            for name, cols in items:
                w[name] = pk[n][:, at:at + cols].bitcast(BF16) if n == "half" else pk[n][:, at:at + cols]
                at += cols
        col = {}
        for base, names in (("cols0", COL0), ("cols1", COL1), ("cols2", COL2)):
            for i, name in enumerate(names):
                col[name] = w[base][:, i:i + 1]
        ident = w["ident"]
        identb = w["identb"]

        w1_both = sb("w1_both", [128, 2 * E0 * F0], F32R)
        w1_split = [w1_both[:, E0 * F0 * i:E0 * F0 * (i + 1)] for i in range(2)]
        raw0 = xt[:, 0:2, :].rearrange("p k n -> p (k n)")
        raw1 = xt[:, 2:5, :].rearrange("p k n -> p (k n)")[:, 0:2 * H1ROWS]
        w2_sb = sb("w2_sb", [128, E0 * D])
        u_split = [sb(f"u_split{i}", [128, 2 * H1ROWS], F32R) for i in range(2)]
        x_split = [sb(f"x_split{h}", [128, NT], F32R) for h in range(2)]
        d1_sb = sb("d1_sb", [128, T1 * D])

        def big(name):
            return sb(name, [128, NT])

        conv_t, xn0, h0_t, a0_t, h1_t, h2_t = (big(n) for n in ("conv_t", "xn0", "h0_t", "a0_t", "h1_t", "h2_t"))
        centred, xn = big("centred"), big("xn")
        hid_all = sb("hid_all", [128, 4, NT])
        hid = [hid_all[:, i] for i in range(4)]
        pe_b = sb("pe_b", [128, S])
        stats = sb("stats", [128, 8, 6])
        mv = sb("mv", [128, 8, 2])
        rin = sb("rin", [128, 16])
        rout = sb("rout", [128, 16])
        msq = sb("msq", [128, 8])
        root_sb = sb("root_sb", [128, 16])
        one = sb("one", [128, 1])
        scrap = sb("scrap", [128, 24])

        q_bd = sb("q_bd", [128, NB, 128])
        qv_bd = sb("qv_bd", [128, NB, 128])
        k_t = big("k_t")
        R = [sb(f"R{i}", [128, 512]) for i in range(2)]
        cen_s = [sb(f"cen_s{i}", [128, 512]) for i in range(2)]
        prob = [sb(f"prob{i}", [128, 512]) for i in range(2)]
        prob_t = [sb(f"prob_t{i}", [128, 512]) for i in range(2)]
        queries32 = w1_both[:].rearrange("p (g b h i) -> p g b h i", g=4, b=NB, h=2)
        keys32 = hid_all
        R32 = x_split
        q_parts = [sb(f"q_part{x}", [128, NT], F32R) for x in range(2)]
        k_parts = [sb(f"k_part{x}", [128, NT], F32R) for x in range(2)]
        expand_raw = xt[:, 4:6, :].rearrange("p k n -> p (k n)")
        expander = sb("expander", [128, 4 * 4 * 128], F32R)
        kq_w = sb("kq_w", [128, 1])
        rowmax = [sb(f"rowmax{i}", [128, 8]) for i in range(2)]
        rowsum = [sb(f"rowsum{i}", [128, 32]) for i in range(2)]
        ctx_n = [sb(f"ctx_n{i}", [128, 128]) for i in range(2)]
        ctx_t = big("ctx_t")
        V0 = sb("V0", [128, 2 * NB * 4, 2 * 9])
        V4 = sb("V4", [128, 2 * NB * 2, 2 * 17])
        V32 = xt[:, 0:4, :].rearrange("p k n -> p (k n)").rearrange("p (g c) -> p g c", c=32)
        out_ts = [sb(f"out_ts{i}", [128, 512]) for i in range(2)]
        bqu = sb("bqu", [128, 1])
        bqv = sb("bqv", [128, 1])
        p_pos = sb("p_pos", [128, 4, S])
        pos_all = sb("pos_all", [128, 4, 8, S + 1])
        shifted_all = sb("shifted_all", [128, 4, 8, S])
        pos_sb = [pos_all[:, i] for i in range(4)]
        shifted = [shifted_all[:, i] for i in range(4)]
        h2_n, h2_nb, h4_n = (big(n) for n in ("h2_n", "h2_nb", "h4_n"))
        xa_t, xb_t, z_t = a0_t, a0_t, a0_t
        y_n, y_t, h3_n, h3_nb = conv_t, xn0, h0_t, h2_n
        xc_t, x_n, x2_n, fin_n, f_t, o_t, out_n, h5_n = conv_t, xn0, h0_t, a0_t, h1_t, h2_t, h2_n, h2_nb
        logit = sb("logit", [128, 8, E0])
        top8 = sb("top8", [128, 8, 8])
        top8i = sb("top8i", [128, 8, 8], U32)
        topf = sb("topf", [128, 8, 8])
        gap = sb("gap", [128, 8])
        egap = sb("egap", [128, 8])
        wsum = sb("wsum", [128, 8])
        w12 = sb("w12", [128, 8, 2])
        hot = [sb(f"hot{i}", [128, 8, E0]) for i in range(2)]
        gates = sb("gates", [128, 8, E0])
        resid = sb("resid", [128, 8, E0])
        gates3 = sb("gates3", [128, NQ, 128], BF16)
        gates_t3 = sb("gates_t3", [128, NT], BF16)
        gates_t = ctx_t[0:2 * E0, :]
        gate_sb = silu = out_ts
        sq = shifted_all[:, 0:2].rearrange("p i g t -> p (i g t)")
        qk_ms, qk_r = (shifted[i].rearrange("p g t -> p (g t)") for i in (2, 3))
        qk_n = pos_all[:].rearrange("p i g t -> p (i g t)")[:, 0:1024].rearrange("p (q o c) -> p q o c", q=NQ, o=2)
        rope = [xt[:, 4 + i // 2, NT * (i % 2):NT * (i % 2) + NT] for i in range(4)]
        early = xt[:].rearrange("p k n -> p (k n)")
        early_a = [early[:, NT * i:NT * i + NT] for i in range(EARLY)]
        early_b = [early[:, NT * (EARLY + i):NT * (EARLY + i) + NT] for i in range(EARLY)]

        def heads(t, n):
            return t.rearrange("p (a b) -> p a b", a=n)

        def over(t, n):
            return t.unsqueeze(2).to_broadcast([t.shape[0], t.shape[1], n])

        def each(t, n):
            return t.unsqueeze(1).to_broadcast([t.shape[0], n, t.shape[1]])

        class Attn:

            def __init__(self, H, scale, V, mask, signals, units=None, causal=False, shift=False):
                self.H, self.hd, self.scale = H, D // H, scale
                self.per = 8 // H
                self.units = units or NB // self.per
                self.V, self.mask, self.causal, self.shift = V, mask, causal, shift
                self.base = dict(counted)
                for what in ("scores", "centred", "probs", "turned", "probs_t", "mixed"):
                    counted[what] += self.units
                for what, n in signals.items():
                    counted[what] += n

            def s(self, what):
                return sems[f"attn_{what}"]

            def wait(self, engine, what, n):
                engine.wait_ge(sems[f"attn_{what}"], self.base[what] + n)

        counted = dict.fromkeys(("q", "k_psum", "k", "v_psum", "v", "keys", "scores", "centred", "probs", "turned",
                                 "probs_t", "mixed", "context", "context_t", "context_sb"), 0)
        for what in counted:
            sem(f"attn_{what}")
        attn0 = Attn(8, 1.0 / np.sqrt(8.0), V0, w["mask8"],
                     dict(q=2, k_psum=2, k=1, v_psum=1, v=2, keys=8, context=8, context_t=8, context_sb=2))
        attn1 = Attn(4, 1.0 / 8.0, V4, w["mask4"],
                     dict(q=4, k_psum=2, k=1, v_psum=1, v=2, keys=4, context=4, context_t=4, context_sb=1), shift=True)
        attn2 = Attn(8, 1.0 / np.sqrt(2.0), V32, w["maskr"],
                     dict(v_psum=1, v=4, context=NB, context_t=NB, context_sb=1), units=4 * NB)
        attn3 = Attn(4, 1.0 / 4.0, V4, w["mask4"],
                     dict(q=2, k=1, v_psum=1, v=2, keys=4, context=4, context_t=4, context_sb=1), causal=True)
        N32 = 4 * NB

        for name in ("b1_sb", "early1", "conv", "conv_t", "conv_n", "n0", "xn0_turned", "h0", "pe_b",
                     "setup_pos", "p_pos", "bias1", "zeros", "ones", "moe_zeros", "w1_split", "u_split",
                     "moe0_down", "moe1_down", "x0_split", "x1_split", "half_m", "dve_step", "rin", "rout",
                     "one", "first", "ffn_w", "second", "third", "halfw", "moe0", "moe1", "out", "h1_psum",
                     "h1", "h2", "h2_turned", "h2_n", "h2_nb", "xa_n", "xa_turned", "xa", "pos_psum", "pos_sb",
                     "pos_sb_odd", "h3_psum", "h3", "h3_nb", "y_n", "y_turned", "y", "gate_psum", "gap", "egap",
                     "gates", "gates3", "gates_turned", "gates3_turned", "gates_sb", "up0", "gate_b0", "relu0",
                     "z", "z_turned", "h4", "xb_n", "xb_turned", "xb", "qk_psum", "sq", "ms", "root", "qk_n",
                     "qk_turned", "kq_w", "expander", "q_high", "q_low", "k32", "k_high", "k_low", "q_rows",
                     "k_rows", "queries32", "keys32", "ops2", "ots", "on", "h5_psum", "h5", "xc_n", "xc_turned",
                     "xc", "x_n", "rope_psum", "x2_psum", "x2", "fin", "f_n", "f_turned", "f", "gate1_psum",
                     "shift1", "exp1", "gates1", "gates31", "gates1_turned", "gates1_sb", "a1", "b1", "g1",
                     "silu1", "hid1", "moe1_out", "o_sb", "o_turned", "out_ready", "gate_rows", "down0",
                     "weighed0", "bias0"):
            sem(name)
        for n in range(2):
            for what in ("up", "gelu", "down"):
                sem(f"ffn{n}_{what}")
        s_x = [sem(f"patches{k}") for k in range(KC)]
        s_pos_out = [sem(f"pos_out{i}") for i in range(4)]
        s_pos_in = [sem(f"pos_in{i}") for i in range(4)]
        block = ctx.enter_context(nc.Block())

        @block.sync
        def _(sp):
            sp.dma_start(pk["first"][:], first).then_inc(sems["first"], 16)
            for k in range(KC):
                sp.dma_start(xt[:, k, :], patches[k]).then_inc(s_x[k], 16)
            sp.dma_start(pk["ffn"][:], ffn_w).then_inc(sems["ffn_w"], 16)
            sp.dma_start(pk["second"][:], second).then_inc(sems["second"], 16)
            sp.dma_start(pk["third"][:], third).then_inc(sems["third"], 16)
            sp.dma_start(pk["half"][:], half_consts).then_inc(sems["halfw"], 16)
            sp.dma_start(w2_sb[:], moe0_w2).then_inc(sems["moe0_down"], 16)
            sp.dma_start(d1_sb[:], moe1_w2).then_inc(sems["moe1_down"], 16)
            sp.wait_ge(sems["conv"], 1)
            for h in range(2):
                sp.dma_start(raw0[64 * h:64 * h + 64, :], moe0_w1).then_inc(sems["moe0"], 16)
            for h in range(2):
                sp.dma_start(raw1[64 * h:64 * h + 64, 0:H1ROWS], moe1_w1).then_inc(sems["moe1"], 16)
                sp.dma_start(raw1[64 * h:64 * h + 64, H1ROWS:2 * H1ROWS], moe1_w3).then_inc(sems["moe1"], 16)
            half = (S + 1) * S
            for step in range(6):
                u = step
                if u < 4:
                    sp.wait_ge(sems["pos_sb_odd" if u % 2 else "pos_sb"], u // 2 + 1)
                    sp.dma_start(pos_scratch[u].rearrange("g (p t) -> p g t", t=S + 1),
                                 pos_sb[u]).then_inc(s_pos_out[u], 16)
                u = step - 2
                if 0 <= u < 4:
                    sp.wait_ge(s_pos_out[u], 16)
                    for h in range(2):
                        sp.dma_start(shifted[u][64 * h:64 * h + 64],
                                     pos_scratch[u, :, half * h + S:half * (h + 1)].rearrange("g (i t) -> i g t", t=S)
                                     ).then_inc(s_pos_in[u], 16)
            sp.wait_ge(sems["u_split"], 4)
            sp.dma_start(expand_raw, expand).then_inc(sems["expander"], 16)
            for n in range(2):
                sp.wait_ge(sems["out_ready"], n + 1)
                sp.dma_start(out[:, 256 * n:256 * n + 256], out_n[:, 256 * n:256 * n + 256]).then_inc(sems["out"], 16)
            sp.wait_ge(sems["out"], 32)

        @block.tensor
        def _(pe):
            mm = nc.tensor.matmul

            def keep_warm(n, bank, early=False):
                for _ in range(n):
                    if early:
                        mm(P[bank][:, 0:128], ident, ident, start=True, stop=True)
                    else:
                        mm(P[bank][:], identb, w["causal"], start=True, stop=True)

            def turn(dst, src):
                for q in range(NQ):
                    last = nc.tensor.transpose(dst[:, 128 * q:128 * q + 128], src[:, 128 * q:128 * q + 128], ident)
                return last

            def ffn(n, src):
                banks = [P[i] for i in (2, 3, 4, 5)]
                for f in range(2):
                    for h in range(2):
                        lhs = w["up_lo" if h == 0 else "up_hi"][:, 128 * f:128 * f + 128]
                        mm(banks[2 * f + h][:], lhs, src[:], start=True, stop=True).then_inc(sems[f"ffn{n}_up"], 1)
                for f in range(2):
                    for h in range(2):
                        pe.wait_ge(sems[f"ffn{n}_gelu"], 2 * f + h + 1)
                        last = mm(P[7][64 * h:64 * h + 64, :], w["down"][:, D * f:D * f + D], hid[2 * f + h][:],
                                  start=(f == 0), stop=(f == 1))
                last.then_inc(sems[f"ffn{n}_down"], 1)

            def values(a, src, wv):
                for b in range(NB):
                    for o in range(2):
                        last = mm(P[7][64 * o:64 * o + 64, D * b:D * b + D], src[:, S * b:S * b + S],
                                  wv[:, D * o:D * o + D], start=True, stop=True)
                last.then_inc(a.s("v_psum"), 1)

            def context_t(a, u, images):
                a.wait(pe, "context", u + 1)
                for n, b in enumerate(images):
                    for h in range(2):
                        last = mm(P[6][64 * h:64 * h + 64, S * b:S * b + S], ctx_n[u % 2][:, D * n:D * n + D],
                                  ident[:, 64 * h:64 * h + 64], start=True, stop=True)
                last.then_inc(a.s("context_t"), 1)

            def turn_probs(a, u):
                a.wait(pe, "probs", u + 1)
                if u >= 2:
                    a.wait(pe, "probs_t", u - 1)
                for x in range(4):
                    last = nc.tensor.transpose(P[2 + u % 2][:, 128 * x:128 * x + 128],
                                               prob[u % 2][:, 128 * x:128 * x + 128], ident)
                last.then_inc(a.s("turned"), 1)

            def attention(a):
                wide = 2 * (a.hd + 1)
                for step in range(a.units + 4):
                    u = step
                    if u < a.units:
                        a.wait(pe, "keys", u + 1)
                        if u == 0:
                            a.wait(pe, "q", 2)
                        if u >= 2:
                            a.wait(pe, "centred", u - 1)
                        cols = 512 // a.per
                        for n in range(a.per):
                            if a.causal:
                                mm(P[u % 2][:, cols * n:cols * n + cols], identb, w["causal"][:, 0:cols],
                                   start=True, stop=False)
                            last = mm(P[u % 2][:, cols * n:cols * n + cols], q_bd[:, a.per * u + n, :],
                                      R[u % 2][:, cols * n:cols * n + cols], start=not a.causal, stop=True)
                        last.then_inc(a.s("scores"), 1)
                    u = step - 2
                    if 0 <= u < a.units:
                        turn_probs(a, u)
                    u = step - 3
                    if 0 <= u < a.units:
                        a.wait(pe, "probs_t", u + 1)
                        if u == 0:
                            a.wait(pe, "v", 2)
                        if u >= 2:
                            a.wait(pe, "context", u - 1)
                        for x in range(4):
                            b, hp = a.per * u + x // (4 // a.per), x % (4 // a.per)
                            for h in range(2):
                                last = mm(P[4 + u % 2][64 * h:64 * h + 64, wide * x:wide * x + wide],
                                          prob_t[u % 2][:, 128 * x + 64 * h:128 * x + 64 * h + 64],
                                          a.V[:, (2 * b + h) * (a.H // 2) + hp, :], start=True, stop=True)
                        last.then_inc(a.s("mixed"), 1)
                    u = step - 4
                    if 0 <= u < a.units:
                        context_t(a, u, range(a.per * u, a.per * u + a.per))

            def project_n(src, weight, dst, done):
                for q in range(NQ):
                    last = mm(dst[:, 128 * q:128 * q + 128], src[:, 128 * q:128 * q + 128], weight,
                              start=True, stop=True)
                last.then_inc(done, 1)

            pe.wait_ge(sems["first"], 16)
            for k in range(KC):
                pe.wait_ge(s_x[k], 16)
                for h in range(2):
                    last = mm(P[0][64 * h:64 * h + 64, :], w["conv_w"][:, D * k:D * k + D],
                              xt[:, k, NT * h:NT * h + NT], start=(k == 0), stop=(k == KC - 1))
            last.then_inc(sems["conv"], 1)
            keep_warm(2, 7, early=True)
            pe.wait_ge(sems["conv_t"], 1)
            turn(P[1], conv_t).then_inc(sems["conv_n"], 1)
            keep_warm(6, 7, early=True)
            pe.wait_ge(sems["rin"], 1)
            keep_warm(4, 7, early=True)
            pe.wait_ge(sems["n0"], 1)
            turn(P[2], xn0).then_inc(sems["xn0_turned"], 1)
            keep_warm(3, 7, early=True)
            pe.wait_ge(sems["h0"], 1)
            pe.wait_ge(sems["ffn_w"], 16)
            ffn(0, h0_t)
            pe.wait_ge(sems["second"], 16)
            mm(P[6][:, 0:S], w["wpos"][0:64, :], w["pe_s"][0:64, :], start=True,
               stop=True).then_inc(sems["setup_pos"], 1)
            pe.wait_ge(sems["ffn0_down"], 1)
            pe.wait_ge(sems["halfw"], 16)
            keep_warm(2, 1, early=True)
            attn0.wait(pe, "context_sb", 1)
            mm(P[5][:], w["wk0"], a0_t[:], start=True, stop=True).then_inc(attn0.s("k_psum"), 1)
            mm(P[4][:], w["wq0"], a0_t[:], start=True, stop=True).then_inc(attn0.s("k_psum"), 1)
            values(attn0, a0_t, w["wv0"])
            keep_warm(1, 3)
            attention(attn0)
            keep_warm(3, 1)
            attn0.wait(pe, "context_sb", 2)
            mm(P[0][:], w["wp0"], ctx_t[:], start=True, stop=True).then_inc(sems["h1_psum"], 1)
            keep_warm(3, 1)
            pe.wait_ge(sems["h1"], 1)
            ffn(1, h1_t)
            keep_warm(3, 1)
            pe.wait_ge(sems["h2"], 1)
            turn(P[0], h2_t).then_inc(sems["h2_turned"], 1)
            keep_warm(6, 3)
            pe.wait_ge(sems["rin"], 2)
            keep_warm(4, 3)
            pe.wait_ge(sems["xa_n"], 1)
            turn(P[1], xn).then_inc(sems["xa_turned"], 1)
            keep_warm(3, 3)
            pe.wait_ge(sems["xa"], 1)
            mm(P[4][:], w["wq1"], xa_t[:], start=True, stop=True).then_inc(attn1.s("k_psum"), 1)
            keep_warm(3, 0)
            pe.wait_ge(sems["p_pos"], 1)
            attn1.wait(pe, "q", 2)
            for u in range(4):
                if u >= 2:
                    pe.wait_ge(sems["pos_sb_odd" if u % 2 else "pos_sb"], u // 2)
                for n in range(2):
                    last = mm(P[2 + u % 2][:, 256 * n:256 * n + 256], qv_bd[:, 2 * u + n, :],
                              p_pos[:].rearrange("p h t -> p (h t)"), start=True, stop=True)
                last.then_inc(sems["pos_psum"], 1)
                if u == 1:
                    mm(P[5][:], w["wk1"], xa_t[:], start=True, stop=True).then_inc(attn1.s("k_psum"), 1)
            values(attn1, xa_t, w["wv1"])
            attn1.wait(pe, "q", 4)
            keep_warm(1, 0)
            attention(attn1)
            keep_warm(2, 1)
            attn1.wait(pe, "context_sb", 1)
            project_n(ctx_t, w["wo1"], P[0], sems["h3_psum"])
            keep_warm(8, 3)
            pe.wait_ge(sems["rin"], 3)
            keep_warm(4, 3)
            pe.wait_ge(sems["y_n"], 1)
            turn(P[1], y_n).then_inc(sems["y_turned"], 1)
            keep_warm(2, 3)
            pe.wait_ge(sems["y"], 1)
            for q in range(NQ):
                last = mm(P[7][:, 32 * q:32 * q + 32], y_t[:, 128 * q:128 * q + 128], w["gate"], start=True, stop=True)
            last.then_inc(sems["gate_psum"], 1)

            def gates_turn3(dst, wait, done):
                pe.wait_ge(sems[wait], 1)
                t = dst[:].bitcast(BF16)
                for q in range(NQ):
                    last = nc.tensor.transpose(t[:, 128 * q:128 * q + 128], gates3[:, q, :], identb)
                last.then_inc(sems[done], 1)

            UB = [P[0], P[1], P[5]]
            EB = [P[2], P[3], P[6]]
            pe.wait_ge(sems["w1_split"], 4)
            keep_warm(1, 3)
            pe.wait_ge(sems["moe0_down"], 16)

            def gate_rows(e):
                if e >= 2:
                    pe.wait_ge(sems["gate_rows"], e - 1)
                for h in range(2):
                    last = mm(P[4 + 3 * (e % 2)][64 * h:64 * h + 64, :],
                              w["eye3"][:, E0 * h + e:E0 * h + e + 1].to_broadcast([128, D]), gates_t3[:],
                              start=True, stop=True)
                last.then_inc(sems["gate_b0"], 1)

            for step in range(2 * E0 + 3):
                i = step
                if i < 2 * E0:
                    if i < 2:
                        pe.wait_ge(sems["x0_split"], i + 1)
                    if i >= 3:
                        pe.wait_ge(sems["relu0"], i - 2)
                    for k in range(2):
                        last = mm(UB[i % 3][:], w1_split[k][:, F0 * (i // 2):F0 * (i // 2) + F0], x_split[i % 2][:],
                                  start=(k == 0), stop=(k == 1))
                    last.then_inc(sems["up0"], 1)
                if i == 2 * E0:
                    pe.wait_ge(sems["relu0"], 30)
                    mm(P[5][:], w["b2"][0:2 * E0, :], gates_t, start=True, stop=True).then_inc(sems["bias0"], 1)
                i = step - 3
                if i == 6:
                    pe.wait_ge(sems["gates_sb"], 2)
                    for e in range(3):
                        gate_rows(e)
                if i >= 0:
                    e, h = i // 2, i % 2
                    pe.wait_ge(sems["relu0"], i + 1)
                    if h == 0 and e >= 3:
                        pe.wait_ge(sems["weighed0"], e - 2)
                    mm(EB[e % 3][64 * h:64 * h + 64, :], w2_sb[:, D * e:D * e + D], hid[i % 4][:],
                       start=True, stop=True).then_inc(sems["down0"], 1)
                if i == 5:
                    pe.wait_ge(sems["gates"], 1)
                    for q in range(NQ):
                        last = nc.tensor.transpose(P[7][0:32, 128 * q:128 * q + 128],
                                                   gates[:, 2 * q:2 * q + 2, :].rearrange("p a b -> p (a b)"), ident)
                    last.then_inc(sems["gates_turned"], 1)
                    gates_turn3(P[4], "gates3", "gates3_turned")
                if i >= 7 and i % 2 == 1:
                    gate_rows(i // 2)
            pe.wait_ge(sems["weighed0"], 14)
            keep_warm(5, 0)
            pe.wait_ge(sems["weighed0"], 16)
            keep_warm(2, 0)
            pe.wait_ge(sems["z"], 1)
            turn(P[0], z_t).then_inc(sems["z_turned"], 1)
            keep_warm(6, 3)
            pe.wait_ge(sems["rin"], 4)
            keep_warm(8, 3)
            pe.wait_ge(sems["h4"], 1)
            keep_warm(6, 3)
            pe.wait_ge(sems["rin"], 5)
            keep_warm(4, 3)
            pe.wait_ge(sems["xb_n"], 1)
            turn(P[1], xn).then_inc(sems["xb_turned"], 1)
            keep_warm(3, 6)
            pe.wait_ge(sems["xb"], 1)
            for q in range(NQ):
                last = mm(P[2 + q // 2][:, 256 * (q % 2):256 * (q % 2) + 256], xb_t[:, 128 * q:128 * q + 128],
                          w["wqk2"], start=True, stop=True)
                if q % 2:
                    last.then_inc(sems["qk_psum"], 1)
            values(attn2, xb_t, w["wv2"])
            keep_warm(7, 6)
            for n in range(2):
                pe.wait_ge(sems["qk_n"], n + 1)
                for o in range(2):
                    for q in (2 * n, 2 * n + 1):
                        last = nc.tensor.transpose(P[4 + o][:, 128 * q:128 * q + 128], qk_n[:, q, o, :], ident)
                    if n == 1:
                        last.then_inc(sems["qk_turned"], 1)
            keep_warm(3, 6)
            pe.wait_ge(sems["expander"], 17)
            attn2.wait(pe, "v", 4)
            sides = ((0, (6, 7, 2, 3), q_parts, "q_high", "q_low", "q_rows"),
                     (1, (0, 1, 4, 5), k_parts, "k_high", "k_low", "k_rows"))
            for side, g in ((0, 0), (0, 1), (1, 0), (1, 1), (0, 2), (1, 2), (0, 3), (1, 3)):
                o, banks, parts, high, low, done = sides[side]
                pe.wait_ge(sems[high], 1)
                pe.wait_ge(sems[low], 1)
                for x in range(2):
                    at = 128 * (4 * (2 * o + x) + g)
                    last = mm(P[banks[g]][:], expander[:, at:at + 128], parts[x][:], start=(x == 0), stop=(x == 1))
                last.then_inc(sems[done], 1)
            a = attn2
            for step in range(N32 + 8):
                u = step
                if u < N32:
                    b, g = u // 4, u % 4
                    pe.wait_ge(sems["ops2"], u + 1)
                    if u < 4:
                        pe.wait_ge(sems["queries32"], g + 1)
                    if u < 2:
                        pe.wait_ge(sems["keys32"], u + 1)
                    if u >= 2:
                        a.wait(pe, "centred", u - 1)
                    mm(P[u % 2][:], identb, w["causal"], start=True, stop=False)
                    mm(P[u % 2][:], queries32[:, g, b].rearrange("p h i -> p (h i)"), R32[u % 2][:],
                       start=False, stop=True).then_inc(a.s("scores"), 1)
                u = step - 2
                if 0 <= u < N32:
                    if u == 0:
                        pe.wait_ge(sems["queries32"], 4)
                    turn_probs(a, u)
                u = step - 3
                if 0 <= u < N32:
                    b, g = u // 4, u % 4
                    a.wait(pe, "probs_t", u + 1)
                    if u == 0:
                        pe.wait_ge(sems["keys32"], 4)
                    if g == 0 and b >= 2:
                        pe.wait_ge(sems["ots"], b - 1)
                    for x in range(4):
                        last = mm(P[4 + b % 2][32 * x:32 * x + 32, 128 * g:128 * g + 128],
                                  V32[:, 16 * b + 4 * g + x, :], prob_t[u % 2][:, 128 * x:128 * x + 128],
                                  start=True, stop=True)
                    last.then_inc(a.s("mixed"), 1)
                u = step - 5
                if 0 <= u < N32 and u % 4 == 3:
                    b = u // 4
                    pe.wait_ge(sems["ots"], b + 1)
                    if b >= 1:
                        a.wait(pe, "context", b)
                    for g in range(4):
                        last = nc.tensor.transpose(P[7][:, 128 * g:128 * g + 128],
                                                   out_ts[b % 2][:, 128 * g:128 * g + 128], ident)
                    last.then_inc(sems["on"], 1)
                u = step - 8
                if 0 <= u < N32 and u % 4 == 3:
                    context_t(a, u // 4, [u // 4])
            keep_warm(2, 1)
            a.wait(pe, "context_sb", 1)
            project_n(ctx_t, w["wp2"], P[0], sems["h5_psum"])
            keep_warm(9, 3)
            pe.wait_ge(sems["rin"], 6)
            keep_warm(4, 3)
            pe.wait_ge(sems["xc_n"], 1)
            turn(P[1], xn).then_inc(sems["xc_turned"], 1)
            keep_warm(3, 6)
            pe.wait_ge(sems["xc"], 1)
            for bank, name in ((2, "wk3"), (3, "wks3"), (4, "wq3"), (5, "wqs3")):
                mm(P[bank][:], w[name], xc_t[:], start=True, stop=True).then_inc(sems["rope_psum"], 1)
            values(attn3, xc_t, w["wv3"])
            keep_warm(3, 6)
            attention(attn3)
            keep_warm(2, 1)
            attn3.wait(pe, "context_sb", 1)
            project_n(ctx_t, w["wo3"], P[0], sems["x2_psum"])
            keep_warm(9, 3)
            pe.wait_ge(sems["rin"], 7)
            keep_warm(3, 3)
            pe.wait_ge(sems["f_n"], 1)
            turn(P[1], xn).then_inc(sems["f_turned"], 1)
            keep_warm(3, 3)
            pe.wait_ge(sems["f"], 1)
            for q in range(NQ):
                last = mm(P[7][:, 16 * q:16 * q + 16], f_t[:, 128 * q:128 * q + 128], w["router"], start=True,
                          stop=True)
            last.then_inc(sems["gate1_psum"], 1)
            pe.wait_ge(sems["u_split"], 4)
            keep_warm(1, 3)

            def ups1(i):
                t, h = i // 2, i % 2
                rows = min(128, H1ROWS - 128 * t)
                if i < 2:
                    pe.wait_ge(sems["x1_split"], i + 1)
                if i >= 2:
                    pe.wait_ge(sems["silu1"], i - 1)
                for k in range(2):
                    last = mm(P[h][0:rows, :], u_split[k][:, 128 * t:128 * t + rows], x_split[h][:],
                              start=(k == 0), stop=(k == 1))
                last.then_inc(sems["a1"], 1)
                if i >= 2:
                    pe.wait_ge(sems["b1_sb" if i < EARLY + 2 else "hid1"], i - 1)
                for k in range(2):
                    last = mm(P[2 + h][0:rows, :], u_split[k][:, H1ROWS + 128 * t:H1ROWS + 128 * t + rows],
                              x_split[h][:], start=(k == 0), stop=(k == 1))
                last.then_inc(sems["b1"], 1)

            def down1(t):
                rows = min(128, H1ROWS - 128 * t)
                for h in range(2):
                    pe.wait_ge(sems["hid1"], 2 * t + h + 1)
                    last = mm(P[4][64 * h:64 * h + 64, :], d1_sb[0:rows, D * t:D * t + D],
                              hid[(2 * t + h) % 4][0:rows, :], start=(t == 0), stop=(t == T1 - 1))
                return last

            for i in range(EARLY):
                ups1(i)
            keep_warm(1, 5)
            gates_turn3(P[7], "gates31", "gates1_turned")
            pe.wait_ge(sems["gates1_sb"], 1)
            pe.wait_ge(sems["moe1_down"], 16)
            for t in range(T1):
                rows = min(128, H1ROWS - 128 * t)
                for h in range(2):
                    i = 2 * t + h
                    if i >= EARLY + 2:
                        ups1(i)
                    if i >= 2:
                        pe.wait_ge(sems["hid1"], i - 1)
                    mm(P[5 + h][0:rows, :], w["sel1"][:, H1ROWS * h + 128 * t:H1ROWS * h + 128 * t + rows],
                       gates_t3[:], start=True, stop=True).then_inc(sems["g1"], 1)
                    if i in (2, 3):
                        ups1(i + EARLY - 2)
                if t >= 1:
                    down1(t - 1)
            down1(T1 - 1).then_inc(sems["moe1_out"], 1)
            keep_warm(1, 1)
            pe.wait_ge(sems["o_sb"], 1)
            for q in range(NQ):
                if q == NQ // 2:
                    pe.wait_ge(sems["o_sb"], 2)
                nc.tensor.transpose(P[q // 2][:, 128 * q:128 * q + 128], o_t[:, 128 * q:128 * q + 128],
                                    ident).then_inc(sems["o_turned"], 1)

        @block.scalar
        def _(act):
            ac = nc.scalar.activation

            def gelu(n):
                for i in range(4):
                    act.wait_ge(sems[f"ffn{n}_up"], i + 1)
                    ac(hid[i][:], P[2 + i][:], ACT.Gelu_apprx_tanh,
                       bias=col["ff_b1a" if i < 2 else "ff_b1b"]).then_inc(sems[f"ffn{n}_gelu"], 1)

            roots, loads = [0], [0]

            def load_table(function):
                loads[0] += 1
                ac(scrap[:, loads[0]:loads[0] + 1], one[:], function)

            def root(cols=8, then=None):
                roots[0] += 1
                act.wait_ge(sems["rin"], roots[0])
                ac(root_sb[:, 0:cols], rin[:, 0:cols], ACT.Sqrt).then_inc(sems["rout"], 1)
                if then is not None:
                    load_table(then)

            def even_values(a):
                a.wait(act, "v_psum", 1)
                ac(a.V[0:64, :, 0:a.hd], P[7][0:64, :].rearrange("p (a b) -> p a b", b=a.hd),
                   ACT.Copy).then_inc(a.s("v"), 1)

            def attention(a, units):
                for step in range(units + 1):
                    u = step
                    if u < units:
                        a.wait(act, "centred", u + 1)
                        if u >= 2:
                            a.wait(act, "turned", u - 1)
                        ac(prob[u % 2][:], cen_s[u % 2][:], ACT.Exp, scale=a.scale).then_inc(a.s("probs"), 1)
                    u = step - 1
                    if 0 <= u < units:
                        a.wait(act, "turned", u + 1)
                        if u >= 2:
                            a.wait(act, "mixed", u - 1)
                        ac(prob_t[u % 2][:], P[2 + u % 2][:], ACT.Copy).then_inc(a.s("probs_t"), 1)
                        if units == N32 and u % 4 == 1 and u > 4:
                            gather(u // 4 - 1)
                if units == N32:
                    gather(NB - 1)

            def gather(b):
                attn2.wait(act, "mixed", 4 * b + 4)
                if b >= 2:
                    act.wait_ge(sems["on"], b - 1)
                ac(out_ts[b % 2][:], P[4 + b % 2][:], ACT.Copy).then_inc(sems["ots"], 1)

            act.wait_ge(sems["one"], 1)
            load_table(ACT.Sqrt)
            act.wait_ge(sems["first"], 16)
            act.wait_ge(sems["conv"], 1)
            ac(conv_t[:], P[0][:], ACT.Identity, bias=col["conv_b"]).then_inc(sems["conv_t"], 1)
            root(then=ACT.Gelu_apprx_tanh)
            gelu(0)
            load_table(ACT.Exp)
            act.wait_ge(sems["second"], 16)
            act.wait_ge(sems["zeros"], 5)
            attn0.wait(act, "k_psum", 1)
            ac(k_t[:], P[5][:], ACT.Identity, bias=col["bk0"]).then_inc(attn0.s("k"), 1)
            attn0.wait(act, "k_psum", 2)
            ac(q_bd[0:64, :, 0:64], heads(P[4][0:64, :], NB), ACT.Identity,
               bias=col["bq0"][0:64]).then_inc(attn0.s("q"), 1)
            even_values(attn0)
            attention(attn0, attn0.units)
            load_table(ACT.Gelu_apprx_tanh)
            attn0.wait(act, "context_t", attn0.units)
            ac(ctx_t[:], P[6][:], ACT.Identity, bias=col["bv0"]).then_inc(attn0.s("context_sb"), 1)
            gelu(1)
            load_table(ACT.Sqrt)
            root(then=ACT.Exp)
            act.wait_ge(sems["xa_n"], 1)
            ac(h2_n[:], P[0][:], ACT.Copy).then_inc(sems["h2_n"], 1)
            act.wait_ge(sems["xa_turned"], 1)
            ac(xa_t[:], P[1][:], ACT.Identity, bias=col["beta1"], scale=col["gamma1"]).then_inc(sems["xa"], 1)
            act.wait_ge(sems["bias1"], 2)
            attn1.wait(act, "k_psum", 1)
            ac(qv_bd[0:64, :, 0:64], heads(P[4][0:64, :], NB), ACT.Identity,
               bias=bqv[0:64]).then_inc(attn1.s("q"), 1)
            for u in range(0, 4, 2):
                act.wait_ge(sems["pos_psum"], u + 1)
                ac(pos_sb[u][:, :, 1:S + 1], heads(P[2 + u % 2][:], 8), ACT.Copy).then_inc(sems["pos_sb"], 1)
                if u == 0:
                    ac(q_bd[0:64, :, 0:64], heads(P[4][0:64, :], NB), ACT.Identity,
                       bias=bqu[0:64]).then_inc(attn1.s("q"), 1)
            attn1.wait(act, "k_psum", 2)
            ac(k_t[:], P[5][:], ACT.Identity, bias=col["bk1"]).then_inc(attn1.s("k"), 1)
            even_values(attn1)
            attention(attn1, attn1.units)
            load_table(ACT.Sqrt)
            attn1.wait(act, "context_t", attn1.units)
            ac(ctx_t[:], P[6][:], ACT.Identity, bias=col["bv1"]).then_inc(attn1.s("context_sb"), 1)
            act.wait_ge(sems["third"], 16)
            root(then=ACT.Exp)
            act.wait_ge(sems["y_turned"], 1)
            ac(y_t[:], P[1][:], ACT.Copy).then_inc(sems["y"], 1)
            UB = [P[0], P[1], P[5]]

            def gate_rows(e):
                act.wait_ge(sems["gate_b0"], e + 1)
                if e >= 2:
                    act.wait_ge(sems["weighed0"], e - 1)
                ac(gate_sb[e % 2][:], P[4 + 3 * (e % 2)][:], ACT.Copy).then_inc(sems["gate_rows"], 1)

            for i in range(2 * E0):
                if i == 3:
                    act.wait_ge(sems["gap"], 1)
                    ac(egap[:], gap[:], ACT.Exp).then_inc(sems["egap"], 1)
                act.wait_ge(sems["up0"], i + 1)
                if i >= 4:
                    act.wait_ge(sems["down0"], i - 3)
                ac(hid[i % 4][:], UB[i % 3][:], ACT.Relu,
                   bias=w["b1"][:, i // 2:i // 2 + 1]).then_inc(sems["relu0"], 1)
                if i == 7:
                    act.wait_ge(sems["gates_turned"], 1)
                    ac(gates_t, P[7][0:32, :], ACT.Copy).then_inc(sems["gates_sb"], 1)
                if i == 8:
                    for e in range(3):
                        gate_rows(e)
                if i >= 10 and i % 2 == 0:
                    gate_rows(i // 2 - 2)
            for e in range(E0 - 2, E0):
                gate_rows(e)
            load_table(ACT.Sqrt)
            root()
            root()
            act.wait_ge(sems["moe_zeros"], 6)
            act.wait_ge(sems["xb_turned"], 1)
            ac(xb_t[:], P[1][:], ACT.Copy).then_inc(sems["xb"], 1)
            for n in range(2):
                act.wait_ge(sems["qk_psum"], n + 1)
                ac(sq[:, 512 * n:512 * n + 512], P[2 + n][:], ACT.Square).then_inc(sems["sq"], 1)
            for n in range(2):
                act.wait_ge(sems["ms"], n + 1)
                ac(qk_r[:, 256 * n:256 * n + 256], qk_ms[:, 256 * n:256 * n + 256],
                   ACT.Sqrt).then_inc(sems["root"], 1)
            attn2.wait(act, "v_psum", 1)
            v_in = P[7][:].rearrange("p (b h g d) -> p b h g d", b=NB, h=2, d=2)
            v_out = V32.rearrange("p (b g) c -> p b g c", b=NB)
            for h in range(2):
                ac(v_out[0:64, :, :, 6 * h:6 * h + 2], v_in[0:64, :, h], ACT.Copy).then_inc(attn2.s("v"), 1)
            load_table(ACT.Exp)
            act.wait_ge(sems["qk_turned"], 1)
            ac(q_parts[0][:], P[4][:], ACT.Copy).then_inc(sems["q_high"], 1)
            act.wait_ge(sems["qk_turned"], 2)
            act.wait_ge(sems["kq_w"], 1)
            ac(k_t[:], P[5][:], ACT.Copy, scale=kq_w[:]).then_inc(sems["k32"], 1)
            for g in range(4):
                act.wait_ge(sems["q_rows"], g + 1)
                for h in range(2):
                    last = ac(queries32[:, g, :, h], heads(P[(6, 7, 2, 3)[g]][:], NB), ACT.Copy,
                              scale=w["maskh"][:, h:h + 1])
                last.then_inc(sems["queries32"], 1)
            attention(attn2, N32)
            load_table(ACT.Sqrt)
            attn2.wait(act, "context_t", NB)
            ac(ctx_t[:], P[6][:], ACT.Copy).then_inc(attn2.s("context_sb"), 1)
            root(16, then=ACT.Exp)
            act.wait_ge(sems["xc_turned"], 1)
            ac(xc_t[:], P[1][:], ACT.Copy, scale=col["ln1"]).then_inc(sems["xc"], 1)
            even_values(attn3)
            attention(attn3, attn3.units)
            load_table(ACT.Sqrt)
            attn3.wait(act, "context_t", attn3.units)
            ac(ctx_t[:], P[6][:], ACT.Copy).then_inc(attn3.s("context_sb"), 1)
            root(then=ACT.Exp)
            act.wait_ge(sems["f_turned"], 1)
            ac(f_t[:], P[1][:], ACT.Copy, scale=col["ln2"]).then_inc(sems["f"], 1)
            act.wait_ge(sems["shift1"], 1)
            ac(resid[:, :, 0:E1], logit[:, :, 0:E1], ACT.Exp).then_inc(sems["exp1"], 1)
            load_table(ACT.Silu)
            for i in range(2 * T1):
                rows = min(128, H1ROWS - 128 * (i // 2))
                act.wait_ge(sems["a1"], i + 1)
                if i >= EARLY + 2:
                    act.wait_ge(sems["hid1"], i - 1)
                dst = early_a[i] if i < EARLY else silu[i % 2][0:rows, :]
                ac(dst, P[i % 2][0:rows, :], ACT.Silu).then_inc(sems["silu1"], 1)
                if i < EARLY:
                    act.wait_ge(sems["b1"], i + 1)
                    ac(early_b[i], P[2 + i % 2][:], ACT.Copy).then_inc(sems["b1_sb"], 1)
            act.wait_ge(sems["moe1_out"], 1)
            for n in range(2):
                ac(o_t[:, 256 * n:256 * n + 256], P[4][:, 256 * n:256 * n + 256], ACT.Copy).then_inc(sems["o_sb"], 1)

        @block.vector
        def _(dve):
            v = nc.vector
            steps = [0]

            def link(ins):
                steps[0] += 1
                ins.then_inc(sems["dve_step"], 1)
                dve.wait_ge(sems["dve_step"], steps[0])

            def link_all(ins):
                steps[0] += 1
                ins.then_inc(sems["dve_step"], 1)

            def moments(src):
                for g in range(8):
                    link_all(v.bn_stats(stats[:, g, :], src[:, D * g:D * g + D]))
                dve.wait_ge(sems["dve_step"], steps[0])
                for g in range(8):
                    link_all(v.bn_aggr(mv[:, g, :], stats[:, g, :]))
                dve.wait_ge(sems["dve_step"], steps[0])

            roots = [0]

            def root(cols=8):
                roots[0] += 1
                dve.wait_ge(sems["rout"], roots[0])
                link(v.reciprocal(rout[:, 0:cols], root_sb[:, 0:cols]))

            def centre(src):
                link(v.tensor_tensor(heads(centred[:], 8), heads(src, 8), over(mv[:, :, 0], D), ALU.subtract))

            def scaled(dst, r):
                return v.tensor_tensor(heads(dst, 8), heads(centred[:], 8), over(r, D), ALU.mult)

            EPS = 1e-5

            def double_norm(src, dst, done, eps2):
                moments(src)
                v.tensor_scalar(rin[:, 0:8], mv[:, :, 1], 1.0 + eps2, EPS * eps2, ALU.mult,
                                ALU.add).then_inc(sems["rin"], 1)
                centre(src)
                root()
                scaled(dst, rout[:, 0:8]).then_inc(done, 1)

            def odd_values(a):
                a.wait(dve, "v_psum", 1)
                v.tensor_copy(a.V[64:128, :, a.hd + 1:2 * a.hd + 1],
                              P[7][64:128, :].rearrange("p (a b) -> p a b", b=a.hd)).then_inc(a.s("v"), 1)

            def centre_scores(a, u):
                a.wait(dve, "scores", u + 1)
                if u >= 2:
                    a.wait(dve, "probs", u - 1)
                src = P[u % 2][:]
                if a.shift:
                    dve.wait_ge(s_pos_in[u], 32)
                    src = cen_s[u % 2][:]
                    link(v.tensor_tensor(src, P[u % 2][:], shifted[u].rearrange("p g t -> p (g t)"), ALU.add))
                link(v.tensor_reduce(rowmax[u % 2][:], heads(src, 8), AX.X, ALU.max))
                v.tensor_tensor(heads(cen_s[u % 2][:], 8), heads(src, 8), over(rowmax[u % 2][:], S),
                                ALU.subtract).then_inc(a.s("centred"), 1)

            def normalise(a, u):
                a.wait(dve, "mixed", u + 1)
                if u >= 2:
                    a.wait(dve, "context_t", u - 1)
                o = P[4 + u % 2][:, 0:8 * (a.hd + 1)].rearrange("p (g d) -> p g d", g=8)
                link(v.reciprocal(rowsum[u % 2][:, 0:8], o[:, :, a.hd]))
                v.tensor_tensor(ctx_n[u % 2][:, 0:8 * a.hd].rearrange("p (g d) -> p g d", g=8), o[:, :, 0:a.hd],
                                over(rowsum[u % 2][:, 0:8], a.hd), ALU.mult).then_inc(a.s("context"), 1)

            def attention(a):
                for step in range(a.units + 3):
                    if step < a.units:
                        centre_scores(a, step)
                    if step >= 3:
                        normalise(a, step - 3)

            def one_hots(n):
                for k in range(2):
                    link_all(v.tensor_tensor(hot[k][:, :, 0:n], each(w["iota"][:, 0:n], 8), over(topf[:, :, k], n),
                                             ALU.is_equal))

            def weigh(n, done):
                for k in range(2):
                    link_all(v.tensor_tensor(hot[k][:, :, 0:n], hot[k][:, :, 0:n], over(w12[:, :, k], n), ALU.mult))
                dve.wait_ge(sems["dve_step"], steps[0])
                v.tensor_tensor(gates[:, :, 0:n], hot[0][:, :, 0:n], hot[1][:, :, 0:n],
                                ALU.add).then_inc(sems[done], 1)
                dve.wait_ge(sems[done], 1)

            def split3(n, done):
                def part(k):
                    return gates3[:, :, 2 * n * k:2 * n * k + 2 * n].rearrange("p q (h e) -> p q h e", h=2)
                g = gates[:, :, 0:n].rearrange("p (q h) e -> p q h e", h=2)
                r = resid[:, :, 0:n].rearrange("p (q h) e -> p q h e", h=2)
                link(v.tensor_copy(part(0), g))
                link(v.tensor_tensor(r, g, part(0), ALU.subtract))
                link(v.tensor_copy(part(1), r))
                v.tensor_tensor(part(2), r, part(1), ALU.subtract).then_inc(sems[done], 1)

            def split_x(src, ready, done):
                dve.wait_ge(sems[ready], 1)
                for h in range(2):
                    p, other = slice(64 * h, 64 * h + 64), slice(64 - 64 * h, 128 - 64 * h)
                    link(v.tensor_copy(x_split[h][p, :], src[p, :]))
                    v.tensor_tensor(x_split[h][other, :], src[p, :], x_split[h][p, :].bitcast(F32),
                                    ALU.subtract).then_inc(sems[done], 1)

            dve.wait_ge(sems["conv_n"], 1)
            moments(P[1])
            v.tensor_scalar(rin[:, 0:8], mv[:, :, 1], EPS, None, ALU.add).then_inc(sems["rin"], 1)
            centre(P[1][:])
            root()
            scaled(xn0[:], rout[:, 0:8]).then_inc(sems["n0"], 1)
            dve.wait_ge(sems["xn0_turned"], 1)
            dve.wait_ge(sems["pe_b"], 1)
            v.scalar_tensor_tensor(out=heads(h0_t[:], NB), in0=heads(P[2][:], NB), scalar=col["ln_w"],
                                   in1=each(pe_b[:], NB), op0=ALU.mult, op1=ALU.add).then_inc(sems["h0"], 1)
            dve.wait_ge(sems["ffn0_down"], 1)
            v.tensor_scalar(a0_t[:], P[7][:], col["ff_b2"], None, ALU.add).then_inc(attn0.s("context_sb"), 1)
            dve.wait_ge(sems["second"], 16)
            dve.wait_ge(sems["setup_pos"], 1)
            v.tensor_tensor(p_pos[:], each(P[6][:, 0:S], 4), over(w["mask4"], S), ALU.mult).then_inc(sems["p_pos"], 1)
            dve.wait_ge(sems["zeros"], 5)
            attn0.wait(dve, "k_psum", 2)
            v.tensor_scalar(q_bd[64:128, :, 64:128], heads(P[4][64:128, :], NB), col["bq0"][64:128], None,
                            ALU.add).then_inc(attn0.s("q"), 1)
            odd_values(attn0)
            attention(attn0)
            dve.wait_ge(sems["h1_psum"], 1)
            v.scalar_tensor_tensor(out=h1_t[:], in0=P[0][:], scalar=col["bp0"], in1=h0_t[:], op0=ALU.add,
                                   op1=ALU.add).then_inc(sems["h1"], 1)
            dve.wait_ge(sems["h1"], 1)
            dve.wait_ge(sems["ffn1_down"], 1)
            v.scalar_tensor_tensor(out=h2_t[:], in0=P[7][:], scalar=col["ff_b2"], in1=h1_t[:], op0=ALU.add,
                                   op1=ALU.add).then_inc(sems["h2"], 1)
            dve.wait_ge(sems["h2_turned"], 1)
            double_norm(P[0][:], xn[:], sems["xa_n"], EPS)
            dve.wait_ge(sems["bias1"], 2)
            attn1.wait(dve, "k_psum", 1)
            v.tensor_scalar(qv_bd[64:128, :, 64:128], heads(P[4][64:128, :], NB), bqv[64:128], None,
                            ALU.add).then_inc(attn1.s("q"), 1)
            for u in range(1, 4, 2):
                dve.wait_ge(sems["pos_psum"], u + 1)
                v.tensor_copy(pos_sb[u][:, :, 1:S + 1], heads(P[3][:], 8)).then_inc(sems["pos_sb_odd"], 1)
                if u == 1:
                    v.tensor_scalar(q_bd[64:128, :, 64:128], heads(P[4][64:128, :], NB), bqu[64:128], None,
                                    ALU.add).then_inc(attn1.s("q"), 1)
            odd_values(attn1)
            attention(attn1)
            dve.wait_ge(sems["h3_psum"], 1)
            dve.wait_ge(sems["h2_nb"], 1)
            v.tensor_tensor(h3_n[:], P[0][:], h2_nb[:], ALU.add).then_inc(sems["h3"], 1)
            dve.wait_ge(sems["h3"], 1)
            moments(h3_n)
            v.tensor_scalar(rin[:, 0:8], mv[:, :, 1], EPS, None, ALU.add).then_inc(sems["rin"], 1)
            centre(h3_n[:])
            root()
            scaled(y_n[:], rout[:, 0:8]).then_inc(sems["y_n"], 1)
            split_x(y_t, "y", "x0_split")
            dve.wait_ge(sems["third"], 16)
            dve.wait_ge(sems["gate_psum"], 1)
            link(v.tensor_tensor(logit[:], P[7][:, 0:8 * E0].rearrange("p (g e) -> p g e", g=8),
                                 each(w["gate_b"], 8), ALU.add))
            for g in range(8):
                link_all(v.max(top8[:, g, :], logit[:, g, :]))
            dve.wait_ge(sems["dve_step"], steps[0])
            for g in range(8):
                link_all(v.max_index(top8i[:, g, :], top8[:, g, :], logit[:, g, :]))
            v.tensor_tensor(gap[:], top8[:, :, 1], top8[:, :, 0], ALU.subtract).then_inc(sems["gap"], 1)
            dve.wait_ge(sems["dve_step"], steps[0])
            link(v.tensor_copy(topf[:], top8i[:]))
            one_hots(E0)
            dve.wait_ge(sems["egap"], 1)
            link(v.tensor_scalar(wsum[:], egap[:], 1.0, None, ALU.add))
            link(v.reciprocal(w12[:, :, 0], wsum[:]))
            link(v.tensor_tensor(w12[:, :, 1], w12[:, :, 0], egap[:], ALU.mult))
            weigh(E0, "gates")
            dve.wait_ge(sems["moe_zeros"], 1)
            split3(E0, "gates3")
            dve.wait_ge(sems["gates3_turned"], 1)
            v.tensor_copy(gates_t3[:], P[4][:].bitcast(BF16)[:, 0:NT]).then_inc(sems["gates_sb"], 1)
            EB = [P[2], P[3], P[6]]
            for e in range(E0):
                if e == E0 - 2:
                    dve.wait_ge(sems["bias0"], 1)
                    link(v.tensor_tensor(z_t[:], P[5][:], z_t[:], ALU.add))
                dve.wait_ge(sems["down0"], 2 * e + 2)
                dve.wait_ge(sems["gate_rows"], e + 1)
                v.tensor_tensor(centred[:], EB[e % 3][:], gate_sb[e % 2][:], ALU.mult).then_inc(sems["weighed0"], 1)
                dve.wait_ge(sems["weighed0"], e + 1)
                last = v.tensor_tensor(z_t[:], centred[:], (y_t if e == 0 else z_t)[:], ALU.add)
                if e == E0 - 1:
                    last.then_inc(sems["z"], 1)
                else:
                    link(last)
            dve.wait_ge(sems["z_turned"], 1)
            moments(P[0])
            v.tensor_scalar(rin[:, 0:8], mv[:, :, 1], EPS, None, ALU.add).then_inc(sems["rin"], 1)
            centre(P[0][:])
            root()
            link(scaled(xn[:], rout[:, 0:8]))
            link(v.tensor_tensor(heads(centred[:], 8), heads(xn[:], 8), each(w["gamma"], 8), ALU.mult))
            dve.wait_ge(sems["h3_nb"], 1)
            v.tensor_tensor(h4_n[:], centred[:], h3_nb[:], ALU.add).then_inc(sems["h4"], 1)
            dve.wait_ge(sems["h4"], 1)
            v.tensor_tensor(kq_w[:], col["kn"], col["qn"], ALU.mult).then_inc(sems["kq_w"], 1)
            moments(h4_n)
            v.tensor_scalar(rin[:, 0:8], mv[:, :, 1], EPS, None, ALU.add).then_inc(sems["rin"], 1)
            centre(h4_n[:])
            root()
            scaled(xn[:], rout[:, 0:8]).then_inc(sems["xb_n"], 1)
            for n in range(2):
                dve.wait_ge(sems["sq"], n + 1)
                pair = sq[:, 512 * n:512 * n + 512].rearrange("p (a d) -> p a d", d=2)
                link(v.tensor_tensor(qk_ms[:, 256 * n:256 * n + 256], pair[:, :, 0], pair[:, :, 1], ALU.add))
                v.tensor_scalar(qk_ms[:, 256 * n:256 * n + 256], qk_ms[:, 256 * n:256 * n + 256], 0.5, 1e-6,
                                ALU.mult, ALU.add).then_inc(sems["ms"], 1)
            for n in range(2):
                dve.wait_ge(sems["root"], n + 1)
                link(v.reciprocal(qk_ms[:, 256 * n:256 * n + 256], qk_r[:, 256 * n:256 * n + 256]))
                v.tensor_tensor(qk_n[:, 2 * n:2 * n + 2].rearrange("p q o (a d) -> p (q o a) d", d=2),
                                P[2 + n][:].rearrange("p (a d) -> p a d", d=2),
                                over(qk_ms[:, 256 * n:256 * n + 256], 2), ALU.mult).then_inc(sems["qk_n"], 1)
            attn2.wait(dve, "v_psum", 1)
            v_in = P[7][:].rearrange("p (b h g d) -> p b h g d", b=NB, h=2, d=2)
            v_out = V32.rearrange("p (b g) c -> p b g c", b=NB)
            for h in range(2):
                v.tensor_copy(v_out[64:128, :, :, 6 * h + 3:6 * h + 5], v_in[64:128, :, h]).then_inc(attn2.s("v"), 1)
            dve.wait_ge(sems["q_high"], 1)
            v.tensor_tensor(q_parts[1][:], P[4][:], q_parts[0][:].bitcast(F32), ALU.subtract).then_inc(sems["q_low"], 1)
            dve.wait_ge(sems["k32"], 1)
            v.tensor_copy(k_parts[0][:], k_t[:]).then_inc(sems["k_high"], 1)
            dve.wait_ge(sems["k_high"], 1)
            v.tensor_tensor(k_parts[1][:], k_t[:], k_parts[0][:].bitcast(F32), ALU.subtract).then_inc(sems["k_low"], 1)
            for g in range(4):
                dve.wait_ge(sems["k_rows"], g + 1)
                v.tensor_copy(keys32[:, g, :], P[(0, 1, 4, 5)[g]][:]).then_inc(sems["keys32"], 1)

            def normalise32(b):
                dve.wait_ge(sems["on"], b + 1)
                if b >= 2:
                    attn2.wait(dve, "context_t", b - 1)
                o = P[7][:].rearrange("p (a c) -> p a c", c=32)
                rs = rowsum[b % 2][:].rearrange("p (a o) -> p a o", o=2)
                cn = ctx_n[b % 2][:, 0:D].rearrange("p (a o d) -> p a o d", o=2, d=2)
                for h in range(2):
                    p = slice(64 * h, 64 * h + 64)
                    of = o[p, :, 6 * h:6 * h + 6].rearrange("p a (o d) -> p a o d", o=2)
                    link_all(v.reciprocal(rs[p], of[:, :, :, 2]))
                dve.wait_ge(sems["dve_step"], steps[0])
                for h in range(2):
                    p = slice(64 * h, 64 * h + 64)
                    of = o[p, :, 6 * h:6 * h + 6].rearrange("p a (o d) -> p a o d", o=2)
                    last = v.tensor_tensor(cn[p], of[:, :, :, 0:2],
                                           rs[p].unsqueeze(3).to_broadcast([64, 16, 2, 2]), ALU.mult)
                    if h == 0:
                        link_all(last)
                last.then_inc(attn2.s("context"), 1)

            for step in range(N32 + 7):
                if step < N32:
                    centre_scores(attn2, step)
                u = step - 7
                if 0 <= u < N32 and u % 4 == 3:
                    normalise32(u // 4)
            dve.wait_ge(sems["h5_psum"], 1)
            v.tensor_tensor(h5_n[:], P[0][:], h4_n[:], ALU.add).then_inc(sems["h5"], 1)
            dve.wait_ge(sems["h5"], 1)
            moments(h5_n)
            link(v.tensor_scalar(rin[:, 8:16], mv[:, :, 1], EPS, None, ALU.add))
            v.tensor_scalar(rin[:, 0:8], mv[:, :, 1], 1.0 + 1e-6, EPS * 1e-6, ALU.mult,
                            ALU.add).then_inc(sems["rin"], 1)
            centre(h5_n[:])
            root(16)
            scaled(xn[:], rout[:, 0:8]).then_inc(sems["xc_n"], 1)
            scaled(x_n[:], rout[:, 8:16]).then_inc(sems["x_n"], 1)
            for i, bank in enumerate((2, 3, 4, 5)):
                dve.wait_ge(sems["rope_psum"], i + 1)
                link_all(v.tensor_tensor(heads(rope[i], NB), heads(P[bank][:], NB),
                                         each(w["rope_c" if i % 2 == 0 else "rope_s"], NB), ALU.mult))
                if i == 1:
                    dve.wait_ge(sems["dve_step"], steps[0])
                    v.tensor_tensor(k_t[:], rope[0], rope[1], ALU.add).then_inc(attn3.s("k"), 1)
            dve.wait_ge(sems["dve_step"], steps[0])
            for h in range(2):
                p = slice(64 * h, 64 * h + 64)
                v.tensor_tensor(q_bd[p, :, 64 * h:64 * h + 64], heads(rope[2][p, :], NB),
                                heads(rope[3][p, :], NB), ALU.add).then_inc(attn3.s("q"), 1)
            odd_values(attn3)
            attention(attn3)
            dve.wait_ge(sems["x2_psum"], 1)
            dve.wait_ge(sems["x_n"], 1)
            v.tensor_tensor(x2_n[:], P[0][:], x_n[:], ALU.add).then_inc(sems["x2"], 1)
            dve.wait_ge(sems["x2"], 1)
            moments(x2_n)
            link(v.tensor_tensor(msq[:], mv[:, :, 0], mv[:, :, 0], ALU.mult))
            v.scalar_tensor_tensor(out=rin[:, 0:8], in0=mv[:, :, 1], scalar=1e-6, in1=msq[:], op0=ALU.add,
                                   op1=ALU.add).then_inc(sems["rin"], 1)
            root()
            v.tensor_tensor(heads(xn[:], 8), heads(x2_n[:], 8), over(rout[:, 0:8], D),
                            ALU.mult).then_inc(sems["f_n"], 1)
            split_x(f_t, "f", "x1_split")
            dve.wait_ge(sems["gate1_psum"], 1)
            lg = P[7][:, 0:8 * E1].rearrange("p (g e) -> p g e", g=8)
            link(v.tensor_reduce(gap[:], lg, AX.X, ALU.max))
            v.tensor_tensor(logit[:, :, 0:E1], lg, over(gap[:], E1), ALU.subtract).then_inc(sems["shift1"], 1)
            dve.wait_ge(sems["exp1"], 1)
            link(v.tensor_reduce(wsum[:], resid[:, :, 0:E1], AX.X, ALU.add))
            link(v.reciprocal(gap[:], wsum[:]))
            link(v.tensor_tensor(logit[:, :, 0:E1], resid[:, :, 0:E1], over(gap[:], E1), ALU.mult))
            for g in range(8):
                link_all(v.max(top8[:, g, :], logit[:, g, 0:E1]))
            dve.wait_ge(sems["dve_step"], steps[0])
            for g in range(8):
                link_all(v.max_index(top8i[:, g, :], top8[:, g, :], logit[:, g, 0:E1]))
            link_all(v.tensor_tensor(wsum[:], top8[:, :, 0], top8[:, :, 1], ALU.add))
            dve.wait_ge(sems["dve_step"], steps[0])
            link_all(v.tensor_copy(topf[:], top8i[:]))
            link(v.tensor_scalar(wsum[:], wsum[:], 1e-9, None, ALU.add))
            one_hots(E1)
            link(v.reciprocal(gap[:], wsum[:]))
            link(v.tensor_tensor(w12[:], top8[:, :, 0:2], over(gap[:], 2), ALU.mult))
            weigh(E1, "gates1")
            dve.wait_ge(sems["half_m"], 1)
            split3(E1, "gates31")
            dve.wait_ge(sems["gates1_turned"], 1)
            v.tensor_copy(gates_t3[:], P[7][:].bitcast(BF16)[:, 0:NT]).then_inc(sems["gates1_sb"], 1)
            for i in range(2 * T1):
                rows = min(128, H1ROWS - 128 * (i // 2))
                if i < EARLY:
                    dve.wait_ge(sems["early1"], i + 1)
                    hidden = early_a[i]
                else:
                    dve.wait_ge(sems["silu1"], i + 1)
                    dve.wait_ge(sems["b1"], i + 1)
                    hidden = silu[i % 2][0:rows, :]
                    link(v.tensor_tensor(hidden, P[2 + i % 2][0:rows, :], hidden, ALU.mult))
                dve.wait_ge(sems["g1"], i + 1)
                v.tensor_tensor(hid[i % 4][0:rows, :], P[5 + i % 2][0:rows, :], hidden,
                                ALU.mult).then_inc(sems["hid1"], 1)
            dve.wait_ge(sems["fin"], 1)
            for n in range(2):
                dve.wait_ge(sems["o_turned"], 2 * n + 2)
                c = slice(256 * n, 256 * n + 256)
                v.tensor_tensor(out_n[:, c], P[n][:, c], fin_n[:, c], ALU.add).then_inc(sems["out_ready"], 1)

        @block.gpsimd
        def _(pool):
            g = nc.gpsimd

            def keys(a):
                cols = S * a.per
                for u in range(a.units):
                    if u == 0:
                        a.wait(pool, "k", 1)
                    if u >= 2:
                        a.wait(pool, "scores", u - 1)
                    for n in range(a.per):
                        b = a.per * u + n
                        ins = g.tensor_tensor(
                            R[u % 2][:, 512 // a.per * n:512 // a.per * (n + 1)].rearrange("p (h j) -> p h j", j=S),
                            each(k_t[:, S * b:S * b + S], a.H), over(a.mask, S), ALU.mult)
                    ins.then_inc(a.s("keys"), 1)

            def split_weights(raw, split, loaded, n, done):
                pool.wait_ge(sems[loaded], n)
                for h in range(2):
                    p = slice(64 * h, 64 * h + 64)
                    g.tensor_copy(split[h][p, :], raw[p, :]).then_inc(sems[done], 1)
                pool.wait_ge(sems[done], 2)
                for h in range(2):
                    p = slice(64 * h, 64 * h + 64)
                    g.tensor_tensor(split[1 - h][p, :], raw[p, :], split[h][p, :].bitcast(F32),
                                    ALU.subtract).then_inc(sems[done], 1)
                pool.wait_ge(sems[done], 4)

            g.memset(one[:], 1.0).then_inc(sems["one"], 1)
            g.memset(q_bd[:], 0.0).then_inc(sems["zeros"], 1)
            g.memset(V0[:], 0.0).then_inc(sems["zeros"], 1)
            g.memset(qv_bd[:], 0.0).then_inc(sems["zeros"], 1)
            pool.wait_ge(sems["zeros"], 3)
            g.memset(V0[0:64, :, 8:9], 1.0).then_inc(sems["zeros"], 1)
            g.memset(V0[64:128, :, 17:18], 1.0).then_inc(sems["zeros"], 1)
            pool.wait_ge(sems["zeros"], 5)
            pool.wait_ge(sems["first"], 16)
            g.tensor_scalar(pe_b[:], w["pe_t"], col["ln_b"], None, ALU.add).then_inc(sems["pe_b"], 1)
            g.memset(V4[:], 0.0).then_inc(sems["ones"], 1)
            for i in range(4):
                g.memset(pos_sb[i], 0.0).then_inc(sems["ones"], 1)
            pool.wait_ge(sems["ones"], 5)
            g.memset(V4[0:64, :, 16:17], 1.0).then_inc(sems["ones"], 1)
            g.memset(V4[64:128, :, 33:34], 1.0).then_inc(sems["ones"], 1)
            pool.wait_ge(sems["ones"], 7)
            keys(attn0)
            attn0.wait(pool, "keys", attn0.units)
            split_weights(raw0, w1_split, "moe0", 32, "w1_split")
            pool.wait_ge(sems["second"], 16)
            g.tensor_tensor(bqv[:], col["bq1"], col["v1"], ALU.add).then_inc(sems["bias1"], 1)
            g.tensor_tensor(bqu[:], col["bq1"], col["u1"], ALU.add).then_inc(sems["bias1"], 1)
            pool.wait_ge(sems["h2_n"], 1)
            g.tensor_tensor(heads(h2_nb[:], 8), heads(h2_n[:], 8), each(w["bout"], 8),
                            ALU.add).then_inc(sems["h2_nb"], 1)
            keys(attn1)
            g.memset(gates3[:], 0.0).then_inc(sems["moe_zeros"], 1)
            pool.wait_ge(sems["third"], 16)
            pool.wait_ge(sems["h3"], 1)
            g.tensor_tensor(heads(h3_nb[:], 8), heads(h3_n[:], 8), each(w["beta"], 8),
                            ALU.add).then_inc(sems["h3_nb"], 1)
            pool.wait_ge(sems["h3_nb"], 1)
            split_weights(raw1, u_split, "moe1", 64, "u_split")
            g.memset(V32, 0.0).then_inc(sems["moe_zeros"], 1)
            pool.wait_ge(sems["moe_zeros"], 2)
            for h in range(2):
                g.memset(V32[0:64, :, 6 * h + 2:6 * h + 3], 1.0).then_inc(sems["moe_zeros"], 1)
                g.memset(V32[64:128, :, 6 * h + 5:6 * h + 6], 1.0).then_inc(sems["moe_zeros"], 1)
            pool.wait_ge(sems["moe_zeros"], 6)
            pool.wait_ge(sems["expander"], 16)
            g.tensor_copy(expander[:], expand_raw).then_inc(sems["expander"], 1)
            for u in range(N32):
                b, grp = u // 4, u % 4
                if u < 4:
                    pool.wait_ge(sems["keys32"], grp + 1)
                if u >= 2:
                    attn2.wait(pool, "scores", u - 1)
                g.tensor_tensor(heads(R32[u % 2][:], 8), each(keys32[:, grp, S * b:S * b + S], 8),
                                over(w["maskr"], S), ALU.mult).then_inc(sems["ops2"], 1)
            keys(attn3)
            pool.wait_ge(sems["x2"], 1)
            g.tensor_tensor(fin_n[:], x2_n[:], h5_n[:], ALU.add).then_inc(sems["fin"], 1)
            g.memset(gates3[:], 0.0).then_inc(sems["half_m"], 1)
            for i in range(EARLY):
                pool.wait_ge(sems["silu1"], i + 1)
                pool.wait_ge(sems["b1_sb"], i + 1)
                g.tensor_tensor(early_a[i], early_b[i], early_a[i], ALU.mult).then_inc(sems["early1"], 1)


def block_diagonal(a):
    k, n = a.shape
    out = np.zeros((2 * k, 2 * n), a.dtype)
    out[:k, :n] = a
    out[k:, n:] = a
    return out


def rows128(a):
    out = np.zeros((128, a.shape[1]), a.dtype)
    out[:a.shape[0]] = a
    return out


def twice(a):
    return np.concatenate([a, a], axis=0)


def value_weights(wv, H):
    d = D // H
    v = wv.reshape(D, H // 2, 2, d)
    return np.concatenate([block_diagonal(np.ascontiguousarray(v[:, :, o, :]).reshape(D, D // 2)) for o in range(2)],
                          axis=1)


def angles(n, positions):
    i = np.arange(0, n, 2, dtype=np.float32)
    return i, np.arange(positions, dtype=np.float32)[:, None]


def lay_out(a):
    f = np.float32
    a = {k: np.asarray(v) for k, v in a.items()}
    x = a["x"].reshape(B, C, IMG // PATCH, PATCH, IMG // PATCH, PATCH)
    patches = np.ascontiguousarray(x.transpose(1, 3, 5, 0, 2, 4)).reshape(KC, 128, 2 * NT)

    i, pos = angles(D, S)
    div = np.exp(-np.log(f(10000.0)) * i / f(D)).astype(f)
    pe = np.zeros((S, D), f)
    pe[:, 0::2], pe[:, 1::2] = np.sin(pos * div), np.cos(pos * div)
    div1 = np.exp(i * f(-np.log(10000.0) / D)).astype(f)
    pe1 = np.zeros((S, D), f)
    pe1[:, 0::2], pe1[:, 1::2] = np.sin(pos * div1), np.cos(pos * div1)

    c = np.arange(D)

    def mask(n, of):
        return twice((of[:, None] == np.arange(n)[None, :]).astype(f))

    def column(*cols):
        return np.stack([twice(x.reshape(-1, 1))[:, 0] if x.size == D else x.reshape(-1) for x in cols], axis=1)

    def pad(m, n):
        return np.concatenate([m, np.zeros((128, n - m.shape[1]), m.dtype)], axis=1)

    qkv = a["L0_tok_qkv_w"].T
    qkv_b = a["L0_tok_qkv_b"]
    ffup = a["L0_tok_ff_w1"].T
    zero = np.zeros((D, FF), f)
    ffb = a["L0_tok_ff_b1"]
    qn, kn = (np.tile(a[f"L1_attn_{n}n_w"], D // 2) for n in "qk")
    first = {
        "conv_w": a["L0_tok_conv_w"].reshape(D, KC, 128).transpose(2, 1, 0).reshape(128, KC * D),
        "ident": np.eye(128, dtype=f),
        "cols0": pad(column(a["L0_tok_conv_b"], a["L0_tok_ln_w"], a["L0_tok_ln_b"], ffb[:128], ffb[128:],
                            a["L0_tok_ff_b2"]), 8),
        "pe_t": twice(pe.T),
    }
    ffn_w = {
        "up_lo": np.concatenate([ffup, zero]), "up_hi": np.concatenate([zero, ffup]),
        "down": a["L0_tok_ff_w2"].T.reshape(2, 128, D).transpose(1, 0, 2).reshape(128, 2 * D),
    }
    second = {
        "wq0": block_diagonal(qkv[:, :D]), "wk0": block_diagonal(qkv[:, D:2 * D]),
        "wv0": value_weights(qkv[:, 2 * D:], 8), "wp0": block_diagonal(a["L0_tok_proj_w"].T),
        "cols1": pad(column(qkv_b[:D], qkv_b[D:2 * D], qkv_b[2 * D:], a["L0_tok_proj_b"], a["L0_attn_ln_gamma"],
                            a["L0_attn_ln_beta"], a["L0_attn_bq"], a["L0_attn_bk"], a["L0_attn_bv"],
                            a["L0_attn_u_bias"].reshape(-1), a["L0_attn_v_bias"].reshape(-1)), 16),
        "mask8": mask(8, c // 8), "mask4": mask(4, c // 16),
        "wpos": rows128(np.concatenate([a["L0_attn_Wpos"]] * 2, axis=1)), "pe_s": rows128(pe1.T),
        "wq1": block_diagonal(a["L0_attn_Wq"]), "wk1": block_diagonal(a["L0_attn_Wk"]),
        "wv1": value_weights(a["L0_attn_Wv"], 4), "wo1": block_diagonal(a["L0_attn_Wout"]),
        "bout": np.tile(a["L0_attn_bout"], (128, 1)),
    }
    wq, wk, wv = (a[f"L1_ffn_w{n}"].T for n in "qkv")
    rep = (np.arange(4)[:, None] // 2 * 16 + np.arange(16)[None, :]).reshape(-1)
    swap = (np.arange(4)[:, None] * 16 + (np.arange(16)[None, :] + 8) % 16).reshape(-1)
    wk, wv = wk[:, rep], wv[:, rep]
    inv = 1.0 / 10000.0 ** (np.arange(0, 16, 2, dtype=f) / 16)
    fr = np.outer(np.arange(S, dtype=f), inv)
    emb = np.concatenate([fr, fr], axis=-1)
    cos, sin = np.cos(emb).astype(f), np.sin(emb).astype(f)
    sign = np.where(np.arange(16) < 8, -1.0, 1.0).astype(f)
    qk2 = a["L1_attn_w_qkv"].T
    third = {
        "gate": block_diagonal(a["L0_ffn_gate_w"]), "gate_b": np.tile(a["L0_ffn_gate_b"], (128, 1)),
        "iota": np.tile(np.arange(E0, dtype=f), (128, 1)), "b2": rows128(block_diagonal(a["L0_ffn_b2"])),
        "b1": a["L0_ffn_b1"].T, "gamma": np.tile(a["L0_ffn_gamma"], (128, 1)),
        "beta": np.tile(a["L0_ffn_beta"], (128, 1)),
        "wqk2": np.concatenate([block_diagonal(qk2[:, :D]), block_diagonal(qk2[:, D:2 * D])], axis=1),
        "wv2": value_weights(qk2[:, 2 * D:], 32), "wp2": block_diagonal(a["L1_attn_w_proj"].T),
        "maskr": mask(8, c // 2 % 8),
        "maskh": (np.arange(128)[:, None] // 16 % 2 == np.arange(2)[None, :]).astype(f),
        "cols2": column(qn, kn, a["L1_ffn_ln1_w"], a["L1_ffn_ln2_w"]),
        "wq3": block_diagonal(wq), "wqs3": block_diagonal(wq[:, swap]),
        "wk3": block_diagonal(wk), "wks3": block_diagonal(wk[:, swap]),
        "wv3": value_weights(wv, 4), "wo3": block_diagonal(a["L1_ffn_wo"].T),
        "rope_c": twice(np.tile(cos.T, (4, 1))), "rope_s": twice(np.tile((sin * sign).T, (4, 1))),
        "router": block_diagonal(a["L1_ffn_router_w"].T),
    }
    key = np.arange(512) % S
    query = np.arange(128) % S
    sel1 = np.zeros((128, 2, H1ROWS), f)
    eye3 = np.zeros((128, 2 * E0), f)
    for p in range(3):
        eye3[2 * E0 * p:2 * E0 * (p + 1)] = np.eye(2 * E0, dtype=f)
        for h in range(2):
            for e in range(E1):
                sel1[2 * E1 * p + E1 * h + e, h, F1 * e:F1 * (e + 1)] = 1.0
    half = {"identb": np.eye(128, dtype=f), "causal": np.where(key[None, :] > query[:, None], f(NEG), f(0.0)),
            "eye3": eye3, "sel1": sel1.reshape(128, -1)}

    row = np.arange(128)
    spread = np.zeros((128, 4, 4, 128), f)
    for part in range(4):
        of = row // 64 if part < 2 else row // 32 % 2
        for g in range(4):
            spread[64 * (row // 16 % 2) + 16 * g + row % 16, part, g, row] = of == part % 2

    def packed(name, parts):
        got = [parts[n] for n, _ in PACKS[name]]
        assert [g.shape[1] for g in got] == [n for _, n in PACKS[name]], name
        return np.ascontiguousarray(np.concatenate(got, axis=1))

    def hidden(wt):
        return np.ascontiguousarray(wt.reshape(H1ROWS, D).T)

    w2 = np.zeros((T1 * 128, D), f)
    w2[:H1ROWS] = a["L1_ffn_w2"].transpose(0, 2, 1).reshape(H1ROWS, D)
    return {
        "patches": patches,
        "first": packed("first", first), "ffn_w": packed("ffn", ffn_w),
        "second": packed("second", second), "third": packed("third", third),
        "half_consts": np.ascontiguousarray(packed("half", half).view(np.uint16)[:, 1::2]),
        "expand": spread.reshape(128, -1),
        "moe0_w1": np.ascontiguousarray(a["L0_ffn_w1"].transpose(1, 0, 2)).reshape(D, E0 * F0),
        "moe0_w2": np.ascontiguousarray(a["L0_ffn_w2"].transpose(1, 0, 2)).reshape(F0, E0 * D),
        "moe1_w1": hidden(a["L1_ffn_w1"]), "moe1_w3": hidden(a["L1_ffn_w3"]),
        "moe1_w2": np.ascontiguousarray(w2.reshape(T1, 128, D).transpose(1, 0, 2)).reshape(128, T1 * D),
    }


def kernel(**inputs):
    import concourse.bacc as bacc
    from concourse.bass_utils import run_bass_kernel_spmd

    arrays = lay_out(inputs)
    nc = bacc.Bacc("TRN2", target_bir_lowering=False, num_devices=1)
    args = {n: nc.dram_tensor(f"in_{n}", x.shape, mybir.dt.from_np(x.dtype), kind="ExternalInput").ap()
            for n, x in arrays.items()}
    out = nc.dram_tensor("out_tokens", (128, NT), F32, kind="ExternalOutput").ap()
    tower_program(nc, **args, out=out)
    r = run_bass_kernel_spmd(nc, [{f"in_{n}": x for n, x in arrays.items()}], core_ids=[0])
    got = r.results[0]["out_tokens"]
    return np.ascontiguousarray(got.reshape(2, S, NQ, 2, D).transpose(3, 2, 0, 1, 4)).reshape(B, S, D)
```
